# Optimizing a Trainium2 kernel written in Bass

```python
import numpy as np
import jax
import jax.numpy as jnp

def _softmax(x, axis=-1):
    return jax.nn.softmax(x, axis=axis)

def _gelu(x):
    return jax.nn.gelu(x, approximate=True)

def _silu(x):
    return jax.nn.silu(x)

def _sigmoid(x):
    return jax.nn.sigmoid(x)

def _layernorm(x, axis=-1, eps=1e-05):
    m = jnp.mean(x, axis=axis, keepdims=True)
    v = jnp.var(x, axis=axis, keepdims=True)
    return (x - m) / jnp.sqrt(v + eps)

def _scatter_add(tgt, idx, src, axis=0):
    return tgt.at[idx].add(src)

def _segment_sum(src, seg, n):
    return jax.ops.segment_sum(src, seg, n)
kernel_name = 'mk_macaron_d1_jaxref_r8_89667c'

def setup_inputs(seed: int=0):
    np.random.seed(seed)
    _w = jnp.asarray

    def _L0_attn_setup():
        import jax, jax.numpy as jnp
        import numpy as np
        HID = 256
        D_SSM = 512
        G = 1
        S = 128
        H = 64
        P = D_SSM // H
        K = 4
        EPS = 1e-05
        CONV_DIM = D_SSM + 2 * G * S
        PROJ = 2 * D_SSM + 2 * G * S + H
        MULT = [0.25, 0.5, 0.75, 1.0, 1.25]

        def _mup_vector():
            v = np.ones(PROJ, np.float32)
            gs = G * S
            v[:D_SSM] *= MULT[0]
            v[D_SSM:2 * D_SSM] *= MULT[1]
            v[2 * D_SSM:2 * D_SSM + gs] *= MULT[2]
            v[2 * D_SSM + gs:2 * D_SSM + 2 * gs] *= MULT[3]
            v[2 * D_SSM + 2 * gs:] *= MULT[4]
            return jnp.asarray(v)

        def _reference_tuple_inner(hidden_states, residual, W_in, conv_w, conv_b, A_log, D, dt_bias, norm_w, W_out, mup_vector):
            B, L, _ = hidden_states.shape
            Hg = H // G
            proj = hidden_states @ W_in * mup_vector
            z, xBC, dt = jnp.split(proj, [D_SSM, D_SSM + CONV_DIM], axis=-1)
            xp = jnp.pad(xBC, ((0, 0), (K - 1, 0), (0, 0)))
            conv = conv_b + sum((conv_w[:, k] * xp[:, k:k + L] for k in range(K)))
            xBC = jax.nn.silu(conv)
            x = xBC[..., :D_SSM].reshape(B, L, G, Hg, P)
            Bm = xBC[..., D_SSM:D_SSM + G * S].reshape(B, L, G, S)
            Cm = xBC[..., D_SSM + G * S:].reshape(B, L, G, S)
            dt = jax.nn.softplus(dt + dt_bias).reshape(B, L, G, Hg)
            dA = jnp.exp(dt * (-jnp.exp(A_log)).reshape(G, Hg))
            xs = (x.transpose(1, 0, 2, 3, 4), Bm.transpose(1, 0, 2, 3), Cm.transpose(1, 0, 2, 3), dA.transpose(1, 0, 2, 3), dt.transpose(1, 0, 2, 3))

            def step(state, inp):
                x_t, B_t, C_t, dA_t, dt_t = inp
                state = state * dA_t[..., None, None] + (dt_t[..., None] * x_t)[..., None] * B_t[:, :, None, None, :]
                y_t = jnp.einsum('bghps,bgs->bghp', state, C_t)
                return (state, y_t)
            state0 = jnp.zeros((B, G, Hg, P, S), hidden_states.dtype)
            _, ys = jax.lax.scan(step, state0, xs)
            y = ys.transpose(1, 0, 2, 3, 4) + D.reshape(G, Hg)[..., None] * x
            y = y.reshape(B, L, D_SSM)
            g = y * jax.nn.silu(z)
            g = g * jax.lax.rsqrt(jnp.mean(jnp.square(g), axis=-1, keepdims=True) + EPS) * norm_w
            out = g @ W_out
            return (out, residual)
        key = jax.random.key(seed)
        ks = jax.random.split(key, 10)
        B, L = (2, 256)
        return {'hidden_states': jax.random.normal(ks[0], (B, L, HID), jnp.float32), 'residual': jax.random.normal(ks[1], (B, L, HID), jnp.float32), 'W_in': jax.random.normal(ks[2], (HID, PROJ), jnp.float32) * 0.02, 'conv_w': jax.random.normal(ks[3], (CONV_DIM, K), jnp.float32) * 0.2, 'conv_b': jax.random.normal(ks[4], (CONV_DIM,), jnp.float32) * 0.02, 'A_log': jax.random.uniform(ks[5], (H,), jnp.float32, 0.0, 1.0), 'D': jax.random.normal(ks[6], (H,), jnp.float32) * 0.5, 'dt_bias': jax.random.normal(ks[7], (H,), jnp.float32) * 0.5, 'norm_w': jnp.ones((D_SSM,), jnp.float32), 'W_out': jax.random.normal(ks[8], (D_SSM, HID), jnp.float32) * 0.02, 'mup_vector': _mup_vector()}
    _L0_attn_in = _L0_attn_setup()

    def _L0_ffn_setup():
        import jax, jax.numpy as jnp
        import numpy as np
        EPS = 1e-08

        def _quantize(w):
            gamma = jnp.mean(jnp.abs(w))
            return jnp.clip(jnp.round(w / (gamma + EPS)), -1.0, 1.0)

        def _bitlinear(x, w):
            return jnp.matmul(x, _quantize(w).T)
        key = jax.random.key(seed)
        k1, k2, k3, k4 = jax.random.split(key, 4)
        d, h = (256, 704)
        x = jax.random.normal(k1, (4, 256, d), dtype=jnp.float32)
        w1 = jax.random.normal(k2, (h, d), dtype=jnp.float32)
        w2 = jax.random.normal(k3, (h, d), dtype=jnp.float32)
        w3 = jax.random.normal(k4, (d, h), dtype=jnp.float32)
        return {'x': x, 'w1': w1, 'w2': w2, 'w3': w3}
    _L0_ffn_in = _L0_ffn_setup()
    _d = {'L0_attn_hidden_states': _L0_attn_in['hidden_states'], 'L0_attn_residual': _L0_attn_in['residual'], 'L0_attn_W_in': _L0_attn_in['W_in'], 'L0_attn_conv_w': _L0_attn_in['conv_w'], 'L0_attn_conv_b': _L0_attn_in['conv_b'], 'L0_attn_A_log': _L0_attn_in['A_log'], 'L0_attn_D': _L0_attn_in['D'], 'L0_attn_dt_bias': _L0_attn_in['dt_bias'], 'L0_attn_norm_w': _L0_attn_in['norm_w'], 'L0_attn_W_out': _L0_attn_in['W_out'], 'L0_attn_mup_vector': _L0_attn_in['mup_vector'], 'L0_ffn_w1': _L0_ffn_in['w1'], 'L0_ffn_w2': _L0_ffn_in['w2'], 'L0_ffn_w3': _L0_ffn_in['w3']}
    _x0 = _d['L0_attn_hidden_states']
    _d['L0_attn_hidden_states'] = jax.random.normal(jax.random.fold_in(jax.random.key(seed), 1), (2, 2048, 256), dtype=_x0.dtype)
    del _x0
    return _d

def reference(L0_attn_hidden_states, L0_attn_residual, L0_attn_W_in, L0_attn_conv_w, L0_attn_conv_b, L0_attn_A_log, L0_attn_D, L0_attn_dt_bias, L0_attn_norm_w, L0_attn_W_out, L0_attn_mup_vector, L0_ffn_w1, L0_ffn_w2, L0_ffn_w3):

    def _L0_attn_ref(hidden_states, residual, W_in, conv_w, conv_b, A_log, D, dt_bias, norm_w, W_out, mup_vector):
        import jax, jax.numpy as jnp
        import numpy as np
        HID = 256
        D_SSM = 512
        G = 1
        S = 128
        H = 64
        P = D_SSM // H
        K = 4
        EPS = 1e-05
        CONV_DIM = D_SSM + 2 * G * S
        PROJ = 2 * D_SSM + 2 * G * S + H
        MULT = [0.25, 0.5, 0.75, 1.0, 1.25]

        def _mup_vector():
            v = np.ones(PROJ, np.float32)
            gs = G * S
            v[:D_SSM] *= MULT[0]
            v[D_SSM:2 * D_SSM] *= MULT[1]
            v[2 * D_SSM:2 * D_SSM + gs] *= MULT[2]
            v[2 * D_SSM + gs:2 * D_SSM + 2 * gs] *= MULT[3]
            v[2 * D_SSM + 2 * gs:] *= MULT[4]
            return jnp.asarray(v)

        def _reference_tuple_inner(hidden_states, residual, W_in, conv_w, conv_b, A_log, D, dt_bias, norm_w, W_out, mup_vector):
            B, L, _ = hidden_states.shape
            Hg = H // G
            proj = hidden_states @ W_in * mup_vector
            z, xBC, dt = jnp.split(proj, [D_SSM, D_SSM + CONV_DIM], axis=-1)
            xp = jnp.pad(xBC, ((0, 0), (K - 1, 0), (0, 0)))
            conv = conv_b + sum((conv_w[:, k] * xp[:, k:k + L] for k in range(K)))
            xBC = jax.nn.silu(conv)
            x = xBC[..., :D_SSM].reshape(B, L, G, Hg, P)
            Bm = xBC[..., D_SSM:D_SSM + G * S].reshape(B, L, G, S)
            Cm = xBC[..., D_SSM + G * S:].reshape(B, L, G, S)
            dt = jax.nn.softplus(dt + dt_bias).reshape(B, L, G, Hg)
            dA = jnp.exp(dt * (-jnp.exp(A_log)).reshape(G, Hg))
            xs = (x.transpose(1, 0, 2, 3, 4), Bm.transpose(1, 0, 2, 3), Cm.transpose(1, 0, 2, 3), dA.transpose(1, 0, 2, 3), dt.transpose(1, 0, 2, 3))

            def step(state, inp):
                x_t, B_t, C_t, dA_t, dt_t = inp
                state = state * dA_t[..., None, None] + (dt_t[..., None] * x_t)[..., None] * B_t[:, :, None, None, :]
                y_t = jnp.einsum('bghps,bgs->bghp', state, C_t)
                return (state, y_t)
            state0 = jnp.zeros((B, G, Hg, P, S), hidden_states.dtype)
            _, ys = jax.lax.scan(step, state0, xs)
            y = ys.transpose(1, 0, 2, 3, 4) + D.reshape(G, Hg)[..., None] * x
            y = y.reshape(B, L, D_SSM)
            g = y * jax.nn.silu(z)
            g = g * jax.lax.rsqrt(jnp.mean(jnp.square(g), axis=-1, keepdims=True) + EPS) * norm_w
            out = g @ W_out
            return (out, residual)
        return _reference_tuple_inner(hidden_states, residual, W_in, conv_w, conv_b, A_log, D, dt_bias, norm_w, W_out, mup_vector)[0]

    def _L0_ffn_ref(x, w1, w2, w3):
        import jax, jax.numpy as jnp
        import numpy as np
        EPS = 1e-08

        def _quantize(w):
            gamma = jnp.mean(jnp.abs(w))
            return jnp.clip(jnp.round(w / (gamma + EPS)), -1.0, 1.0)

        def _bitlinear(x, w):
            return jnp.matmul(x, _quantize(w).T)
        x1 = _bitlinear(x, w1)
        x2 = _bitlinear(x, w2)
        hidden = jax.nn.sigmoid(x1) * x2
        return _bitlinear(hidden, w3)
    x = L0_attn_hidden_states
    x = x + 0.5 * _L0_ffn_ref(_layernorm(x, axis=-1), L0_ffn_w1, L0_ffn_w2, L0_ffn_w3)
    x = x + _L0_attn_ref(_layernorm(x, axis=-1), L0_attn_residual, L0_attn_W_in, L0_attn_conv_w, L0_attn_conv_b, L0_attn_A_log, L0_attn_D, L0_attn_dt_bias, L0_attn_norm_w, L0_attn_W_out, L0_attn_mup_vector)
    x = x + 0.5 * _L0_ffn_ref(_layernorm(x, axis=-1), L0_ffn_w1, L0_ffn_w2, L0_ffn_w3)
    return x

_drawn_inputs = setup_inputs


def setup_inputs(seed=0):
    import zlib

    import numpy as np

    out = dict(_drawn_inputs(seed))
    spreads = {'L0_attn_norm_w': (1.0, 0.6)}
    factors = {'L0_attn_W_in': 8.0,
     'L0_attn_conv_w': 8.0,
     'L0_attn_conv_b': 64.0,
     'L0_attn_A_log': 37.755,
     'L0_attn_D': 64.0,
     'L0_attn_dt_bias': 25.243,
     'L0_attn_W_out': 8.0,
     'L0_attn_mup_vector': 8.0}
    for name, (base, spread) in spreads.items():
        noise = np.random.default_rng([zlib.crc32(name.encode()), seed]).standard_normal(out[name].shape)
        drawn = base * np.exp(spread * noise) if base else spread * noise
        out[name] = jnp.asarray(drawn.astype(out[name].dtype))
    for name, factor in factors.items():
        out[name] = (out[name] * factor).astype(out[name].dtype)
    return out
```

```python
from contextlib import ExitStack

import concourse.bass as bass
from concourse import mybir

F32 = mybir.dt.float32
F16 = mybir.dt.float16
ALU = mybir.AluOpType
ACT = mybir.ActivationFunctionType

P = 128
TILES = 4
UNIT = P * TILES
BATCH, LEN, HID = 2, 2048, 256
UNITS = BATCH * LEN // UNIT
KH = HID // P
FF = 704
CH = (FF + P - 1) // P
LAST = FF - (CH - 1) * P
D_SSM, STATE, HEADS, TAPS = 512, 128, 64, 4
HP = D_SSM // HEADS
Q = D_SSM // P
HQ = HEADS // Q
CT = Q + 2
BLK = 32
NB = P // BLK
PROJ = 2 * D_SSM + 2 * STATE + HEADS
DT0 = 2 * D_SSM + 2 * STATE
LN_EPS, RMS_EPS, Q_EPS = 1e-5, 1e-5, 1e-8
XS = 2.0 ** 11
W2S = 2.0 ** -4
W3S = 0.5 / (XS * W2S)
A_MAX = 120.0
AS = 2.0 ** 9
XPS = 3
SERIES = 8

V_BLK, V_TILE, U_1, U_2, U_3, W_END, TOTAL = range(7)
DECAYS = 7
SEG0 = 4
SEGS = SEG0 + BLK // 2
PROJS = KH + 1 + CT
BANKS = PROJS + Q

LN_STEPS = 3
CONV = CT * (TAPS - 1)
DTC = 12 + SERIES


def spread(list_a, list_b):
    out, j = [], 0
    for i, item in enumerate(list_a):
        out.append(item)
        while j < len(list_b) * (i + 1) // len(list_a):
            out.append(list_b[j])
            j += 1
    return out


def slot_items(has_next):
    other = [("z", n) for n in range(Q)]
    if has_next:
        other += [("t", 0), ("t", 1), ("dt", 0)] + [("c", n) for n in range(CT)]
    return spread([("seg", s) for s in range(SEGS)], other)


def macaron_program(nc, x_in, W_in, conv_w, conv_b, A_log, D_w, dt_bias, norm_w, W_out, mup,
                    w1, w2, w3, out):
    ctx = ExitStack()
    with ctx:
        def sb(name, shape, dt=F32):
            return ctx.enter_context(nc.sbuf_tensor(name, shape, dt))

        def sem(name):
            return ctx.enter_context(nc.semaphore(name))

        mid1 = nc.dram_tensor("x_after_ffn1", (BATCH * LEN, HID), F32, kind="Internal").ap()
        mid2 = nc.dram_tensor("x_after_mamba", (BATCH * LEN, HID), F32, kind="Internal").ap()
        x_flat = x_in.rearrange("b l d -> (b l) d")
        out_flat = out.rearrange("b l d -> (b l) d")

        identf = sb("identf", [P, P])
        ident16 = sb("ident16", [P, P], F16)
        ones = sb("ones", [P, P])
        mhalf = sb("mhalf", [P, TILES])
        tok_mask = sb("tok_mask", [P, 8, P], F16)
        blk_mask = sb("blk_mask", [P, BLK, P], F16)
        causal = sb("causal", [P, BLK])
        off_mask = sb("off_mask", [P, P])
        wi = sb("wi", [P, KH, PROJ])
        wo = sb("wo", [P, Q, HID])
        w12T = sb("w12T", [P, KH, 2 * FF], F16)
        w3T = sb("w3T", [P, CH, HID], F16)
        nw = sb("nw", [P, Q])
        cw = sb("cw", [P, CT, TAPS])
        cb = sb("cb", [P, CT])
        mupc = sb("mupc", [P, DT0 // P])
        dcol = sb("dcol", [P, Q])
        mup_dt = sb("mup_dt", [P, HEADS])
        bias_dt = sb("bias_dt", [P, HEADS])
        expA = sb("expA", [P, HEADS])
        xln = sb("xln", [P, TILES, HID])
        xres = sb("xres", [P, TILES, HID])
        xn = sb("xn", [P, TILES, HID])
        stats = sb("stats", [P, TILES, 6])
        mv = sb("mv", [P, TILES, 2])
        veps = sb("veps", [P, TILES])
        rstd = sb("rstd", [P, TILES])

        shared = sb("shared", [P, BLK * TILES * HEADS])
        L = shared[:].rearrange("p (i t h) -> p i t h", i=BLK, t=TILES)
        s16 = shared[:].bitcast(F16)
        xs_n, h_n = KH * UNIT, CH * UNIT
        xsplit = [[s16[:, (2 * b + j) * xs_n:(2 * b + j + 1) * xs_n].rearrange("p (k n) -> p k n", k=KH)
                   for j in range(2)] for b in range(2)]
        hsplit = [s16[:, 4 * xs_n + j * h_n:4 * xs_n + (j + 1) * h_n].rearrange("p (m n) -> p m n", m=CH)
                  for j in range(2)]
        used = (4 * xs_n + 2 * h_n) // 2
        sig = [shared[:, used + j * UNIT:used + (j + 1) * UNIT] for j in range(2)]
        hid = [shared[:, used + (2 + j) * UNIT:used + (3 + j) * UNIT] for j in range(2)]

        dec = sb("dec", [P, 8, TILES, HEADS])
        M = [sb(f"M{i}", [P, HEADS, BLK]) for i in range(2)]
        XB = [sb(f"XB{i}", [P, NB, HQ, Q * HP]) for i in range(2)]
        xp = sb("xp", [P, XPS, UNIT + TAPS - 1])
        tails = [sb(f"tail{b}", [P, CT, TAPS - 1]) for b in range(2)]
        xc = [sb(f"xc{b}", [P, CT, UNIT]) for b in range(2)]
        zs = sb("zs", [P, Q, UNIT])
        xnT = sb("xnT", [P, KH, UNIT])
        dtr = sb("dtr", [P, TILES, HEADS])
        dt_q = sb("dt_q", [P, TILES, HEADS])
        dt_e = sb("dt_e", [P, TILES, HEADS])
        dt_s = sb("dt_s", [P, TILES, HEADS])
        dt_p = sb("dt_p", [P, TILES, HEADS])
        dts = [sb(f"dts{b}", [P, TILES, HEADS]) for b in range(2)]
        a16 = [sb(f"a16_{b}", [P, 2, TILES, HEADS], F16) for b in range(2)]
        as16 = [sb(f"as16_{b}", [P, 2, TILES, NB, HQ], F16) for b in range(2)]
        S = [sb(f"S{b}", [P, D_SSM]) for b in range(2)]
        SD = sb("SD", [P, D_SSM])
        xdt = [sb(f"xdt{i}", [P, D_SSM]) for i in range(2)]
        xw = sb("xw", [P, D_SSM])
        xu = sb("xu", [P, NB - 1, D_SSM])
        Btok = sb("Btok", [P, STATE])
        Goff = sb("Goff", [P, P])
        Gd = sb("Gd", [P, NB, BLK])
        t1 = sb("t1", [P, D_SSM])
        t2 = sb("t2", [P, D_SSM])
        y = sb("y", [P, D_SSM])
        yd = sb("yd", [P, Q, P])
        g = sb("g", [P, Q, P])
        g2 = sb("g2", [P, Q, P])
        g2h = sb("g2h", [P, 2, P])
        g2s = sb("g2s", [P, P])
        ms = [sb(f"ms{i}", [P, 1]) for i in range(2)]
        rs = [sb(f"rs{i}", [P, 1]) for i in range(2)]

        wst = [xc[0][:].rearrange("p a b -> p (a b)")[:, 0:CH * HID], xc[1][:].rearrange("p a b -> p (a b)")[:, 0:CH * HID],
               xp[:].rearrange("p a b -> p (a b)")[:, 0:KH * FF]]
        wneg = M[0][:].rearrange("p a b -> p (a b)").bitcast(F16)[:, 0:CH * HID]
        wq16 = [M[1][:].rearrange("p a b -> p (a b)").bitcast(F16)[:, 0:CH * HID],
                M[1][:].rearrange("p a b -> p (a b)").bitcast(F16)[:, CH * HID:2 * CH * HID],
                zs[:].rearrange("p a b -> p (a b)").bitcast(F16)[:, 0:CH * HID]]
        wabs = shared[:, 0:CH * HID]
        wsum = sb("wsum", [P, 3])
        thr = sb("thr", [P, 2, 3])

        bank = [ctx.enter_context(nc.psum_tensor(f"bank{i}", [P, 512], F32)) for i in range(8)]
        A0, A1, B0, B1, YIN, YST, YOFF, DS = bank

        cst = sem("constants_made")
        zero = sem("zeros_set")
        wl = [sem(f"w_loaded{i}") for i in range(3)]
        pl = sem("params_loaded")
        alog = sem("A_log_loaded")
        absd = sem("abs_summed")
        sumd = sem("sums_spread")
        qstep = sem("quant_step")
        wT = sem("weights_turned")
        wTe = sem("weights_kept")
        setup = sem("params_ready")
        expA_r = sem("expA_ready")

        xln_in, xres_in, x_out = sem("xln_in"), sem("xres_in"), sem("x_out")
        ln_step, ln_pow, xn_ready = sem("ln_step"), sem("ln_pow"), sem("xn_ready")
        turned, xhi_ready, xlo_ready = sem("xn_turned"), sem("ffn_xhi_ready"), sem("ffn_xlo_ready")
        up_ready, sig_ready, hid_ready = sem("up_ready"), sem("sig_ready"), sem("hid_ready")
        hhi_ready, hlo_ready, down_done = sem("hhi_ready"), sem("hlo_ready"), sem("down_done")
        res_done = sem("residual_added")
        bank_full, bank_read = sem("proj_bank_full"), sem("proj_bank_read")
        dtc, dt_abs, dt_exp, a_ready = sem("dt_chain"), sem("dt_abs_ready"), sem("dt_exp_ready"), sem("a_ready")
        tail_in, tail_out, tap0, conv_step = sem("tail_in"), sem("tail_kept"), sem("tap0_done"), sem("conv_step")
        silu_c, silu_z = sem("xBC_ready"), sem("z_ready")
        seg_full, seg_read = sem("seg_bank_full"), sem("seg_bank_read")
        xT_r, bg_r, yst_r, yoff_r = sem("xtok_ready"), sem("BG_ready"), sem("yst_ready"), sem("yoff_ready")
        ds_r, yin_r, yT_r, out_r = sem("dS_ready"), sem("yin_ready"), sem("yT_ready"), sem("proj_out_ready")
        bt_r, xb_r, g2_r = sem("Btok_ready"), sem("XB_ready"), sem("g2_ready")
        xdt_r, gm_r, m_r = sem("xdt_ready"), sem("G_masked"), sem("M_ready")
        t1_r, t2_r, st_r, y_r = sem("t1_ready"), sem("t2_ready"), sem("state_ready"), sem("y_ready")
        yd_r, g_r, ms_r, fin_r = sem("yd_ready"), sem("g_ready"), sem("ms_ready"), sem("tile_done")
        xu_r, xw_r, sd_r, t12_r = sem("xu_ready"), sem("xw_ready"), sem("SD_ready"), sem("t12_ready")
        g2h_r, g2s_r, rs_r = sem("g2_halved"), sem("g2s_ready"), sem("rs_ready")

        ctx.enter_context(nc.allow_non_contiguous_dma(reason="a few hundred parameters, one to a partition"))
        block = ctx.enter_context(nc.Block())

        def layer_norm(dve, u, f=None):
            dve.wait_ge(xln_in, u * 16 + 16)
            for t in range(TILES):
                ins = nc.vector.bn_stats(stats[:, t, :], xln[:, t, :])
            ins.then_inc(ln_step, 1)
            dve.wait_ge(ln_step, LN_STEPS * u + 1)
            nc.vector.memset(veps[:], 0.0)
            for t in range(TILES):
                ins = nc.vector.bn_aggr(mv[:, t, :], stats[:, t, :])
            ins.then_inc(ln_step, 1)
            dve.wait_ge(ln_step, LN_STEPS * u + 2)
            nc.vector.tensor_scalar_add(veps[:], mv[:, :, 1], LN_EPS).then_inc(ln_step, 1)
            dve.wait_ge(ln_pow, u + 1)
            if f is not None:
                dve.wait_ge(turned, f)
            for t in range(TILES):
                ins = nc.vector.tensor_scalar(xn[:, t, :], xln[:, t, :], mv[:, t, 0:1], rstd[:, t:t + 1],
                                              ALU.subtract, ALU.mult)
            ins.then_inc(xn_ready, 1)

        def ln_power(pool, u):
            pool.wait_ge(ln_step, LN_STEPS * u + 3)
            nc.gpsimd.tensor_tensor(rstd[:], veps[:], mhalf[:], ALU.pow).then_inc(ln_pow, 1)

        def up_banks(m):
            return bank[2 * (m % 2)], bank[2 * (m % 2) + 1]

        down = [bank[4], bank[5]]
        xTb = [bank[6], bank[7]]

        def pe_turn(pe, u, ffn_u):
            pe.wait_ge(xn_ready, u + 1)
            if isinstance(ffn_u, int) and ffn_u == 0:
                pass
            else:
                pe.wait_ge(xlo_ready, ffn_u)
            for k in range(KH):
                for t in range(TILES):
                    ins = nc.tensor.transpose(xTb[k][:, t * P:(t + 1) * P], xn[:, t, k * P:(k + 1) * P], identf[:])
            ins.then_inc(turned, 1)

        def pe_up(pe, f, b, m):
            if m == 0:
                pe.wait_ge(xlo_ready, f + 1)
            if not (isinstance(f, int) and f == 0 and m < 2):
                pe.wait_ge(hid_ready, CH * f + m - 1)
            banks = up_banks(m)
            halves = [(banks[0], 2 * m * P, P), (banks[1], (2 * m + 1) * P, P)]
            if m == CH - 1:
                halves = [(banks[0], 2 * m * P, 2 * LAST)]
            for dst, col, n in halves:
                for k in range(KH):
                    for j in range(2):
                        ins = nc.tensor.matmul(dst[0:n, :], w12T[:, k, col:col + n], xsplit[b][j][:, k, :],
                                               start=(k == 0 and j == 0), stop=(k == KH - 1 and j == 1))
            ins.then_inc(up_ready, 1)

        def pe_down(pe, f, m):
            pe.wait_ge(hlo_ready, CH * f + m + 1)
            if m == 0 and not (isinstance(f, int) and f == 0):
                pe.wait_ge(res_done, f)
            n = P if m < CH - 1 else LAST
            for t in range(TILES):
                dst = down[t // 2][:, (t % 2) * HID:(t % 2 + 1) * HID]
                for j in range(2):
                    ins = nc.tensor.matmul(dst, hsplit[j][0:n, m, t * P:(t + 1) * P], w3T[0:n, m, :],
                                           start=(m == 0 and j == 0 and t % 2 == 0),
                                           stop=(m == CH - 1 and j == 1), skip_group_check=True)
            ins.then_inc(down_done, 1)

        def pe_ffn_unit(pe, f, u, b, first, has_next):
            for m in range(CH):
                pe_up(pe, f, b, m)
                if m == 3 and has_next:
                    pe_turn(pe, u + 1, f + 1)
                if m >= 2:
                    pe_down(pe, f, m - 2)
                elif not first:
                    pe_down(pe, f - 1, CH - 2 + m)

        def act_split_x(act, f, u, b):
            act.wait_ge(turned, f + 1)
            if not (isinstance(f, int) and f < 2):
                act.wait_ge(up_ready, CH * (f - 1))
            for k in range(KH):
                ins = nc.scalar.activation(xsplit[b][0][:, k, :], xTb[k][:], ACT.Copy, scale=XS)
            ins.then_inc(xhi_ready, 1)

        def dve_split_x(dve, f, b):
            dve.wait_ge(xhi_ready, f + 1)
            for k in range(KH):
                ins = nc.vector.scalar_tensor_tensor(out=xsplit[b][1][:, k, :], in0=xTb[k][:], scalar=XS,
                                                     in1=xsplit[b][0][:, k, :], op0=ALU.mult, op1=ALU.subtract)
            ins.then_inc(xlo_ready, 1)

        def rows(m):
            return P if m < CH - 1 else LAST

        def act_sig(act, f, m):
            act.wait_ge(up_ready, CH * f + m + 1)
            if not (isinstance(f, int) and f == 0 and m < 2):
                act.wait_ge(hid_ready, CH * f + m - 1)
            n, banks = rows(m), up_banks(m)
            src = banks[0][:] if m < CH - 1 else banks[0][LAST:2 * LAST, :]
            nc.scalar.activation(sig[m % 2][0:n, :], src, ACT.Sigmoid, scale=1.0 / XS).then_inc(sig_ready, 1)

        def act_hhi(act, f, m):
            act.wait_ge(hid_ready, CH * f + m + 1)
            if not (isinstance(f, int) and f == 0):
                act.wait_ge(down_done, CH * (f - 1) + m + 1)
            n = rows(m)
            nc.scalar.activation(hsplit[0][0:n, m, :], hid[m % 2][0:n, :], ACT.Copy).then_inc(hhi_ready, 1)

        def dve_hid(dve, f, m):
            dve.wait_ge(sig_ready, CH * f + m + 1)
            if not (isinstance(f, int) and f == 0 and m < 2):
                dve.wait_ge(hlo_ready, CH * f + m - 1)
            n, banks = rows(m), up_banks(m)
            src = banks[1][:] if m < CH - 1 else banks[0][0:LAST, :]
            nc.vector.tensor_tensor(hid[m % 2][0:n, :], src, sig[m % 2][0:n, :], ALU.mult).then_inc(hid_ready, 1)

        def dve_hlo(dve, f, m):
            dve.wait_ge(hhi_ready, CH * f + m + 1)
            n = rows(m)
            nc.vector.tensor_tensor(hsplit[1][0:n, m, :], hid[m % 2][0:n, :], hsplit[0][0:n, m, :],
                                    ALU.subtract).then_inc(hlo_ready, 1)

        def dve_residual(dve, f, u):
            dve.wait_ge(down_done, CH * (f + 1))
            dve.wait_ge(xres_in, 16 * (u + 1))
            for j in range(2):
                ins = nc.vector.tensor_tensor(xres[:, 2 * j:2 * j + 2, :], xres[:, 2 * j:2 * j + 2, :],
                                              down[j][:].rearrange("p (t n) -> p t n", t=2), ALU.add)
            ins.then_inc(res_done, 1)

        def act_ffn_unit(act, f, u, b, first, has_next):
            for m in range(CH):
                act_sig(act, f, m)
                if m > 0:
                    act_hhi(act, f, m - 1)
                elif not first:
                    act_hhi(act, f - 1, CH - 1)
                if m == 3 and has_next:
                    act_split_x(act, f + 1, u + 1, 1 - b)

        def dve_ffn_unit(dve, f, u, b, first, has_next):
            for m in range(CH):
                dve_hid(dve, f, m)
                if m > 0:
                    dve_hlo(dve, f, m - 1)
                elif not first:
                    dve_hlo(dve, f - 1, CH - 1)
                if m == 1 and has_next:
                    layer_norm(dve, u + 1, f + 1)
                if m == 2 and not first:
                    dve_residual(dve, f - 1, u - 1)
                if m == 3 and has_next:
                    dve_split_x(dve, f + 1, 1 - b)

        def units(eng, body, f0, u0):
            body(eng, f0, u0, 0, True, True)
            with eng.Fori(0, (UNITS - 2) // 2) as i:
                body(eng, i * 2 + (f0 + 1), i * 2 + (u0 + 1), 1, False, True)
                body(eng, i * 2 + (f0 + 2), i * 2 + (u0 + 2), 0, False, True)
            body(eng, f0 + UNITS - 1, u0 + UNITS - 1, 1, False, False)

        def pe_ffn(pe, f0, u0):
            pe_turn(pe, u0, f0)
            units(pe, pe_ffn_unit, f0, u0)
            for m in (CH - 2, CH - 1):
                pe_down(pe, f0 + UNITS - 1, m)

        def act_ffn(act, f0, u0):
            act_split_x(act, f0, u0, 0)
            units(act, act_ffn_unit, f0, u0)
            act_hhi(act, f0 + UNITS - 1, CH - 1)

        def dve_ffn(dve, f0, u0):
            layer_norm(dve, u0, f0)
            dve_split_x(dve, f0, 0)
            units(dve, dve_ffn_unit, f0, u0)
            dve_hlo(dve, f0 + UNITS - 1, CH - 1)
            dve_residual(dve, f0 + UNITS - 1, u0 + UNITS - 1)

        def tokens(dram, row):
            return dram[bass.ds(row, UNIT), :].rearrange("(t p) d -> p t d", p=P)

        def known(eng, value):
            return value if isinstance(value, int) else eng.snap(value)

        def sp_ffn(sp, src, dst, f0, u0):
            sp.dma_start(xln[:], tokens(src, 0)).then_inc(xln_in, 16)
            sp.wait_ge(xn_ready, u0 + 1)
            sp.dma_start(xln[:], tokens(src, UNIT)).then_inc(xln_in, 16)

            def unit(i, ahead):
                row, row2 = known(sp, i * UNIT), known(sp, i * UNIT + 2 * UNIT) if ahead else None
                read, added, stored = (known(sp, i + (u0 + 2)), known(sp, i + (f0 + 1)),
                                       known(sp, i * 16 + 16 * u0))
                sp.wait_ge(x_out, stored)
                sp.dma_start(xres[:], tokens(src, row)).then_inc(xres_in, 16)
                if ahead:
                    sp.wait_ge(xn_ready, read)
                    sp.dma_start(xln[:], tokens(src, row2)).then_inc(xln_in, 16)
                sp.wait_ge(res_done, added)
                sp.dma_start(tokens(dst, row), xres[:]).then_inc(x_out, 16)
            unit(0, True)
            with sp.Fori(1, UNITS - 2) as i:
                unit(i, True)
            unit(UNITS - 2, False)
            unit(UNITS - 1, False)

        M0 = UNITS

        def front_bank(b, n):
            return bank[(b * BANKS + n) % 2]

        def heads_bc(ap):
            return ap.unsqueeze(2).broadcast_to([P, HEADS, HP])

        def by_head(ap):
            return ap.rearrange("p (h c) -> p h c", h=HEADS)

        def pe_bank_free(pe, k_base, n, v_is_first):
            if v_is_first and n < 2:
                return
            pe.wait_ge(bank_read, k_base + n - 1)

        def pe_front(pe, kind, n, v, b):
            first = isinstance(v, int) and v == 0
            at = {"t": 0, "dt": KH, "c": KH + 1}[kind] + n
            dst = front_bank(b, at)
            pe_bank_free(pe, v * BANKS, at, first)
            if kind == "t":
                if n == 0:
                    pe.wait_ge(xn_ready, v + M0 + 1)
                for t in range(TILES):
                    ins = nc.tensor.transpose(dst[:, t * P:(t + 1) * P], xn[:, t, n * P:(n + 1) * P], identf[:])
            elif kind == "dt":
                pe.wait_ge(bank_read, v * BANKS + KH)
                for t in range(TILES):
                    for k in range(KH):
                        ins = nc.tensor.matmul(dst[:, t * HEADS:(t + 1) * HEADS], xnT[:, k, t * P:(t + 1) * P],
                                               wi[:, k, DT0:PROJ], start=(k == 0), stop=(k == KH - 1))
            else:
                col = D_SSM + n * P
                for k in range(KH):
                    ins = nc.tensor.matmul(dst[:], wi[:, k, col:col + P], xnT[:, k, :],
                                           start=(k == 0), stop=(k == KH - 1))
            ins.then_inc(bank_full, 1)

        def pe_z(pe, n, u, b):
            at = PROJS + n
            pe_bank_free(pe, u * BANKS, at, False)
            if n < 2:
                pe.wait_ge(xdt_r, u * TILES)
                pe.wait_ge(bt_r, u * TILES)
                pe.wait_ge(gm_r, u * TILES)
            dst = front_bank(b, at)
            for k in range(KH):
                ins = nc.tensor.matmul(dst[:], wi[:, k, n * P:(n + 1) * P], xnT[:, k, :],
                                       start=(k == 0), stop=(k == KH - 1))
            ins.then_inc(bank_full, 1)

        def masks_of(s):
            if s < SEG0:
                return [(tok_mask[:, n, :], False) for n in (2 * s, 2 * s + 1) if n < DECAYS]
            return [(blk_mask[:, n, :], True) for n in (2 * (s - SEG0), 2 * (s - SEG0) + 1)]

        def pe_seg(pe, s, u, b):
            dst = (B0, B1)[s % 2]
            if s < 2:
                pe.wait_ge((yd_r, fin_r)[s], u * TILES)
            else:
                pe.wait_ge(seg_read, u * SEGS + s - 1)
            if s == 0:
                pe.wait_ge(a_ready, u + 1)
            for j, (mask, stacked) in enumerate(masks_of(s)):
                for part in range(2):
                    src = (as16[b][:, part].rearrange("p t c h -> p (t c h)") if stacked
                           else a16[b][:, part].rearrange("p t h -> p (t h)"))
                    ins = nc.tensor.matmul(dst[:, j * 256:(j + 1) * 256], mask, src,
                                           start=(part == 0), stop=(part == 1))
            ins.then_inc(seg_full, 1)

        def pe_item(pe, item, u, b):
            kind, n = item
            if kind == "seg":
                pe_seg(pe, n, u, b)
            elif kind == "z":
                pe_z(pe, n, u, b)
            else:
                pe_front(pe, kind, n, u + 1, 1 - b)

        def pe_tile_in(pe, t, u, b, has_next):
            T = u * TILES + t
            if t == 0:
                pe.wait_ge(bank_read, (u + 1) * BANKS + (PROJS if has_next else 0))
                pe.wait_ge(silu_c, (u + 1) * CT)
            pe.wait_ge(xdt_r, T)
            tok = slice(t * P, (t + 1) * P)
            for q in range(Q):
                ins = nc.tensor.transpose(A0[:, q * P:(q + 1) * P], xc[b][:, q, tok], identf[:])
            ins.then_inc(xT_r, 1)
            pe.wait_ge(bt_r, T)
            pe.wait_ge(gm_r, T)
            nc.tensor.transpose(A1[:, 0:P], xc[b][:, Q, tok], identf[:])
            nc.tensor.matmul(A1[:, P:2 * P], xc[b][:, Q, tok], xc[b][:, Q + 1, tok], start=True, stop=True)
            for c in range(NB):
                blk = slice(t * P + c * BLK, t * P + (c + 1) * BLK)
                for q in range(Q):
                    ins = nc.tensor.matmul(A1[q * BLK:(q + 1) * BLK, 2 * P + c * BLK:2 * P + (c + 1) * BLK],
                                           xc[b][:, Q, blk], xc[b][:, Q + 1, blk], start=True, stop=True,
                                           tile_position=(0, q * BLK))
            ins.then_inc(bg_r, 1)

        def pe_tile_state(pe, t, u, b):
            T = u * TILES + t
            pe.wait_ge(t1_r, T)
            pe.wait_ge(st_r, T)
            for c in range(NB):
                blk = slice(t * P + c * BLK, t * P + (c + 1) * BLK)
                ins = nc.tensor.matmul(YST[c * BLK:(c + 1) * BLK, :], xc[b][:, Q + 1, blk], S[b][:],
                                       start=True, stop=True, tile_position=(0, c * BLK))
            ins.then_inc(yst_r, 1)
            pe.wait_ge(t2_r, T)
            pe.wait_ge(gm_r, T + 1)
            pe.wait_ge(xu_r, T + 1)
            for c in range(NB):
                ins = nc.tensor.matmul(YOFF[c * BLK:(c + 1) * BLK, :], Goff[:, c * BLK:(c + 1) * BLK],
                                       xu[:, max(c - 1, 0), :], start=True, stop=True,
                                       tile_position=(0, c * BLK))
            ins.then_inc(yoff_r, 1)
            pe.wait_ge(bt_r, T + 1)
            pe.wait_ge(xw_r, T + 1)
            nc.tensor.matmul(DS[:], Btok[:], xw[:], start=True, stop=True).then_inc(ds_r, 1)

        def pe_tile_diag(pe, t, u):
            T = u * TILES + t
            pe.wait_ge(y_r, T)
            pe.wait_ge(m_r, T + 1)
            pe.wait_ge(xb_r, T + 1)
            for h in range(HQ):
                for c in range(NB):
                    dst = YIN[c * BLK:(c + 1) * BLK, :].rearrange("i (q h p) -> i q h p", q=Q, h=HQ)[:, :, h, :]
                    ins = nc.tensor.matmul(dst, M[t % 2][:, c * HQ + h, :], XB[t % 2][:, c, h, :],
                                           start=True, stop=True, tile_position=(0, c * BLK))
            ins.then_inc(yin_r, 1)

        def pe_tile_turn(pe, t, u):
            T = u * TILES + t
            if t == 0:
                pe.wait_ge(seg_read, (u + 1) * SEGS)
            pe.wait_ge(yd_r, T)
            pe.wait_ge(y_r, T + 1)
            for q in range(Q):
                ins = nc.tensor.transpose(B0[:, q * P:(q + 1) * P], y[:, q * P:(q + 1) * P], identf[:])
            ins.then_inc(yT_r, 1)

        def pe_tile_out(pe, t, u):
            T = u * TILES + t
            pe.wait_ge(fin_r, T)
            pe.wait_ge(g_r, T + 1)
            for q in range(Q):
                nc.tensor.matmul(B1[:, 0:HID], g[:, q, :], wo[:, q, :], start=(q == 0), stop=(q == Q - 1))
            pe.wait_ge(g2s_r, T + 1)
            nc.tensor.matmul(B1[:, HID:HID + 1], g2s[:], ones[:, 0:1], start=True, stop=True).then_inc(out_r, 1)

        def pe_slot(pe, u, b, has_next):
            for item in slot_items(has_next):
                pe_item(pe, item, u, b)
            pe_tile_in(pe, 0, u, b, has_next)
            for t in range(TILES):
                pe_tile_state(pe, t, u, b)
                if t + 1 < TILES:
                    pe_tile_in(pe, t + 1, u, b, has_next)
                if t > 0:
                    pe_tile_turn(pe, t - 1, u)
                pe_tile_diag(pe, t, u)
                if t > 0:
                    pe_tile_out(pe, t - 1, u)
            pe_tile_turn(pe, TILES - 1, u)
            pe_tile_out(pe, TILES - 1, u)

        def act_front(act, kind, n, v, b):
            at = {"t": 0, "dt": KH, "c": KH + 1}[kind] + n
            src = front_bank(b, at)
            act.wait_ge(bank_full, v * BANKS + at + 1)
            if kind == "t":
                nc.scalar.activation(xnT[:, n, :], src[:], ACT.Copy).then_inc(bank_read, 1)
            elif kind == "dt":
                if not (isinstance(v, int) and v == 0):
                    act.wait_ge(dtc, v * DTC)
                nc.scalar.activation(dtr[:].rearrange("p t h -> p (t h)"), src[:, 0:TILES * HEADS],
                                     ACT.Copy).then_inc(bank_read, 1)
            else:
                rows_of = xp[:, n % XPS]
                if not (isinstance(v, int) and v == 0 and n < XPS):
                    act.wait_ge(tail_out, v * CT + n - XPS + 1)
                nc.scalar.activation(rows_of[:, 0:TAPS - 1], tails[b][:, n, :], ACT.Copy).then_inc(tail_in, 1)
                nc.scalar.activation(rows_of[:, TAPS - 1:], src[:], ACT.Copy).then_inc(bank_read, 1)
                act.wait_ge(tail_in, v * CT + n + 1)
                act.wait_ge(bank_read, v * BANKS + at + 1)
                nc.scalar.activation(xc[b][:, n, :], rows_of[:, 0:UNIT], ACT.Identity,
                                     scale=cw[:, n, 0:1], bias=cb[:, n:n + 1]).then_inc(tap0, 1)

        def act_z(act, n, u, b):
            act.wait_ge(bank_full, u * BANKS + PROJS + n + 1)
            if n == 0:
                act.wait_ge(g_r, u * TILES)
            nc.scalar.activation(zs[:, n, :], front_bank(b, PROJS + n)[:], ACT.Copy,
                                 scale=mupc[:, n:n + 1]).then_inc(bank_read, 1)

        def act_seg(act, s, u):
            act.wait_ge(seg_full, u * SEGS + s + 1)
            if s == 0:
                act.wait_ge(m_r, u * TILES)
                act.wait_ge(sd_r, u * TILES)
                act.wait_ge(xu_r, u * TILES)
                act.wait_ge(xw_r, u * TILES)
                act.wait_ge(t2_r, u * TILES)
            src = (B0, B1)[s % 2]
            n = len(masks_of(s))
            dst = dec[:, 2 * s:2 * s + n] if s < SEG0 else L[:, 2 * (s - SEG0):2 * (s - SEG0) + n]
            nc.scalar.activation(dst.rearrange("p n t h -> p (n t h)"), src[:, 0:n * 256], ACT.Exp,
                                 scale=-1.0 / AS).then_inc(seg_read, 1)

        def act_dt_exp(act, v):
            act.wait_ge(dt_abs, v + 1)
            nc.scalar.activation(dt_e[:], dt_e[:], ACT.Exp, scale=-1.0).then_inc(dt_exp, 1)

        def act_silu_conv(act, n, v, b):
            act.wait_ge(conv_step, v * CONV + (n + 1) * (TAPS - 1))
            nc.scalar.activation(xc[b][:, n, :], xc[b][:, n, :], ACT.Silu).then_inc(silu_c, 1)

        def act_silu_z(act, n, u):
            act.wait_ge(bank_read, u * BANKS + PROJS + n + 1)
            nc.scalar.activation(zs[:, n, :], zs[:, n, :], ACT.Silu).then_inc(silu_z, 1)

        def act_tile_in(act, t, u):
            T = u * TILES + t
            act.wait_ge(gm_r, T + 1)
            act.wait_ge(ds_r, T)
            nc.scalar.activation(Btok[:], A1[:, 0:P], ACT.Copy).then_inc(bt_r, 1)
            act.wait_ge(xdt_r, T + 1)
            act.wait_ge(yin_r, max(t - 1, 0) + u * TILES)
            for q in range(Q):
                for c in range(NB):
                    ins = nc.scalar.activation(
                        XB[t % 2][q * BLK:(q + 1) * BLK, c, :, q * HP:(q + 1) * HP],
                        xdt[t % 2][c * BLK:(c + 1) * BLK, q * P:(q + 1) * P].rearrange("p (h c) -> p h c", c=HP),
                        ACT.Copy)
            ins.then_inc(xb_r, 1)

        def act_tile_sq(act, t, u):
            T = u * TILES + t
            act.wait_ge(g_r, T + 1)
            act.wait_ge(g2s_r, T)
            nc.scalar.activation(g2[:], g[:], ACT.Square).then_inc(g2_r, 1)

        def act_slot(act, u, b, has_next):
            items = slot_items(has_next)
            for item in items:
                kind, n = item
                if kind == "seg":
                    act_seg(act, n, u)
                elif kind == "z":
                    act_z(act, n, u, b)
                else:
                    act_front(act, kind, n, u + 1, 1 - b)
                if item == ("c", 2):
                    act_dt_exp(act, u + 1)
            act_tile_in(act, 0, u)
            for n in range(Q):
                act_silu_z(act, n, u)
            for t in range(TILES):
                if t + 1 < TILES:
                    act_tile_in(act, t + 1, u)
                if has_next and t < CT // 2:
                    act_silu_conv(act, 2 * t, u + 1, 1 - b)
                    act_silu_conv(act, 2 * t + 1, u + 1, 1 - b)
                if t > 0:
                    act_tile_sq(act, t - 1, u)
            act_tile_sq(act, TILES - 1, u)

        def dve_dt_head(dve, v):
            c = v * DTC
            dve.wait_ge(bank_read, v * BANKS + KH + 1)
            mb = mup_dt[:].unsqueeze(1).broadcast_to([P, TILES, HEADS])
            bb = bias_dt[:].unsqueeze(1).broadcast_to([P, TILES, HEADS])
            nc.vector.tensor_tensor(dt_q[:], dtr[:], mb, ALU.mult).then_inc(dtc, 1)
            dve.wait_ge(dtc, c + 1)
            nc.vector.tensor_tensor(dt_q[:], dt_q[:], bb, ALU.add).then_inc(dtc, 1)
            dve.wait_ge(dtc, c + 2)
            nc.vector.scalar_tensor_tensor(out=dt_e[:], in0=dt_q[:], scalar=-1.0, in1=dt_q[:],
                                           op0=ALU.mult, op1=ALU.max).then_inc(dt_abs, 1)

        def dve_dt_tail(dve, v, b):
            n = v * DTC + 2

            def step(k):
                dve.wait_ge(dtc, n + k)

            dve.wait_ge(dt_exp, v + 1)
            nc.vector.tensor_scalar_add(dt_p[:], dt_e[:], 2.0).then_inc(dtc, 1)
            step(1)
            nc.vector.reciprocal(dt_s[:], dt_p[:]).then_inc(dtc, 1)
            step(2)
            nc.vector.tensor_tensor(dt_s[:], dt_e[:], dt_s[:], ALU.mult).then_inc(dtc, 1)
            step(3)
            nc.vector.tensor_tensor(dtr[:], dt_s[:], dt_s[:], ALU.mult).then_inc(dtc, 1)
            step(4)
            nc.vector.tensor_scalar(dt_p[:], dtr[:], 1.0 / (2 * SERIES - 1), None, ALU.mult).then_inc(dtc, 1)
            for k in range(SERIES - 2):
                step(5 + k)
                nc.vector.scalar_tensor_tensor(out=dt_p[:], in0=dt_p[:], scalar=1.0 / (2 * (SERIES - 2 - k) + 1),
                                               in1=dtr[:], op0=ALU.add, op1=ALU.mult).then_inc(dtc, 1)
            k = 5 + SERIES - 2
            step(k)
            nc.vector.scalar_tensor_tensor(out=dt_p[:], in0=dt_p[:], scalar=1.0, in1=dt_s[:],
                                           op0=ALU.add, op1=ALU.mult).then_inc(dtc, 1)
            step(k + 1)
            nc.vector.tensor_scalar(dt_p[:], dt_p[:], 2.0, None, ALU.mult).then_inc(dtc, 1)
            step(k + 2)
            nc.vector.scalar_tensor_tensor(out=dts[b][:], in0=dt_q[:], scalar=0.0, in1=dt_p[:],
                                           op0=ALU.max, op1=ALU.add).then_inc(dtc, 1)
            step(k + 3)
            ea = expA[:].unsqueeze(1).broadcast_to([P, TILES, HEADS])
            nc.vector.tensor_tensor(dt_p[:], dts[b][:], ea, ALU.mult).then_inc(dtc, 1)
            step(k + 4)
            nc.vector.tensor_scalar(dt_p[:], dt_p[:], A_MAX, AS, ALU.min, ALU.mult).then_inc(dtc, 1)
            step(k + 5)
            nc.vector.tensor_copy(a16[b][:, 0], dt_p[:]).then_inc(dtc, 1)
            step(k + 6)
            nc.vector.tensor_tensor(a16[b][:, 1], dt_p[:], a16[b][:, 0], ALU.subtract).then_inc(dtc, 1)
            assert 2 + k + 7 == DTC
            step(k + 7)
            for q in range(Q):
                for c in range(NB):
                    ins = nc.vector.tensor_copy(as16[b][q * BLK:(q + 1) * BLK, :, :, c, :],
                                                a16[b][c * BLK:(c + 1) * BLK, :, :, q * HQ:(q + 1) * HQ])
            ins.then_inc(a_ready, 1)

        def dve_conv(dve, n, v, b):
            dve.wait_ge(tap0, v * CT + n + 1)
            for k in range(1, TAPS):
                if k > 1:
                    dve.wait_ge(conv_step, v * CONV + n * (TAPS - 1) + k - 1)
                nc.vector.scalar_tensor_tensor(out=xc[b][:, n, :], in0=xp[:, n % XPS, k:k + UNIT], scalar=cw[:, n, k:k + 1],
                                               in1=xc[b][:, n, :], op0=ALU.mult, op1=ALU.add).then_inc(conv_step, 1)

            nc.vector.tensor_copy(tails[b][:, n, :], xp[:, n % XPS, UNIT:]).then_inc(tail_out, 1)

        def dve_tile_in(dve, t, u, b):
            T = u * TILES + t
            lag = max(t - 1, 0) + u * TILES
            dve.wait_ge(xT_r, T + 1)
            dve.wait_ge(xb_r, lag)
            dve.wait_ge(xu_r, lag)
            dve.wait_ge(xw_r, lag)
            nc.vector.tensor_tensor(by_head(xdt[t % 2][:]), by_head(A0[:]), heads_bc(dts[b][:, t, :]),
                                    ALU.mult).then_inc(xdt_r, 1)
            dve.wait_ge(bg_r, T + 1)
            dve.wait_ge(yoff_r, T)
            dve.wait_ge(m_r, T)
            nc.vector.tensor_tensor(Gd[:], A1[:, 2 * P:3 * P].rearrange("p (c i) -> p c i", c=NB),
                                    causal[:].unsqueeze(1).broadcast_to([P, NB, BLK]), ALU.mult)
            nc.vector.tensor_tensor(Goff[:], A1[:, P:2 * P], off_mask[:], ALU.mult).then_inc(gm_r, 1)

        def dve_tile_m(dve, t, u):
            T = u * TILES + t
            if t == 0:
                dve.wait_ge(seg_read, (u + 1) * SEGS)
            dve.wait_ge(gm_r, T + 1)
            dve.wait_ge(yin_r, max(t - 1, 0) + u * TILES)
            nc.vector.tensor_tensor(M[t % 2][:].rearrange("p (c h) i -> p c h i", c=NB),
                                    L[:, :, t, :].rearrange("p i (c h) -> p c h i", c=NB),
                                    Gd[:].unsqueeze(2).broadcast_to([P, NB, HQ, BLK]), ALU.mult).then_inc(m_r, 1)

        def dve_tile_state(dve, t, u, b):
            T = u * TILES + t
            dve.wait_ge(yst_r, T + 1)
            dve.wait_ge(y_r, T)
            nc.vector.tensor_tensor(by_head(t1[:]), by_head(YST[:]), heads_bc(dec[:, V_TILE, t, :]),
                                    ALU.mult).then_inc(t1_r, 1)
            dve.wait_ge(yoff_r, T + 1)
            dve.wait_ge(t12_r, T)
            nc.vector.tensor_tensor(by_head(t2[:]), by_head(YOFF[:]), heads_bc(dec[:, V_BLK, t, :]),
                                    ALU.mult).then_inc(t2_r, 1)
            dve.wait_ge(ds_r, T + 1)
            dve.wait_ge(sd_r, T + 1)
            nc.vector.tensor_tensor(S[b][:], SD[:], DS[:], ALU.add).then_inc(st_r, 1)

        def dve_tile_gate(dve, t, u, b):
            T = u * TILES + t
            tok = slice(t * P, (t + 1) * P)
            dve.wait_ge(yT_r, T + 1)
            dve.wait_ge(g_r, T)
            for q in range(Q):
                ins = nc.vector.scalar_tensor_tensor(out=yd[:, q, :], in0=xc[b][:, q, tok], scalar=dcol[:, q:q + 1],
                                                     in1=B0[:, q * P:(q + 1) * P], op0=ALU.mult, op1=ALU.add)
            ins.then_inc(yd_r, 1)
            if t == 0:
                dve.wait_ge(silu_z, (u + 1) * Q)
            dve.wait_ge(yd_r, T + 1)
            dve.wait_ge(out_r, T)
            dve.wait_ge(g2_r, T)
            nc.vector.tensor_tensor(g[:], yd[:], zs[:, :, tok], ALU.mult).then_inc(g_r, 1)

        def dve_tile_y(dve, t, u):
            T = u * TILES + t
            dve.wait_ge(yin_r, T + 1)
            dve.wait_ge(t12_r, T + 1)
            dve.wait_ge(yT_r, T)
            nc.vector.tensor_tensor(y[:], t1[:], YIN[:], ALU.add).then_inc(y_r, 1)

        def dve_tile_ms(dve, t, u):
            T = u * TILES + t
            dve.wait_ge(out_r, T + 1)
            nc.vector.tensor_scalar(ms[t % 2][:], B1[:, HID:HID + 1], 1.0 / D_SSM, RMS_EPS,
                                    ALU.mult, ALU.add).then_inc(ms_r, 1)

        def dve_tile_fin(dve, t, u):
            T = u * TILES + t
            if t == 0:
                dve.wait_ge(xres_in, (u + M0 + 1) * 16)
            dve.wait_ge(rs_r, T + 1)
            nc.vector.scalar_tensor_tensor(out=xres[:, t, :], in0=B1[:, 0:HID], scalar=rs[t % 2][:],
                                           in1=xres[:, t, :], op0=ALU.mult, op1=ALU.add).then_inc(fin_r, 1)

        def dve_slot(dve, u, b, has_next):
            if has_next:
                v, bv = u + 1, 1 - b
                layer_norm(dve, v + M0)
                dve_dt_head(dve, v)
                dve_conv(dve, 0, v, bv)
                dve_conv(dve, 1, v, bv)
                dve_conv(dve, 2, v, bv)
                dve_dt_tail(dve, v, bv)
                for n in range(3, CT):
                    dve_conv(dve, n, v, bv)
            dve_tile_in(dve, 0, u, b)
            dve_tile_m(dve, 0, u)
            for t in range(TILES):
                dve_tile_state(dve, t, u, b)
                if t >= 2:
                    dve_tile_fin(dve, t - 2, u)
                if t + 1 < TILES:
                    dve_tile_in(dve, t + 1, u, b)
                if t > 0:
                    dve_tile_gate(dve, t - 1, u, b)
                if t + 1 < TILES:
                    dve_tile_m(dve, t + 1, u)
                dve_tile_y(dve, t, u)
                if t > 0:
                    dve_tile_ms(dve, t - 1, u)
            dve_tile_fin(dve, TILES - 2, u)
            dve_tile_gate(dve, TILES - 1, u, b)
            dve_tile_ms(dve, TILES - 1, u)
            dve_tile_fin(dve, TILES - 1, u)

        def pool_tile_x(pool, t, u):
            T = u * TILES + t
            src = by_head(xdt[t % 2][:])
            pool.wait_ge(xdt_r, T + 1)
            if t == 0:
                pool.wait_ge(seg_read, u * SEGS + SEG0)
            pool.wait_ge(yoff_r, T)
            for i in range(NB - 1):
                ins = nc.gpsimd.tensor_tensor(by_head(xu[:, i, :]), src, heads_bc(dec[:, U_1 + i, t, :]), ALU.mult)
            ins.then_inc(xu_r, 1)
            pool.wait_ge(ds_r, T)
            nc.gpsimd.tensor_tensor(by_head(xw[:]), src, heads_bc(dec[:, W_END, t, :]), ALU.mult).then_inc(xw_r, 1)

        def pool_tile_state(pool, t, u, b):
            T = u * TILES + t
            pool.wait_ge(st_r, T)
            nc.gpsimd.tensor_tensor(by_head(SD[:]), by_head(S[b][:]), heads_bc(dec[:, TOTAL, t, :]),
                                    ALU.mult).then_inc(sd_r, 1)
            pool.wait_ge(t1_r, T + 1)
            pool.wait_ge(t2_r, T + 1)
            nc.gpsimd.tensor_tensor(t1[:], t1[:], t2[:], ALU.add).then_inc(t12_r, 1)

        def pool_tile_sq(pool, t, u):
            T = u * TILES + t
            pool.wait_ge(g2_r, T + 1)
            nc.gpsimd.tensor_tensor(g2h[:], g2[:, 0:2, :], g2[:, 2:4, :], ALU.add).then_inc(g2h_r, 1)
            pool.wait_ge(g2h_r, T + 1)
            pool.wait_ge(out_r, T)
            nc.gpsimd.tensor_tensor(g2s[:], g2h[:, 0, :], g2h[:, 1, :], ALU.add).then_inc(g2s_r, 1)

        def pool_tile_rs(pool, t, u):
            T = u * TILES + t
            pool.wait_ge(ms_r, T + 1)
            pool.wait_ge(fin_r, max(t - 1, 0) + u * TILES)
            nc.gpsimd.tensor_tensor(rs[t % 2][:], ms[t % 2][:], mhalf[:, 0:1], ALU.pow).then_inc(rs_r, 1)

        def pool_slot(pool, u, b, has_next):
            if has_next:
                ln_power(pool, u + (M0 + 1))
            pool_tile_x(pool, 0, u)
            for t in range(TILES):
                pool_tile_state(pool, t, u, b)
                if t + 1 < TILES:
                    pool_tile_x(pool, t + 1, u)
                if t > 0:
                    pool_tile_sq(pool, t - 1, u)
                    pool_tile_rs(pool, t - 1, u)
            pool_tile_sq(pool, TILES - 1, u)
            pool_tile_rs(pool, TILES - 1, u)

        def slots(eng, body):
            body(eng, 0, 0, True)
            with eng.Fori(0, UNITS // 2 - 1) as i:
                body(eng, i * 2 + 1, 1, True)
                body(eng, i * 2 + 2, 0, True)
            body(eng, UNITS - 1, 1, False)

        def row_of(i, b):
            return i * UNIT + b * LEN

        def sp_mamba(sp):
            def load(row):
                sp.dma_start(xln[:], tokens(mid1, row)).then_inc(xln_in, 16)

            def unit(i, b, ahead):
                u = i * 2 + b
                row, row2 = known(sp, row_of(i, b)), known(sp, row_of(i, b) + UNIT) if ahead else None
                read, summed, stored = (known(sp, u + (M0 + 2)), known(sp, u * TILES + TILES),
                                        known(sp, u * 16 + 16 * M0))
                sp.wait_ge(x_out, stored)
                sp.dma_start(xres[:], tokens(mid1, row)).then_inc(xres_in, 16)
                if ahead:
                    sp.wait_ge(xn_ready, read)
                    load(row2)
                sp.wait_ge(fin_r, summed)
                sp.dma_start(tokens(mid2, row), xres[:]).then_inc(x_out, 16)
            load(row_of(0, 0))
            sp.wait_ge(xn_ready, M0 + 1)
            load(row_of(0, 1))
            unit(0, 0, True)
            unit(0, 1, True)
            with sp.Fori(1, UNITS // 2 - 1) as i:
                unit(i, 0, True)
                unit(i, 1, True)
            unit(UNITS // 2 - 1, 0, False)
            unit(UNITS // 2 - 1, 1, False)

        def phase_wait(eng, n):
            eng.wait_ge(x_out, 16 * UNITS * n)

        NPARAM = 10

        @block.sync
        def _(sp):
            sp.wait_ge(zero, 1)
            for i, w in enumerate((w1, w2)):
                full = (CH - 1) * P
                v = wst[i].rearrange("p (r k) -> p r k", k=HID)
                sp.dma_start(v[:, 0:CH - 1, :], w[0:full, :].rearrange("(r p) k -> p r k", p=P)).then_inc(wl[i], 16)
                sp.dma_start(v[0:LAST, CH - 1, :], w[full:FF, :]).then_inc(wl[i], 16)
            sp.dma_start(wst[2].rearrange("p (o f) -> p o f", f=FF),
                         w3.rearrange("(o p) f -> p o f", p=P)).then_inc(wl[2], 16)
            sp_ffn(sp, x_flat, mid1, 0, 0)
            phase_wait(sp, 1)
            sp_mamba(sp)
            phase_wait(sp, 2)
            sp_ffn(sp, mid2, out_flat, UNITS, 2 * UNITS)
            phase_wait(sp, 3)

        @block.gpsimd
        def _(pool):
            fp = nc.gpsimd
            fp.memset(wst[0][:, (CH - 1) * HID:], 0.0)
            fp.memset(wst[1][:, (CH - 1) * HID:], 0.0).then_inc(zero, 1)
            fp.memset(identf[:], 0.0)
            fp.memset(ident16[:], 0.0)
            fp.memset(ones[:], 1.0)
            fp.memset(mhalf[:], -0.5)
            fp.memset(tok_mask[:], 1.0)
            fp.memset(causal[:], 1.0)
            fp.memset(off_mask[:], 1.0)
            fp.memset(blk_mask[:], 1.0).then_inc(cst, 1)
            def cols(ap, n):
                return ap.rearrange("(c p) -> p c", p=P)
            pool.dma_start(wi[:], W_in.rearrange("(k p) n -> p k n", p=P)).then_inc(pl, 16)
            pool.dma_start(wo[:], W_out.rearrange("(q p) n -> p q n", p=P)).then_inc(pl, 16)
            pool.dma_start(nw[:], cols(norm_w, Q)).then_inc(pl, 16)
            pool.dma_start(cw[:], conv_w.rearrange("(c p) k -> p c k", p=P)).then_inc(pl, 16)
            pool.dma_start(cb[:], cols(conv_b, CT)).then_inc(pl, 16)
            pool.dma_start(mupc[:], cols(mup[0:DT0], DT0 // P)).then_inc(pl, 16)
            for q in range(Q):
                pool.dma_start(dcol[:, q:q + 1],
                               D_w[q * HQ:(q + 1) * HQ].unsqueeze(1).broadcast_to([HQ, HP])).then_inc(pl, 16)
            pool.dma_start(mup_dt[:], mup[DT0:PROJ].unsqueeze(0).broadcast_to([P, HEADS])).then_inc(alog, 16)
            pool.dma_start(bias_dt[:], dt_bias.unsqueeze(0).broadcast_to([P, HEADS])).then_inc(alog, 16)
            pool.dma_start(expA[:], A_log.unsqueeze(0).broadcast_to([P, HEADS])).then_inc(alog, 16)

            pool.wait_ge(cst, 1)

            made = [1]

            def select(ap, op, fill, base, pattern, mult):
                pool.wait_ge(cst, made[0])
                made[0] += 1
                fp.affine_select(out=ap, in_=ap, compare_op=op, fill=fill, base=base, pattern=pattern,
                                 channel_multiplier=mult).then_inc(cst, 1)
            select(identf[:], ALU.not_equal, 1.0, 0, [[-1, P]], 1)
            select(ident16[:], ALU.not_equal, 1.0, 0, [[-1, P]], 1)
            select(tok_mask[:, V_BLK], ALU.is_ge, 0.0, 0, [[1, P]], -1)
            select(tok_mask[:, V_TILE], ALU.is_ge, 0.0, 0, [[1, P]], -1)
            for i in range(NB - 1):
                select(tok_mask[:, U_1 + i], ALU.is_gt, 0.0, 0, [[-1, P]], 1)
            select(tok_mask[:, W_END], ALU.is_gt, 0.0, 0, [[-1, P]], 1)
            select(off_mask[:].rearrange("p (c i) -> p c i", c=NB), ALU.is_gt, 0.0, 0, [[BLK, NB], [0, BLK]], -1)
            for q in range(NB):
                select(causal[q * BLK:(q + 1) * BLK, :], ALU.is_ge, 0.0, 0, [[1, BLK]], -1)
            bm = blk_mask[:].rearrange("p i (q j) -> p i q j", q=Q)
            select(bm, ALU.is_gt, 0.0, 0, [[0, BLK], [-BLK, Q], [-1, BLK]], 1)
            select(tok_mask[:, V_BLK].rearrange("p (c i) -> p c i", c=NB), ALU.is_ge, 0.0, 0,
                   [[-BLK, NB], [0, BLK]], 1)
            for i in range(NB - 1):
                select(tok_mask[:, U_1 + i], ALU.is_ge, 0.0, BLK * (i + 1) - 1, [[0, P]], -1)
            select(bm, ALU.is_ge, 0.0, 0, [[1, BLK], [BLK, Q], [0, BLK]], -1)

            pool.wait_ge(cst, made[0])
            for i in range(2):
                fp.memset(XB[i][:], 0.0)
                fp.memset(S[i][:], 0.0)
                ins = fp.memset(tails[i][:], 0.0)
            ins.then_inc(cst, 1)

            ln_power(pool, 0)
            with pool.Fori(1, UNITS) as i:
                ln_power(pool, i)
            ln_power(pool, M0)
            slots(pool, pool_slot)
            with pool.Fori(2 * UNITS, 3 * UNITS) as i:
                ln_power(pool, i)

        ALLC = 21

        @block.tensor
        def _(pe):
            pe.wait_ge(cst, ALLC)
            pe.wait_ge(absd, 3)
            nc.tensor.matmul(DS[:, 0:3], ones[:], wsum[:], start=True, stop=True).then_inc(sumd, 1)
            for i in range(6):
                w, k = i // 2, i % 2
                dst = bank[i][:].bitcast(F16)
                pe.wait_ge(qstep, 5 + 2 * w)
                if w < 2:
                    v = wq16[w].rearrange("p (r k) -> p r k", k=HID)
                    for r in range(CH):
                        n = P if r < CH - 1 else LAST
                        ins = nc.tensor.transpose(dst[:, r * P:r * P + n], v[0:n, r, k * P:(k + 1) * P],
                                                  ident16[0:n, 0:n])
                else:
                    v = wq16[2][:, 0:KH * FF].rearrange("p (o f) -> p o f", f=FF)
                    for r in range(CH):
                        n = P if r < CH - 1 else LAST
                        ins = nc.tensor.transpose(dst[0:n, r * P:(r + 1) * P], v[:, k, r * P:r * P + n], ident16[:])
                ins.then_inc(wT, 1)
            pe.wait_ge(wTe, 6)
            pe_ffn(pe, 0, 0)
            phase_wait(pe, 1)
            pe.wait_ge(setup, 2)
            for n in range(KH):
                pe_front(pe, "t", n, 0, 0)
            pe_front(pe, "dt", 0, 0, 0)
            for n in range(CT):
                pe_front(pe, "c", n, 0, 0)
            slots(pe, pe_slot)
            phase_wait(pe, 2)
            pe_ffn(pe, UNITS, 2 * UNITS)

        @block.scalar
        def _(act):
            for i in range(3):
                act.wait_ge(wl[i], 32 if i < 2 else 16)
                if i > 0:
                    act.wait_ge(absd, i)
                n = CH * HID if i < 2 else KH * FF
                nc.scalar.activation(wabs[:, 0:n], wst[i][:, 0:n], ACT.Abs, accum_out=wsum[:, i:i + 1]).then_inc(absd, 1)
            act.wait_ge(alog, 48)
            nc.scalar.activation(expA[:], expA[:], ACT.Exp).then_inc(expA_r, 1)
            for i in range(6):
                w, k = i // 2, i % 2
                src = bank[i][:].bitcast(F16)
                act.wait_ge(wT, i + 1)
                if w < 2:
                    scale = (1.0, W2S)[w]
                    main = w12T[:, k, 0:2 * (CH - 1) * P].rearrange("p (m s n) -> p m s n", s=2, n=P)[:, :, w, :]
                    col = 2 * (CH - 1) * P + (LAST if w == 0 else 0)
                    nc.scalar.activation(main, src[:, 0:(CH - 1) * P].rearrange("p (m n) -> p m n", n=P),
                                         ACT.Copy, scale=scale)
                    nc.scalar.activation(w12T[:, k, col:col + LAST], src[:, (CH - 1) * P:(CH - 1) * P + LAST],
                                         ACT.Copy, scale=scale).then_inc(wTe, 1)
                else:
                    nc.scalar.activation(w3T[:, 0:CH - 1, k * P:(k + 1) * P],
                                         src[:, 0:(CH - 1) * P].rearrange("p (m n) -> p m n", n=P),
                                         ACT.Copy, scale=W3S)
                    nc.scalar.activation(w3T[0:LAST, CH - 1, k * P:(k + 1) * P],
                                         src[0:LAST, (CH - 1) * P:CH * P], ACT.Copy, scale=W3S).then_inc(wTe, 1)
            act_ffn(act, 0, 0)
            phase_wait(act, 1)
            act.wait_ge(setup, 2)
            act.wait_ge(cst, ALLC)
            for n in range(KH):
                act_front(act, "t", n, 0, 0)
            act_front(act, "dt", 0, 0, 0)
            for n in range(CT):
                act_front(act, "c", n, 0, 0)
                if n == 2:
                    act_dt_exp(act, 0)
            for n in range(CT):
                act_silu_conv(act, n, 0, 0)
            slots(act, act_slot)
            phase_wait(act, 2)
            act_ffn(act, UNITS, 2 * UNITS)

        @block.vector
        def _(dve):
            dve.wait_ge(sumd, 1)
            nc.vector.tensor_scalar(thr[:, 0, :], DS[:, 0:3], 1.0 / (FF * HID), Q_EPS, ALU.mult, ALU.add).then_inc(qstep, 1)
            dve.wait_ge(qstep, 1)
            nc.vector.tensor_scalar(thr[:, 1, :], thr[:, 0, :], -0.5, None, ALU.mult).then_inc(qstep, 1)
            dve.wait_ge(qstep, 2)
            nc.vector.tensor_scalar(thr[:, 0, :], thr[:, 0, :], 0.5, None, ALU.mult).then_inc(qstep, 1)
            dve.wait_ge(qstep, 3)
            for i in range(3):
                n = CH * HID if i < 2 else KH * FF
                nc.vector.tensor_scalar(wneg[:, 0:n], wst[i][:, 0:n], thr[:, 1, i:i + 1], None, ALU.is_lt).then_inc(qstep, 1)
                dve.wait_ge(qstep, 4 + 2 * i)
                nc.vector.scalar_tensor_tensor(out=wq16[i][:, 0:n], in0=wst[i][:, 0:n], scalar=thr[:, 0, i:i + 1],
                                               in1=wneg[:, 0:n], op0=ALU.is_gt, op1=ALU.subtract).then_inc(qstep, 1)
                dve.wait_ge(qstep, 5 + 2 * i)
            dve.wait_ge(pl, 16 * NPARAM)
            for q in range(Q):
                ins = nc.vector.tensor_scalar(wo[:, q, :], wo[:, q, :], nw[:, q:q + 1], None, ALU.mult)
            ins.then_inc(setup, 1)
            for n in range(CT):
                ins = nc.vector.tensor_scalar(cw[:, n, :], cw[:, n, :], mupc[:, Q + n:Q + n + 1], None, ALU.mult)
            ins.then_inc(setup, 1)
            dve.wait_ge(setup, 2)
            dve.wait_ge(expA_r, 1)
            dve_ffn(dve, 0, 0)
            phase_wait(dve, 1)
            layer_norm(dve, M0)
            dve_dt_head(dve, 0)
            for n in range(3):
                dve_conv(dve, n, 0, 0)
            dve_dt_tail(dve, 0, 0)
            for n in range(3, CT):
                dve_conv(dve, n, 0, 0)
            slots(dve, dve_slot)
            phase_wait(dve, 2)
            dve_ffn(dve, UNITS, 2 * UNITS)


_INS = ['L0_attn_hidden_states', 'L0_attn_W_in', 'L0_attn_conv_w', 'L0_attn_conv_b', 'L0_attn_A_log', 'L0_attn_D',
        'L0_attn_dt_bias', 'L0_attn_norm_w', 'L0_attn_W_out', 'L0_attn_mup_vector', 'L0_ffn_w1', 'L0_ffn_w2',
        'L0_ffn_w3']


def kernel(**inputs):
    import numpy as _np
    import concourse.bacc as _bacc
    from concourse import mybir as _mybir
    from concourse.bass_utils import run_bass_kernel_spmd as _run

    nc = _bacc.Bacc("TRN2", target_bir_lowering=False, num_devices=1)
    arrays, args = {}, []
    for name in _INS:
        a = _np.ascontiguousarray(inputs[name])
        arrays[f"in_{name}_dram"] = a
        args.append(nc.dram_tensor(f"in_{name}_dram", a.shape, _mybir.dt.from_np(a.dtype), kind="ExternalInput").ap())
    out = nc.dram_tensor("out_0_dram", (BATCH, LEN, HID), _mybir.dt.float32, kind="ExternalOutput").ap()
    macaron_program(nc, *args, out)
    r = _run(nc, [arrays], core_ids=[0])
    return r.results[0]["out_0_dram"]
```

```python
from contextlib import ExitStack

import concourse.bass as bass
from concourse import mybir

F32 = mybir.dt.float32
F16 = mybir.dt.float16
ALU = mybir.AluOpType
ACT = mybir.ActivationFunctionType

P = 128
TILES = 4
UNIT = P * TILES
BATCH, LEN, HID = 2, 2048, 256
UNITS = BATCH * LEN // UNIT
KH = HID // P
FF = 704
CH = (FF + P - 1) // P
LAST = FF - (CH - 1) * P
D_SSM, STATE, HEADS, TAPS = 512, 128, 64, 4
HP = D_SSM // HEADS
Q = D_SSM // P
HQ = HEADS // Q
CT = Q + 2
BLK = 32
NB = P // BLK
PROJ = 2 * D_SSM + 2 * STATE + HEADS
DT0 = 2 * D_SSM + 2 * STATE
LN_EPS, RMS_EPS, Q_EPS = 1e-5, 1e-5, 1e-8
XS = 2.0 ** 11
W2S = 2.0 ** -4
W3S = 0.5 / (XS * W2S)
A_MAX = 120.0
AS = 2.0 ** 9
XPS = 3
SERIES = 8

V_BLK, V_TILE, U_1, U_2, U_3, W_END, TOTAL = range(7)
DECAYS = 7
SEG0 = 4
SEGS = SEG0 + BLK // 2
PROJS = KH + 1 + CT
BANKS = PROJS + Q

LN_STEPS = 3
CONV = CT * (TAPS - 1)
DTC = 12 + SERIES


def slot_head(has_next):
    seg = [("seg", s) for s in range(SEGS)]
    front = has_next
    return (seg[0:4] + [("out", 0), ("z", 0)] + seg[4:5] + [("z", 1)] + seg[5:6] + [("state", 0)]
            + [("z", 2)] + seg[6:7] + [("z", 3)] + seg[7:9]
            + ([("t", 0)] if front else []) + seg[9:10] + ([("t", 1)] if front else []) + seg[10:11]
            + ([("dt", 0)] if front else []) + seg[11:])


def macaron_program(nc, x_in, W_in, conv_w, conv_b, A_log, D_w, dt_bias, norm_w, W_out, mup,
                    w1, w2, w3, out):
    ctx = ExitStack()
    with ctx:
        def sb(name, shape, dt=F32):
            return ctx.enter_context(nc.sbuf_tensor(name, shape, dt))

        def sem(name):
            return ctx.enter_context(nc.semaphore(name))

        mid1 = nc.dram_tensor("x_after_ffn1", (BATCH * LEN, HID), F32, kind="Internal").ap()
        mid2 = nc.dram_tensor("x_after_mamba", (BATCH * LEN, HID), F32, kind="Internal").ap()
        x_flat = x_in.rearrange("b l d -> (b l) d")
        out_flat = out.rearrange("b l d -> (b l) d")

        identf = sb("identf", [P, P])
        ident16 = sb("ident16", [P, P], F16)
        ones = sb("ones", [P, P])
        mhalf = sb("mhalf", [P, TILES])
        tok_mask = sb("tok_mask", [P, 8, P], F16)
        blk_mask = sb("blk_mask", [P, BLK, P], F16)
        causal = sb("causal", [P, BLK])
        off_mask = sb("off_mask", [P, P])
        wi = sb("wi", [P, KH, PROJ])
        wo = sb("wo", [P, Q, HID])
        w12T = sb("w12T", [P, KH, 2 * FF], F16)
        w3T = sb("w3T", [P, CH, HID], F16)
        nw = sb("nw", [P, Q])
        cw = sb("cw", [P, CT, TAPS])
        cb = sb("cb", [P, CT])
        mupc = sb("mupc", [P, DT0 // P])
        dcol = sb("dcol", [P, Q])
        mup_dt = sb("mup_dt", [P, HEADS])
        bias_dt = sb("bias_dt", [P, HEADS])
        expA = sb("expA", [P, HEADS])
        xln = sb("xln", [P, TILES, HID])
        xres = sb("xres", [P, TILES, HID])
        xn = sb("xn", [P, TILES, HID])
        stats = sb("stats", [P, TILES, 6])
        mv = sb("mv", [P, TILES, 2])
        veps = sb("veps", [P, TILES])
        rstd = sb("rstd", [P, TILES])

        shared = sb("shared", [P, BLK * TILES * HEADS])
        L = shared[:].rearrange("p (i t h) -> p i t h", i=BLK, t=TILES)
        s16 = shared[:].bitcast(F16)
        xs_n, h_n = KH * UNIT, CH * UNIT
        xsplit = [[s16[:, (2 * b + j) * xs_n:(2 * b + j + 1) * xs_n].rearrange("p (k n) -> p k n", k=KH)
                   for j in range(2)] for b in range(2)]
        hsplit = [s16[:, 4 * xs_n + j * h_n:4 * xs_n + (j + 1) * h_n].rearrange("p (m n) -> p m n", m=CH)
                  for j in range(2)]
        used = (4 * xs_n + 2 * h_n) // 2
        sig = [shared[:, used + j * UNIT:used + (j + 1) * UNIT] for j in range(2)]
        hid = [shared[:, used + (2 + j) * UNIT:used + (3 + j) * UNIT] for j in range(2)]

        dec = sb("dec", [P, 8, TILES, HEADS])
        M = [sb(f"M{i}", [P, HEADS, BLK]) for i in range(2)]
        XB = [sb(f"XB{i}", [P, NB, HQ, Q * HP]) for i in range(2)]
        xp = sb("xp", [P, XPS, UNIT + TAPS - 1])
        tails = [sb(f"tail{b}", [P, CT, TAPS - 1]) for b in range(2)]
        xc = [sb(f"xc{b}", [P, CT, UNIT]) for b in range(2)]
        zs = sb("zs", [P, Q, UNIT])
        xnT = sb("xnT", [P, KH, UNIT])
        dtr = sb("dtr", [P, TILES, HEADS])
        dt_q = sb("dt_q", [P, TILES, HEADS])
        dt_e = sb("dt_e", [P, TILES, HEADS])
        dt_s = sb("dt_s", [P, TILES, HEADS])
        dt_p = sb("dt_p", [P, TILES, HEADS])
        dts = [sb(f"dts{b}", [P, TILES, HEADS]) for b in range(2)]
        a16 = [sb(f"a16_{b}", [P, 2, TILES, HEADS], F16) for b in range(2)]
        as16 = [sb(f"as16_{b}", [P, 2, TILES, NB, HQ], F16) for b in range(2)]
        S = [sb(f"S{b}", [P, D_SSM]) for b in range(2)]
        SD = sb("SD", [P, D_SSM])
        xdt = [sb(f"xdt{i}", [P, D_SSM]) for i in range(2)]
        xw = sb("xw", [P, D_SSM])
        xu = sb("xu", [P, NB - 1, D_SSM])
        Btok = sb("Btok", [P, STATE])
        Goff = sb("Goff", [P, P])
        Gd = sb("Gd", [P, NB, BLK])
        t1 = sb("t1", [P, D_SSM])
        t2 = sb("t2", [P, D_SSM])
        y = sb("y", [P, D_SSM])
        yd = sb("yd", [P, Q, P])
        g = sb("g", [P, Q, P])
        g2 = sb("g2", [P, Q, P])
        g2h = sb("g2h", [P, 2, P])
        g2s = sb("g2s", [P, P])
        ms = [sb(f"ms{i}", [P, 1]) for i in range(2)]
        rs = [sb(f"rs{i}", [P, 1]) for i in range(2)]

        wst = [xc[0][:].rearrange("p a b -> p (a b)")[:, 0:CH * HID], xc[1][:].rearrange("p a b -> p (a b)")[:, 0:CH * HID],
               xp[:].rearrange("p a b -> p (a b)")[:, 0:KH * FF]]
        wneg = M[0][:].rearrange("p a b -> p (a b)").bitcast(F16)[:, 0:CH * HID]
        wq16 = [M[1][:].rearrange("p a b -> p (a b)").bitcast(F16)[:, 0:CH * HID],
                M[1][:].rearrange("p a b -> p (a b)").bitcast(F16)[:, CH * HID:2 * CH * HID],
                zs[:].rearrange("p a b -> p (a b)").bitcast(F16)[:, 0:CH * HID]]
        wabs = shared[:, 0:CH * HID]
        wsum = sb("wsum", [P, 3])
        thr = sb("thr", [P, 2, 3])

        bank = [ctx.enter_context(nc.psum_tensor(f"bank{i}", [P, 512], F32)) for i in range(8)]
        B0, B1, YIN, YST, YOFF, DS = bank[2:]
        YT, XT, BG, OUT = YIN, YST, YOFF, DS

        cst = sem("constants_made")
        zero = sem("zeros_set")
        wl = [sem(f"w_loaded{i}") for i in range(3)]
        pl = sem("params_loaded")
        absd = sem("abs_summed")
        sumd = sem("sums_spread")
        qstep = sem("quant_step")
        wT = sem("weights_turned")
        wTe = sem("weights_kept")
        setup = sem("params_ready")
        expA_r = sem("expA_ready")

        xln_in, xres_in, x_out = sem("xln_in"), sem("xres_in"), sem("x_out")
        ln_step, ln_pow, xn_ready = sem("ln_step"), sem("ln_pow"), sem("xn_ready")
        turned, xhi_ready, xlo_ready = sem("xn_turned"), sem("ffn_xhi_ready"), sem("ffn_xlo_ready")
        up_ready, sig_ready, hid_ready = sem("up_ready"), sem("sig_ready"), sem("hid_ready")
        hhi_ready, hlo_ready, down_done = sem("hhi_ready"), sem("hlo_ready"), sem("down_done")
        res_done = sem("residual_added")
        bank_full, bank_read = sem("proj_bank_full"), sem("proj_bank_read")
        dtc, dt_abs, dt_exp, a_ready = sem("dt_chain"), sem("dt_abs_ready"), sem("dt_exp_ready"), sem("a_ready")
        tail_in, tail_out, tap0, conv_step = sem("tail_in"), sem("tail_kept"), sem("tap0_done"), sem("conv_step")
        silu_c, silu_z = sem("xBC_ready"), sem("z_ready")
        seg_full, seg_read = sem("seg_bank_full"), sem("seg_bank_read")
        xT_r, bg_r, yst_r, yoff_r = sem("xtok_ready"), sem("BG_ready"), sem("yst_ready"), sem("yoff_ready")
        ds_r, yin_r, yT_r, out_r = sem("dS_ready"), sem("yin_ready"), sem("yT_ready"), sem("proj_out_ready")
        bt_r, xb_r, g2_r = sem("Btok_ready"), sem("XB_ready"), sem("g2_ready")
        xdt_r, gm_r, m_r = sem("xdt_ready"), sem("G_masked"), sem("M_ready")
        t1_r, t2_r, st_r, y_r = sem("t1_ready"), sem("t2_ready"), sem("state_ready"), sem("y_ready")
        yd_r, g_r, ms_r, fin_r = sem("yd_ready"), sem("g_ready"), sem("ms_ready"), sem("tile_done")
        xu_r, xw_r, sd_r, t12_r = sem("xu_ready"), sem("xw_ready"), sem("SD_ready"), sem("t12_ready")
        g2h_r, g2s_r, rs_r = sem("g2_halved"), sem("g2s_ready"), sem("rs_ready")

        ctx.enter_context(nc.allow_non_contiguous_dma(reason="a few hundred parameters, one to a partition"))
        block = ctx.enter_context(nc.Block())

        def ln_stats(dve, u):
            dve.wait_ge(xln_in, u * 16 + 16)
            for t in range(TILES):
                ins = nc.vector.bn_stats(stats[:, t, :], xln[:, t, :])
            ins.then_inc(ln_step, 1)
            dve.wait_ge(ln_step, LN_STEPS * u + 1)
            nc.vector.memset(veps[:], 0.0)
            for t in range(TILES):
                ins = nc.vector.bn_aggr(mv[:, t, :], stats[:, t, :])
            ins.then_inc(ln_step, 1)
            dve.wait_ge(ln_step, LN_STEPS * u + 2)
            nc.vector.tensor_scalar_add(veps[:], mv[:, :, 1], LN_EPS).then_inc(ln_step, 1)

        def ln_apply(dve, u, f=None):
            dve.wait_ge(ln_pow, u + 1)
            if f is not None:
                dve.wait_ge(turned, f)
            for t in range(TILES):
                ins = nc.vector.tensor_scalar(xn[:, t, :], xln[:, t, :], mv[:, t, 0:1], rstd[:, t:t + 1],
                                              ALU.subtract, ALU.mult)
            ins.then_inc(xn_ready, 1)

        def ln_power(pool, u):
            pool.wait_ge(ln_step, LN_STEPS * u + 3)
            nc.gpsimd.tensor_tensor(rstd[:], veps[:], mhalf[:], ALU.pow).then_inc(ln_pow, 1)

        def up_banks(m):
            return bank[2 * (m % 2)], bank[2 * (m % 2) + 1]

        down = [bank[4], bank[5]]
        xTb = [bank[6], bank[7]]

        def pe_turn(pe, u, ffn_u):
            pe.wait_ge(xn_ready, u + 1)
            if isinstance(ffn_u, int) and ffn_u == 0:
                pass
            else:
                pe.wait_ge(xlo_ready, ffn_u)
            for k in range(KH):
                for t in range(TILES):
                    ins = nc.tensor.transpose(xTb[k][:, t * P:(t + 1) * P], xn[:, t, k * P:(k + 1) * P], identf[:])
            ins.then_inc(turned, 1)

        def pe_up(pe, f, b, m):
            if m == 0:
                pe.wait_ge(xlo_ready, f + 1)
            if not (isinstance(f, int) and f == 0 and m < 2):
                pe.wait_ge(hid_ready, CH * f + m - 1)
            banks = up_banks(m)
            halves = [(banks[0], 2 * m * P, P), (banks[1], (2 * m + 1) * P, P)]
            if m == CH - 1:
                halves = [(banks[0], 2 * m * P, 2 * LAST)]
            for dst, col, n in halves:
                for k in range(KH):
                    for j in range(2):
                        ins = nc.tensor.matmul(dst[0:n, :], w12T[:, k, col:col + n], xsplit[b][j][:, k, :],
                                               start=(k == 0 and j == 0), stop=(k == KH - 1 and j == 1))
            ins.then_inc(up_ready, 1)

        def pe_down(pe, f, m):
            pe.wait_ge(hlo_ready, CH * f + m + 1)
            if m == 0 and not (isinstance(f, int) and f == 0):
                pe.wait_ge(res_done, f)
            n = P if m < CH - 1 else LAST
            for t in range(TILES):
                dst = down[t // 2][:, (t % 2) * HID:(t % 2 + 1) * HID]
                for j in range(2):
                    ins = nc.tensor.matmul(dst, hsplit[j][0:n, m, t * P:(t + 1) * P], w3T[0:n, m, :],
                                           start=(m == 0 and j == 0 and t % 2 == 0),
                                           stop=(m == CH - 1 and j == 1), skip_group_check=True)
            ins.then_inc(down_done, 1)

        def pe_ffn_unit(pe, f, u, b, first, has_next, ahead):
            for m in range(CH):
                pe_up(pe, f, b, m)
                if m == 4 and has_next:
                    pe_turn(pe, u + 1, f + 1)
                if m >= 2:
                    pe_down(pe, f, m - 2)
                elif not first:
                    pe_down(pe, f - 1, CH - 2 + m)

        def act_split_x(act, f, u, b):
            act.wait_ge(turned, f + 1)
            if not (isinstance(f, int) and f < 2):
                act.wait_ge(up_ready, CH * (f - 1))
            for k in range(KH):
                ins = nc.scalar.activation(xsplit[b][0][:, k, :], xTb[k][:], ACT.Copy, scale=XS)
            ins.then_inc(xhi_ready, 1)

        def dve_split_x(dve, f, b):
            dve.wait_ge(xhi_ready, f + 1)
            for k in range(KH):
                ins = nc.vector.scalar_tensor_tensor(out=xsplit[b][1][:, k, :], in0=xTb[k][:], scalar=XS,
                                                     in1=xsplit[b][0][:, k, :], op0=ALU.mult, op1=ALU.subtract)
            ins.then_inc(xlo_ready, 1)

        def rows(m):
            return P if m < CH - 1 else LAST

        def act_sig(act, f, m):
            act.wait_ge(up_ready, CH * f + m + 1)
            if not (isinstance(f, int) and f == 0 and m < 2):
                act.wait_ge(hid_ready, CH * f + m - 1)
            n, banks = rows(m), up_banks(m)
            src = banks[0][:] if m < CH - 1 else banks[0][LAST:2 * LAST, :]
            nc.scalar.activation(sig[m % 2][0:n, :], src, ACT.Sigmoid, scale=1.0 / XS).then_inc(sig_ready, 1)

        def act_hhi(act, f, m):
            act.wait_ge(hid_ready, CH * f + m + 1)
            if not (isinstance(f, int) and f == 0):
                act.wait_ge(down_done, CH * (f - 1) + m + 1)
            n = rows(m)
            nc.scalar.activation(hsplit[0][0:n, m, :], hid[m % 2][0:n, :], ACT.Copy).then_inc(hhi_ready, 1)

        def dve_hid(dve, f, m):
            dve.wait_ge(sig_ready, CH * f + m + 1)
            if not (isinstance(f, int) and f == 0 and m < 2):
                dve.wait_ge(hlo_ready, CH * f + m - 1)
            n, banks = rows(m), up_banks(m)
            src = banks[1][:] if m < CH - 1 else banks[0][0:LAST, :]
            nc.vector.tensor_tensor(hid[m % 2][0:n, :], src, sig[m % 2][0:n, :], ALU.mult).then_inc(hid_ready, 1)

        def pool_hlo(pool, f, m):
            pool.wait_ge(hhi_ready, CH * f + m + 1)
            n = rows(m)
            nc.gpsimd.tensor_tensor(hsplit[1][0:n, m, :], hid[m % 2][0:n, :], hsplit[0][0:n, m, :],
                                    ALU.subtract).then_inc(hlo_ready, 1)

        def dve_residual(dve, f, u):
            dve.wait_ge(down_done, CH * (f + 1))
            dve.wait_ge(xres_in, 16 * (u + 1))
            for j in range(2):
                ins = nc.vector.tensor_tensor(xres[:, 2 * j:2 * j + 2, :], xres[:, 2 * j:2 * j + 2, :],
                                              down[j][:].rearrange("p (t n) -> p t n", t=2), ALU.add)
            ins.then_inc(res_done, 1)

        def act_ffn_unit(act, f, u, b, first, has_next, ahead):
            for m in range(CH):
                act_sig(act, f, m)
                if m > 0:
                    act_hhi(act, f, m - 1)
                elif not first:
                    act_hhi(act, f - 1, CH - 1)
                if m == 4 and has_next:
                    act_split_x(act, f + 1, u + 1, 1 - b)

        def dve_ffn_unit(dve, f, u, b, first, has_next, ahead):
            for m in range(CH):
                dve_hid(dve, f, m)
                if m == 1 and not first:
                    dve_residual(dve, f - 1, u - 1)
                if m == 1 and ahead:
                    ln_stats(dve, u + 1)
                if m == 2 and ahead:
                    ln_apply(dve, u + 1, f + 1)
                if m == 4 and has_next:
                    dve_split_x(dve, f + 1, 1 - b)

        def pool_ffn_unit(pool, f, u, b, first, has_next, ahead):
            for m in range(CH):
                if m > 0:
                    pool_hlo(pool, f, m - 1)
                elif not first:
                    pool_hlo(pool, f - 1, CH - 1)
                if m == 1 and ahead:
                    ln_power(pool, u + 1)

        def units(eng, body, f0, u0, more):
            body(eng, f0, u0, 0, True, True, True)
            with eng.Fori(0, (UNITS - 2) // 2) as i:
                body(eng, i * 2 + (f0 + 1), i * 2 + (u0 + 1), 1, False, True, True)
                body(eng, i * 2 + (f0 + 2), i * 2 + (u0 + 2), 0, False, True, True)
            body(eng, f0 + UNITS - 1, u0 + UNITS - 1, 1, False, False, more)

        def pe_ffn(pe, f0, u0, more):
            units(pe, pe_ffn_unit, f0, u0, more)
            for m in (CH - 2, CH - 1):
                pe_down(pe, f0 + UNITS - 1, m)

        def act_ffn(act, f0, u0, more):
            units(act, act_ffn_unit, f0, u0, more)
            act_hhi(act, f0 + UNITS - 1, CH - 1)

        def dve_ffn(dve, f0, u0, more):
            units(dve, dve_ffn_unit, f0, u0, more)
            dve_residual(dve, f0 + UNITS - 1, u0 + UNITS - 1)

        def pool_ffn(pool, f0, u0, more):
            units(pool, pool_ffn_unit, f0, u0, more)
            pool_hlo(pool, f0 + UNITS - 1, CH - 1)

        def tokens(dram, row):
            return dram[bass.ds(row, UNIT), :].rearrange("(t p) d -> p t d", p=P)

        def known(eng, value):
            return value if isinstance(value, int) else eng.snap(value)

        def sp_ffn(sp, src, dst, f0, u0, after):
            def unit(i, ahead_src, ahead_row):
                row, row2 = known(sp, i * UNIT), known(sp, ahead_row) if ahead_src is not None else None
                read, added, stored = (known(sp, i + (u0 + 2)), known(sp, i + (f0 + 1)),
                                       known(sp, i * 16 + 16 * u0))
                sp.wait_ge(x_out, stored)
                sp.dma_start(xres[:], tokens(src, row)).then_inc(xres_in, 16)
                if ahead_src is not None:
                    sp.wait_ge(xn_ready, read)
                    sp.dma_start(xln[:], tokens(ahead_src, row2)).then_inc(xln_in, 16)
                sp.wait_ge(res_done, added)
                sp.dma_start(tokens(dst, row), xres[:]).then_inc(x_out, 16)
            unit(0, src, 2 * UNIT)
            with sp.Fori(1, UNITS - 2) as i:
                unit(i, src, i * UNIT + 2 * UNIT)
            for i in range(2):
                if after:
                    unit(UNITS - 2 + i, dst, after[i])
                else:
                    unit(UNITS - 2 + i, None, None)

        M0 = UNITS

        def front_bank(b, n):
            return bank[(b * BANKS + n) % 2]

        def heads_bc(ap):
            return ap.unsqueeze(2).broadcast_to([P, HEADS, HP])

        def by_head(ap):
            return ap.rearrange("p (h c) -> p h c", h=HEADS)

        def pe_bank_free(pe, k_base, n, v_is_first):
            if v_is_first and n < 2:
                return
            pe.wait_ge(bank_read, k_base + n - 1)

        def pe_front(pe, kind, n, v, b):
            first = isinstance(v, int) and v == 0
            at = {"t": 0, "dt": KH, "c": KH + 1}[kind] + n
            dst = front_bank(b, at)
            pe_bank_free(pe, v * BANKS, at, first)
            if kind == "t":
                if n == 0:
                    pe.wait_ge(xn_ready, v + M0 + 1)
                for t in range(TILES):
                    ins = nc.tensor.transpose(dst[:, t * P:(t + 1) * P], xn[:, t, n * P:(n + 1) * P], identf[:])
            elif kind == "dt":
                pe.wait_ge(bank_read, v * BANKS + KH)
                for t in range(TILES):
                    for k in range(KH):
                        ins = nc.tensor.matmul(dst[:, t * HEADS:(t + 1) * HEADS], xnT[:, k, t * P:(t + 1) * P],
                                               wi[:, k, DT0:PROJ], start=(k == 0), stop=(k == KH - 1))
            else:
                col = D_SSM + n * P
                for k in range(KH):
                    ins = nc.tensor.matmul(dst[:], wi[:, k, col:col + P], xnT[:, k, :],
                                           start=(k == 0), stop=(k == KH - 1))
            ins.then_inc(bank_full, 1)

        def pe_z(pe, n, u, b):
            at = PROJS + n
            pe_bank_free(pe, u * BANKS, at, False)
            dst = front_bank(b, at)
            for k in range(KH):
                ins = nc.tensor.matmul(dst[:], wi[:, k, n * P:(n + 1) * P], xnT[:, k, :],
                                       start=(k == 0), stop=(k == KH - 1))
            ins.then_inc(bank_full, 1)

        def masks_of(s):
            if s < SEG0:
                return [(tok_mask[:, n, :], False) for n in (2 * s, 2 * s + 1) if n < DECAYS]
            return [(blk_mask[:, n, :], True) for n in (2 * (s - SEG0), 2 * (s - SEG0) + 1)]

        def pe_seg(pe, s, u, b):
            dst = (B0, B1)[s % 2]
            if not (isinstance(u, int) and u == 0 and s < 2):
                pe.wait_ge(seg_read, u * SEGS + s - 1)
            if s == 0:
                pe.wait_ge(a_ready, u + 1)
            for j, (mask, stacked) in enumerate(masks_of(s)):
                for part in range(2):
                    src = (as16[b][:, part].rearrange("p t c h -> p (t c h)") if stacked
                           else a16[b][:, part].rearrange("p t h -> p (t h)"))
                    ins = nc.tensor.matmul(dst[:, j * 256:(j + 1) * 256], mask, src,
                                           start=(part == 0), stop=(part == 1))
            ins.then_inc(seg_full, 1)

        def pe_item(pe, item, u, b):
            kind, n = item
            if kind == "seg":
                pe_seg(pe, n, u, b)
            elif kind == "z":
                pe_z(pe, n, u, b)
            else:
                pe_front(pe, kind, n, u + 1, 1 - b)

        def pe_tile_in(pe, t, u, b):
            T = u * TILES + t
            if t == 0:
                pe.wait_ge(silu_c, (u + 1) * CT)
            pe.wait_ge(t1_r, T)
            tok = slice(t * P, (t + 1) * P)
            for q in range(Q):
                ins = nc.tensor.transpose(XT[:, q * P:(q + 1) * P], xc[b][:, q, tok], identf[:])
            ins.then_inc(xT_r, 1)
            pe.wait_ge(t2_r, T)
            nc.tensor.transpose(BG[:, 0:P], xc[b][:, Q, tok], identf[:])
            nc.tensor.matmul(BG[:, P:2 * P], xc[b][:, Q, tok], xc[b][:, Q + 1, tok], start=True, stop=True)
            for c in range(NB):
                blk = slice(t * P + c * BLK, t * P + (c + 1) * BLK)
                for q in range(Q):
                    ins = nc.tensor.matmul(BG[q * BLK:(q + 1) * BLK, 2 * P + c * BLK:2 * P + (c + 1) * BLK],
                                           xc[b][:, Q, blk], xc[b][:, Q + 1, blk], start=True, stop=True,
                                           tile_position=(0, q * BLK))
            ins.then_inc(bg_r, 1)

        def pe_tile_state(pe, t, u, b):
            T = u * TILES + t
            pe.wait_ge(xdt_r, T + 1)
            pe.wait_ge(st_r, T)
            for c in range(NB):
                blk = slice(t * P + c * BLK, t * P + (c + 1) * BLK)
                ins = nc.tensor.matmul(YST[c * BLK:(c + 1) * BLK, :], xc[b][:, Q + 1, blk], S[b][:],
                                       start=True, stop=True, tile_position=(0, c * BLK))
            ins.then_inc(yst_r, 1)
            pe.wait_ge(gm_r, T + 1)
            pe.wait_ge(bt_r, T + 1)
            pe.wait_ge(xu_r, T + 1)
            for c in range(NB):
                ins = nc.tensor.matmul(YOFF[c * BLK:(c + 1) * BLK, :], Goff[:, c * BLK:(c + 1) * BLK],
                                       xu[:, max(c - 1, 0), :], start=True, stop=True,
                                       tile_position=(0, c * BLK))
            ins.then_inc(yoff_r, 1)
            pe.wait_ge(xw_r, T + 1)
            pe.wait_ge(fin_r, T if t == 0 else T - 1)
            nc.tensor.matmul(DS[:], Btok[:], xw[:], start=True, stop=True).then_inc(ds_r, 1)

        def pe_tile_diag(pe, t, u):
            T = u * TILES + t
            pe.wait_ge(yd_r, T)
            pe.wait_ge(m_r, T + 1)
            pe.wait_ge(xb_r, T + 1)
            for h in range(HQ):
                for c in range(NB):
                    dst = YIN[c * BLK:(c + 1) * BLK, :].rearrange("i (q h p) -> i q h p", q=Q, h=HQ)[:, :, h, :]
                    ins = nc.tensor.matmul(dst, M[t % 2][:, c * HQ + h, :], XB[t % 2][:, c, h, :],
                                           start=True, stop=True, tile_position=(0, c * BLK))
            ins.then_inc(yin_r, 1)

        def pe_tile_turn(pe, t, u):
            T = u * TILES + t
            pe.wait_ge(y_r, T + 1)
            for q in range(Q):
                ins = nc.tensor.transpose(YT[:, q * P:(q + 1) * P], y[:, q * P:(q + 1) * P], identf[:])
            ins.then_inc(yT_r, 1)

        def pe_tile_out(pe, t, u):
            T = u * TILES + t
            pe.wait_ge(st_r, T + 1 if t == TILES - 1 else T + 2)
            pe.wait_ge(g_r, T + 1)
            for q in range(Q):
                nc.tensor.matmul(OUT[:, 0:HID], g[:, q, :], wo[:, q, :], start=(q == 0), stop=(q == Q - 1))
            pe.wait_ge(g2s_r, T + 1)
            nc.tensor.matmul(OUT[:, HID:HID + 1], g2s[:], ones[:, 0:1], start=True, stop=True).then_inc(out_r, 1)

        def pe_slot(pe, u, b, first, has_next):
            if not first:
                pe_tile_turn(pe, TILES - 1, u - 1)
            pe_tile_in(pe, 0, u, b)
            for item in slot_head(has_next):
                kind, n = item
                if kind == "out":
                    if not first:
                        pe_tile_out(pe, TILES - 1, u - 1)
                elif kind == "state":
                    pe_tile_state(pe, 0, u, b)
                else:
                    pe_item(pe, item, u, b)
            for t in range(TILES):
                if t > 0:
                    pe_tile_state(pe, t, u, b)
                if t + 1 < TILES:
                    pe_tile_in(pe, t + 1, u, b)
                if t > 0:
                    pe_tile_turn(pe, t - 1, u)
                if has_next and 2 * t < CT:
                    pe_front(pe, "c", 2 * t, u + 1, 1 - b)
                pe_tile_diag(pe, t, u)
                if has_next and 2 * t < CT:
                    pe_front(pe, "c", 2 * t + 1, u + 1, 1 - b)
                if t > 0:
                    pe_tile_out(pe, t - 1, u)

        def act_front(act, kind, n, v, b):
            at = {"t": 0, "dt": KH, "c": KH + 1}[kind] + n
            src = front_bank(b, at)
            act.wait_ge(bank_full, v * BANKS + at + 1)
            if kind == "t":
                nc.scalar.activation(xnT[:, n, :], src[:], ACT.Copy).then_inc(bank_read, 1)
            elif kind == "dt":
                if not (isinstance(v, int) and v == 0):
                    act.wait_ge(dtc, v * DTC)
                nc.scalar.activation(dtr[:].rearrange("p t h -> p (t h)"), src[:, 0:TILES * HEADS],
                                     ACT.Copy).then_inc(bank_read, 1)
            else:
                rows_of = xp[:, n % XPS]
                if not (isinstance(v, int) and v == 0 and n < XPS):
                    act.wait_ge(tail_out, v * CT + n - XPS + 1)
                nc.scalar.activation(rows_of[:, 0:TAPS - 1], tails[b][:, n, :], ACT.Copy).then_inc(tail_in, 1)
                nc.scalar.activation(rows_of[:, TAPS - 1:], src[:], ACT.Copy).then_inc(bank_read, 1)
                act.wait_ge(tail_in, v * CT + n + 1)
                act.wait_ge(bank_read, v * BANKS + at + 1)
                nc.scalar.activation(xc[b][:, n, :], rows_of[:, 0:UNIT], ACT.Identity,
                                     scale=cw[:, n, 0:1], bias=cb[:, n:n + 1]).then_inc(tap0, 1)

        def act_z(act, n, u, b):
            act.wait_ge(bank_full, u * BANKS + PROJS + n + 1)
            if n == 0:
                act.wait_ge(g_r, u * TILES)
            nc.scalar.activation(zs[:, n, :], front_bank(b, PROJS + n)[:], ACT.Copy,
                                 scale=mupc[:, n:n + 1]).then_inc(bank_read, 1)

        def act_seg(act, s, u):
            act.wait_ge(seg_full, u * SEGS + s + 1)
            if s == 0:
                act.wait_ge(m_r, u * TILES)
                act.wait_ge(sd_r, u * TILES)
                act.wait_ge(xu_r, u * TILES)
                act.wait_ge(xw_r, u * TILES)
                act.wait_ge(t2_r, u * TILES)
            src = (B0, B1)[s % 2]
            n = len(masks_of(s))
            dst = dec[:, 2 * s:2 * s + n] if s < SEG0 else L[:, 2 * (s - SEG0):2 * (s - SEG0) + n]
            nc.scalar.activation(dst.rearrange("p n t h -> p (n t h)"), src[:, 0:n * 256], ACT.Exp,
                                 scale=-1.0 / AS).then_inc(seg_read, 1)

        def act_dt_exp(act, v):
            act.wait_ge(dt_abs, v + 1)
            nc.scalar.activation(dt_e[:], dt_e[:], ACT.Exp, scale=-1.0).then_inc(dt_exp, 1)

        def act_silu_conv(act, n, v, b):
            act.wait_ge(conv_step, v * CONV + (n + 1) * (TAPS - 1))
            nc.scalar.activation(xc[b][:, n, :], xc[b][:, n, :], ACT.Silu).then_inc(silu_c, 1)

        def act_silu_z(act, n, u):
            act.wait_ge(bank_read, u * BANKS + PROJS + n + 1)
            nc.scalar.activation(zs[:, n, :], zs[:, n, :], ACT.Silu).then_inc(silu_z, 1)

        def act_tile_in(act, t, u):
            T = u * TILES + t
            act.wait_ge(gm_r, T + 1)
            act.wait_ge(ds_r, T)
            nc.scalar.activation(Btok[:], BG[:, 0:P], ACT.Copy).then_inc(bt_r, 1)
            act.wait_ge(xdt_r, T + 1)
            act.wait_ge(yin_r, max(t - 1, 0) + u * TILES)
            for q in range(Q):
                for c in range(NB):
                    ins = nc.scalar.activation(
                        XB[t % 2][q * BLK:(q + 1) * BLK, c, :, q * HP:(q + 1) * HP],
                        xdt[t % 2][c * BLK:(c + 1) * BLK, q * P:(q + 1) * P].rearrange("p (h c) -> p h c", c=HP),
                        ACT.Copy)
            ins.then_inc(xb_r, 1)

        def act_tile_sq(act, t, u):
            T = u * TILES + t
            act.wait_ge(g_r, T + 1)
            act.wait_ge(g2s_r, T)
            nc.scalar.activation(g2[:], g[:], ACT.Square).then_inc(g2_r, 1)

        def act_slot(act, u, b, first, has_next):
            for item in slot_head(has_next):
                kind, n = item
                if kind == "seg":
                    act_seg(act, n, u)
                    if n == 14 and has_next:
                        act_dt_exp(act, u + 1)
                elif kind == "out":
                    if not first:
                        act_tile_sq(act, TILES - 1, u - 1)
                    act_tile_in(act, 0, u)
                elif kind == "z":
                    act_z(act, n, u, b)
                elif kind != "state":
                    act_front(act, kind, n, u + 1, 1 - b)
            for t in range(TILES):
                if t + 1 < TILES:
                    act_tile_in(act, t + 1, u)
                if has_next and 2 * t < CT:
                    act_front(act, "c", 2 * t, u + 1, 1 - b)
                if t == 0:
                    for n in range(Q):
                        act_silu_z(act, n, u)
                else:
                    act_tile_sq(act, t - 1, u)
                if has_next and 2 * t < CT:
                    act_front(act, "c", 2 * t + 1, u + 1, 1 - b)
                if has_next and t > 0:
                    act_silu_conv(act, 2 * t - 2, u + 1, 1 - b)
                    act_silu_conv(act, 2 * t - 1, u + 1, 1 - b)

        def dve_dt_head(dve, v):
            c = v * DTC
            dve.wait_ge(bank_read, v * BANKS + KH + 1)
            mb = mup_dt[:].unsqueeze(1).broadcast_to([P, TILES, HEADS])
            bb = bias_dt[:].unsqueeze(1).broadcast_to([P, TILES, HEADS])
            nc.vector.tensor_tensor(dt_q[:], dtr[:], mb, ALU.mult).then_inc(dtc, 1)
            dve.wait_ge(dtc, c + 1)
            nc.vector.tensor_tensor(dt_q[:], dt_q[:], bb, ALU.add).then_inc(dtc, 1)
            dve.wait_ge(dtc, c + 2)
            nc.vector.scalar_tensor_tensor(out=dt_e[:], in0=dt_q[:], scalar=-1.0, in1=dt_q[:],
                                           op0=ALU.mult, op1=ALU.max).then_inc(dt_abs, 1)

        def dve_dt_series(dve, v):
            n = v * DTC + 2

            def step(k):
                dve.wait_ge(dtc, n + k)

            dve.wait_ge(dt_exp, v + 1)
            nc.vector.tensor_scalar_add(dt_p[:], dt_e[:], 2.0).then_inc(dtc, 1)
            step(1)
            nc.vector.reciprocal(dt_s[:], dt_p[:]).then_inc(dtc, 1)
            step(2)
            nc.vector.tensor_tensor(dt_s[:], dt_e[:], dt_s[:], ALU.mult).then_inc(dtc, 1)
            step(3)
            nc.vector.tensor_tensor(dtr[:], dt_s[:], dt_s[:], ALU.mult).then_inc(dtc, 1)
            step(4)
            nc.vector.tensor_scalar(dt_p[:], dtr[:], 1.0 / (2 * SERIES - 1), None, ALU.mult).then_inc(dtc, 1)
            for k in range(SERIES - 2):
                step(5 + k)
                nc.vector.scalar_tensor_tensor(out=dt_p[:], in0=dt_p[:], scalar=1.0 / (2 * (SERIES - 2 - k) + 1),
                                               in1=dtr[:], op0=ALU.add, op1=ALU.mult).then_inc(dtc, 1)

        def dve_dt_tail(dve, v, b):
            n = v * DTC + 2

            def step(k):
                dve.wait_ge(dtc, n + k)

            k = 5 + SERIES - 2
            step(k)
            nc.vector.scalar_tensor_tensor(out=dt_p[:], in0=dt_p[:], scalar=1.0, in1=dt_s[:],
                                           op0=ALU.add, op1=ALU.mult).then_inc(dtc, 1)
            step(k + 1)
            nc.vector.tensor_scalar(dt_p[:], dt_p[:], 2.0, None, ALU.mult).then_inc(dtc, 1)
            step(k + 2)
            nc.vector.scalar_tensor_tensor(out=dts[b][:], in0=dt_q[:], scalar=0.0, in1=dt_p[:],
                                           op0=ALU.max, op1=ALU.add).then_inc(dtc, 1)
            step(k + 3)
            ea = expA[:].unsqueeze(1).broadcast_to([P, TILES, HEADS])
            nc.vector.tensor_tensor(dt_p[:], dts[b][:], ea, ALU.mult).then_inc(dtc, 1)
            step(k + 4)
            nc.vector.tensor_scalar(dt_p[:], dt_p[:], A_MAX, AS, ALU.min, ALU.mult).then_inc(dtc, 1)
            step(k + 5)
            nc.vector.tensor_copy(a16[b][:, 0], dt_p[:]).then_inc(dtc, 1)
            step(k + 6)
            nc.vector.tensor_tensor(a16[b][:, 1], dt_p[:], a16[b][:, 0], ALU.subtract).then_inc(dtc, 1)
            assert 2 + k + 7 == DTC
            step(k + 7)
            for q in range(Q):
                for c in range(NB):
                    ins = nc.vector.tensor_copy(as16[b][q * BLK:(q + 1) * BLK, :, :, c, :],
                                                a16[b][c * BLK:(c + 1) * BLK, :, :, q * HQ:(q + 1) * HQ])
            ins.then_inc(a_ready, 1)

        def dve_conv(dve, n, v, b):
            dve.wait_ge(tap0, v * CT + n + 1)
            for k in range(1, TAPS):
                if k > 1:
                    dve.wait_ge(conv_step, v * CONV + n * (TAPS - 1) + k - 1)
                nc.vector.scalar_tensor_tensor(out=xc[b][:, n, :], in0=xp[:, n % XPS, k:k + UNIT], scalar=cw[:, n, k:k + 1],
                                               in1=xc[b][:, n, :], op0=ALU.mult, op1=ALU.add).then_inc(conv_step, 1)

            nc.vector.tensor_copy(tails[b][:, n, :], xp[:, n % XPS, UNIT:]).then_inc(tail_out, 1)

        def dve_tile_in(dve, t, u, b):
            T = u * TILES + t
            lag = max(t - 1, 0) + u * TILES
            dve.wait_ge(xT_r, T + 1)
            dve.wait_ge(xb_r, lag)
            dve.wait_ge(xu_r, lag)
            dve.wait_ge(xw_r, lag)
            nc.vector.tensor_tensor(by_head(xdt[t % 2][:]), by_head(XT[:]), heads_bc(dts[b][:, t, :]),
                                    ALU.mult).then_inc(xdt_r, 1)
            dve.wait_ge(bg_r, T + 1)
            dve.wait_ge(yoff_r, T)
            dve.wait_ge(m_r, T)
            nc.vector.tensor_tensor(Gd[:], BG[:, 2 * P:3 * P].rearrange("p (c i) -> p c i", c=NB),
                                    causal[:].unsqueeze(1).broadcast_to([P, NB, BLK]), ALU.mult)
            nc.vector.tensor_tensor(Goff[:], BG[:, P:2 * P], off_mask[:], ALU.mult).then_inc(gm_r, 1)

        def dve_tile_m(dve, t, u):
            T = u * TILES + t
            if t == 0:
                dve.wait_ge(seg_read, (u + 1) * SEGS)
            dve.wait_ge(gm_r, T + 1)
            dve.wait_ge(yin_r, max(t - 1, 0) + u * TILES)
            nc.vector.tensor_tensor(M[t % 2][:].rearrange("p (c h) i -> p c h i", c=NB),
                                    L[:, :, t, :].rearrange("p i (c h) -> p c h i", c=NB),
                                    Gd[:].unsqueeze(2).broadcast_to([P, NB, HQ, BLK]), ALU.mult).then_inc(m_r, 1)

        def dve_tile_state(dve, t, u, b):
            T = u * TILES + t
            dve.wait_ge(yst_r, T + 1)
            dve.wait_ge(y_r, T)
            nc.vector.tensor_tensor(by_head(t1[:]), by_head(YST[:]), heads_bc(dec[:, V_TILE, t, :]),
                                    ALU.mult).then_inc(t1_r, 1)
            dve.wait_ge(yoff_r, T + 1)
            dve.wait_ge(t12_r, T)
            nc.vector.tensor_tensor(by_head(t2[:]), by_head(YOFF[:]), heads_bc(dec[:, V_BLK, t, :]),
                                    ALU.mult).then_inc(t2_r, 1)
            dve.wait_ge(ds_r, T + 1)
            dve.wait_ge(sd_r, T + 1)
            nc.vector.tensor_tensor(S[b][:], SD[:], DS[:], ALU.add).then_inc(st_r, 1)

        def dve_tile_gate(dve, t, u, b):
            T = u * TILES + t
            tok = slice(t * P, (t + 1) * P)
            dve.wait_ge(yT_r, T + 1)
            dve.wait_ge(g_r, T)
            for q in range(Q):
                ins = nc.vector.scalar_tensor_tensor(out=yd[:, q, :], in0=xc[b][:, q, tok], scalar=dcol[:, q:q + 1],
                                                     in1=YT[:, q * P:(q + 1) * P], op0=ALU.mult, op1=ALU.add)
            ins.then_inc(yd_r, 1)
            if t == 0:
                dve.wait_ge(silu_z, (u + 1) * Q)
            dve.wait_ge(yd_r, T + 1)
            dve.wait_ge(out_r, T)
            dve.wait_ge(g2_r, T)
            nc.vector.tensor_tensor(g[:], yd[:], zs[:, :, tok], ALU.mult).then_inc(g_r, 1)

        def dve_tile_y(dve, t, u):
            T = u * TILES + t
            dve.wait_ge(yin_r, T + 1)
            dve.wait_ge(t12_r, T + 1)
            dve.wait_ge(yT_r, T)
            nc.vector.tensor_tensor(y[:], t1[:], YIN[:], ALU.add).then_inc(y_r, 1)

        def dve_tile_ms(dve, t, u):
            T = u * TILES + t
            dve.wait_ge(out_r, T + 1)
            nc.vector.tensor_scalar(ms[t % 2][:], OUT[:, HID:HID + 1], 1.0 / D_SSM, RMS_EPS,
                                    ALU.mult, ALU.add).then_inc(ms_r, 1)

        def dve_tile_fin(dve, t, u):
            T = u * TILES + t
            if t == 0:
                dve.wait_ge(xres_in, (u + M0 + 1) * 16)
            dve.wait_ge(rs_r, T + 1)
            nc.vector.scalar_tensor_tensor(out=xres[:, t, :], in0=OUT[:, 0:HID], scalar=rs[t % 2][:],
                                           in1=xres[:, t, :], op0=ALU.mult, op1=ALU.add).then_inc(fin_r, 1)

        def dve_slot(dve, u, b, first, has_next):
            v, bv = u + 1, 1 - b
            if not first:
                dve_tile_gate(dve, TILES - 1, u - 1, bv)
            dve_tile_in(dve, 0, u, b)
            if not first:
                dve_tile_ms(dve, TILES - 1, u - 1)
            ln_stats(dve, v + M0)
            if not first:
                dve_tile_fin(dve, TILES - 1, u - 1)
            ln_apply(dve, v + M0)
            dve_tile_state(dve, 0, u, b)
            if has_next:
                dve_dt_head(dve, v)
            dve_tile_m(dve, 0, u)
            for t in range(TILES):
                if t > 0:
                    dve_tile_state(dve, t, u, b)
                if t + 1 < TILES:
                    dve_tile_in(dve, t + 1, u, b)
                if t > 0:
                    dve_tile_gate(dve, t - 1, u, b)
                if has_next and 0 < 2 * t - 1 < CT:
                    dve_conv(dve, 2 * t - 1, v, bv)
                if t + 1 < TILES:
                    dve_tile_m(dve, t + 1, u)
                dve_tile_y(dve, t, u)
                if has_next and 2 * t < CT:
                    dve_conv(dve, 2 * t, v, bv)
                if t > 0:
                    dve_tile_ms(dve, t - 1, u)
                    dve_tile_fin(dve, t - 1, u)
                if has_next and t == 0:
                    dve_dt_series(dve, v)
            if has_next:
                dve_dt_tail(dve, v, bv)

        def pool_tile_x(pool, t, u):
            T = u * TILES + t
            src = by_head(xdt[t % 2][:])
            pool.wait_ge(xdt_r, T + 1)
            if t == 0:
                pool.wait_ge(seg_read, u * SEGS + SEG0)
            pool.wait_ge(yoff_r, T)
            for i in range(NB - 1):
                ins = nc.gpsimd.tensor_tensor(by_head(xu[:, i, :]), src, heads_bc(dec[:, U_1 + i, t, :]), ALU.mult)
            ins.then_inc(xu_r, 1)
            pool.wait_ge(ds_r, T)
            nc.gpsimd.tensor_tensor(by_head(xw[:]), src, heads_bc(dec[:, W_END, t, :]), ALU.mult).then_inc(xw_r, 1)

        def pool_tile_state(pool, t, u, b):
            T = u * TILES + t
            pool.wait_ge(st_r, T)
            nc.gpsimd.tensor_tensor(by_head(SD[:]), by_head(S[b][:]), heads_bc(dec[:, TOTAL, t, :]),
                                    ALU.mult).then_inc(sd_r, 1)
            pool.wait_ge(t1_r, T + 1)
            pool.wait_ge(t2_r, T + 1)
            nc.gpsimd.tensor_tensor(t1[:], t1[:], t2[:], ALU.add).then_inc(t12_r, 1)

        def pool_tile_sq(pool, t, u):
            T = u * TILES + t
            pool.wait_ge(g2_r, T + 1)
            nc.gpsimd.tensor_tensor(g2h[:], g2[:, 0:2, :], g2[:, 2:4, :], ALU.add).then_inc(g2h_r, 1)
            pool.wait_ge(g2h_r, T + 1)
            pool.wait_ge(out_r, T)
            nc.gpsimd.tensor_tensor(g2s[:], g2h[:, 0, :], g2h[:, 1, :], ALU.add).then_inc(g2s_r, 1)

        def pool_tile_rs(pool, t, u):
            T = u * TILES + t
            pool.wait_ge(ms_r, T + 1)
            pool.wait_ge(fin_r, max(t - 1, 0) + u * TILES)
            nc.gpsimd.tensor_tensor(rs[t % 2][:], ms[t % 2][:], mhalf[:, 0:1], ALU.pow).then_inc(rs_r, 1)

        def pool_slot(pool, u, b, first, has_next):
            if not first:
                pool_tile_sq(pool, TILES - 1, u - 1)
            pool_tile_x(pool, 0, u)
            if not first:
                pool_tile_rs(pool, TILES - 1, u - 1)
            ln_power(pool, u + (M0 + 1))
            for t in range(TILES):
                pool_tile_state(pool, t, u, b)
                if t + 1 < TILES:
                    pool_tile_x(pool, t + 1, u)
                if t > 0:
                    pool_tile_sq(pool, t - 1, u)
                    pool_tile_rs(pool, t - 1, u)

        def slots(eng, body):
            body(eng, 0, 0, True, True)
            with eng.Fori(0, UNITS // 2 - 1) as i:
                body(eng, i * 2 + 1, 1, False, True)
                body(eng, i * 2 + 2, 0, False, True)
            body(eng, UNITS - 1, 1, False, False)

        def row_of(i, b):
            return i * UNIT + b * LEN

        def sp_mamba(sp):
            def unit(i, b, ahead_src, ahead_row):
                u = i * 2 + b
                row, row2 = known(sp, row_of(i, b)), known(sp, ahead_row)
                read, summed, stored = (known(sp, u + (M0 + 2)), known(sp, u * TILES + TILES),
                                        known(sp, u * 16 + 16 * M0))
                sp.wait_ge(x_out, stored)
                sp.dma_start(xres[:], tokens(mid1, row)).then_inc(xres_in, 16)
                sp.wait_ge(xn_ready, read)
                sp.dma_start(xln[:], tokens(ahead_src, row2)).then_inc(xln_in, 16)
                sp.wait_ge(fin_r, summed)
                sp.dma_start(tokens(mid2, row), xres[:]).then_inc(x_out, 16)
            for b in range(2):
                unit(0, b, mid1, row_of(1, b))
            with sp.Fori(1, UNITS // 2 - 1) as i:
                for b in range(2):
                    unit(i, b, mid1, row_of(i, b) + UNIT)
            for b in range(2):
                unit(UNITS // 2 - 1, b, mid2, b * UNIT)

        def last_uses(eng, tiles):
            eng.wait_ge(bank_read, UNITS * BANKS)
            eng.wait_ge(seg_read, UNITS * SEGS)
            for s in (m_r, t1_r, t2_r, yd_r, fin_r):
                eng.wait_ge(s, tiles)

        NPARAM = 9 + Q
        FFN_CONST, MASKS = 3, 23
        LAST_U, LAST_T, LAST_B = UNITS - 1, TILES - 1, (UNITS - 1) % 2

        @block.sync
        def _(sp):
            sp.dma_start(xln[:], tokens(x_flat, 0)).then_inc(xln_in, 16)
            sp.wait_ge(zero, 1)
            for i, w in enumerate((w1, w2)):
                full = (CH - 1) * P
                v = wst[i].rearrange("p (r k) -> p r k", k=HID)
                sp.dma_start(v[:, 0:CH - 1, :], w[0:full, :].rearrange("(r p) k -> p r k", p=P)).then_inc(wl[i], 16)
                sp.dma_start(v[0:LAST, CH - 1, :], w[full:FF, :]).then_inc(wl[i], 16)
            sp.dma_start(wst[2].rearrange("p (o f) -> p o f", f=FF),
                         w3.rearrange("(o p) f -> p o f", p=P)).then_inc(wl[2], 16)
            sp.wait_ge(xn_ready, 1)
            sp.dma_start(xln[:], tokens(x_flat, UNIT)).then_inc(xln_in, 16)

            def cols(ap):
                return ap.rearrange("(c p) -> p c", p=P)
            sp.dma_start(wi[:], W_in.rearrange("(k p) n -> p k n", p=P)).then_inc(pl, 16)
            sp.dma_start(wo[:], W_out.rearrange("(q p) n -> p q n", p=P)).then_inc(pl, 16)
            sp.dma_start(nw[:], cols(norm_w)).then_inc(pl, 16)
            sp.dma_start(cw[:], conv_w.rearrange("(c p) k -> p c k", p=P)).then_inc(pl, 16)
            sp.dma_start(cb[:], cols(conv_b)).then_inc(pl, 16)
            sp.dma_start(mupc[:], cols(mup[0:DT0])).then_inc(pl, 16)
            for q in range(Q):
                sp.dma_start(dcol[:, q:q + 1],
                             D_w[q * HQ:(q + 1) * HQ].unsqueeze(1).broadcast_to([HQ, HP])).then_inc(pl, 16)
            sp.dma_start(mup_dt[:], mup[DT0:PROJ].unsqueeze(0).broadcast_to([P, HEADS])).then_inc(pl, 16)
            sp.dma_start(bias_dt[:], dt_bias.unsqueeze(0).broadcast_to([P, HEADS])).then_inc(pl, 16)
            sp.dma_start(expA[:], A_log.unsqueeze(0).broadcast_to([P, HEADS])).then_inc(pl, 16)

            sp_ffn(sp, x_flat, mid1, 0, 0, (row_of(0, 0), row_of(0, 1)))
            sp_mamba(sp)
            sp_ffn(sp, mid2, out_flat, UNITS, 2 * UNITS, None)
            sp.wait_ge(x_out, 16 * UNITS * 3)

        @block.gpsimd
        def _(pool):
            fp = nc.gpsimd
            made = [0]

            def step(ins):
                ins.then_inc(cst, 1)
                made[0] += 1

            def select(ap, op, fill, base, pattern, mult):
                pool.wait_ge(cst, made[0])
                step(fp.affine_select(out=ap, in_=ap, compare_op=op, fill=fill, base=base, pattern=pattern,
                                      channel_multiplier=mult))

            fp.memset(wst[0][:, (CH - 1) * HID:], 0.0)
            fp.memset(wst[1][:, (CH - 1) * HID:], 0.0).then_inc(zero, 1)
            fp.memset(ones[:], 1.0)
            fp.memset(mhalf[:], -0.5)
            fp.memset(identf[:], 0.0)
            step(fp.memset(ident16[:], 0.0))
            select(identf[:], ALU.not_equal, 1.0, 0, [[-1, P]], 1)
            select(ident16[:], ALU.not_equal, 1.0, 0, [[-1, P]], 1)
            assert made[0] == FFN_CONST
            ln_power(pool, 0)

            fp.memset(tok_mask[:], 1.0)
            fp.memset(causal[:], 1.0)
            step(fp.memset(off_mask[:], 1.0))
            select(tok_mask[:, V_BLK], ALU.is_ge, 0.0, 0, [[1, P]], -1)
            select(tok_mask[:, V_TILE], ALU.is_ge, 0.0, 0, [[1, P]], -1)
            for i in range(NB - 1):
                select(tok_mask[:, U_1 + i], ALU.is_gt, 0.0, 0, [[-1, P]], 1)
            select(tok_mask[:, W_END], ALU.is_gt, 0.0, 0, [[-1, P]], 1)
            select(off_mask[:].rearrange("p (c i) -> p c i", c=NB), ALU.is_gt, 0.0, 0, [[BLK, NB], [0, BLK]], -1)
            for q in range(NB):
                select(causal[q * BLK:(q + 1) * BLK, :], ALU.is_ge, 0.0, 0, [[1, BLK]], -1)
            select(tok_mask[:, V_BLK].rearrange("p (c i) -> p c i", c=NB), ALU.is_ge, 0.0, 0,
                   [[-BLK, NB], [0, BLK]], 1)
            for i in range(NB - 1):
                select(tok_mask[:, U_1 + i], ALU.is_ge, 0.0, BLK * (i + 1) - 1, [[0, P]], -1)

            pool_ffn(pool, 0, 0, True)

            for b in range(2):
                fp.memset(S[b][:], 0.0)
                ins = fp.memset(tails[b][:], 0.0)
            ins.then_inc(zero, 1)
            step(fp.memset(blk_mask[:], 1.0))
            bm = blk_mask[:].rearrange("p i (q j) -> p i q j", q=Q)
            select(bm, ALU.is_gt, 0.0, 0, [[0, BLK], [-BLK, Q], [-1, BLK]], 1)
            select(bm, ALU.is_ge, 0.0, 0, [[1, BLK], [BLK, Q], [0, BLK]], -1)
            fp.memset(XB[0][:], 0.0)
            step(fp.memset(XB[1][:], 0.0))
            assert made[0] == MASKS

            slots(pool, pool_slot)
            pool_tile_sq(pool, LAST_T, LAST_U)
            pool_tile_rs(pool, LAST_T, LAST_U)
            pool_ffn(pool, UNITS, 2 * UNITS, False)

        @block.tensor
        def _(pe):
            pe.wait_ge(cst, FFN_CONST)
            pe.wait_ge(absd, 3)
            nc.tensor.matmul(xTb[0][:, 0:3], ones[:], wsum[:], start=True, stop=True).then_inc(sumd, 1)
            pe.wait_ge(qstep, 1)
            pe_turn(pe, 0, 0)
            for i in range(6):
                w, k = i // 2, i % 2
                dst = bank[i][:].bitcast(F16)
                pe.wait_ge(qstep, 5 + 2 * w)
                if w < 2:
                    v = wq16[w].rearrange("p (r k) -> p r k", k=HID)
                    for r in range(CH):
                        n = P if r < CH - 1 else LAST
                        ins = nc.tensor.transpose(dst[:, r * P:r * P + n], v[0:n, r, k * P:(k + 1) * P],
                                                  ident16[0:n, 0:n])
                else:
                    v = wq16[2][:, 0:KH * FF].rearrange("p (o f) -> p o f", f=FF)
                    for r in range(CH):
                        n = P if r < CH - 1 else LAST
                        ins = nc.tensor.transpose(dst[0:n, r * P:(r + 1) * P], v[:, k, r * P:r * P + n], ident16[:])
                ins.then_inc(wT, 1)
            pe.wait_ge(wTe, 6)
            pe_ffn(pe, 0, 0, True)

            pe.wait_ge(pl, 16 * NPARAM)
            pe.wait_ge(hid_ready, UNITS * CH)
            for n in range(KH):
                pe_front(pe, "t", n, 0, 0)
            pe_front(pe, "dt", 0, 0, 0)
            for n in range(CT):
                pe_front(pe, "c", n, 0, 0)
            pe.wait_ge(xlo_ready, UNITS)
            pe.wait_ge(res_done, UNITS)
            pe.wait_ge(zero, 2)
            pe.wait_ge(setup, 2)
            pe.wait_ge(cst, MASKS)
            slots(pe, pe_slot)
            pe_tile_turn(pe, LAST_T, LAST_U)
            pe_tile_out(pe, LAST_T, LAST_U)

            last_uses(pe, UNITS * TILES)
            pe_turn(pe, 2 * UNITS, UNITS)
            pe_ffn(pe, UNITS, 2 * UNITS, False)

        @block.scalar
        def _(act):
            for i in range(3):
                act.wait_ge(wl[i], 32 if i < 2 else 16)
                if i > 0:
                    act.wait_ge(absd, i)
                n = CH * HID if i < 2 else KH * FF
                nc.scalar.activation(wabs[:, 0:n], wst[i][:, 0:n], ACT.Abs, accum_out=wsum[:, i:i + 1]).then_inc(absd, 1)
            act.wait_ge(absd, 3)
            act_split_x(act, 0, 0, 0)
            for i in range(6):
                w, k = i // 2, i % 2
                src = bank[i][:].bitcast(F16)
                act.wait_ge(wT, i + 1)
                if w < 2:
                    scale = (1.0, W2S)[w]
                    main = w12T[:, k, 0:2 * (CH - 1) * P].rearrange("p (m s n) -> p m s n", s=2, n=P)[:, :, w, :]
                    col = 2 * (CH - 1) * P + (LAST if w == 0 else 0)
                    nc.scalar.activation(main, src[:, 0:(CH - 1) * P].rearrange("p (m n) -> p m n", n=P),
                                         ACT.Copy, scale=scale)
                    nc.scalar.activation(w12T[:, k, col:col + LAST], src[:, (CH - 1) * P:(CH - 1) * P + LAST],
                                         ACT.Copy, scale=scale).then_inc(wTe, 1)
                else:
                    nc.scalar.activation(w3T[:, 0:CH - 1, k * P:(k + 1) * P],
                                         src[:, 0:(CH - 1) * P].rearrange("p (m n) -> p m n", n=P),
                                         ACT.Copy, scale=W3S)
                    nc.scalar.activation(w3T[0:LAST, CH - 1, k * P:(k + 1) * P],
                                         src[0:LAST, (CH - 1) * P:CH * P], ACT.Copy, scale=W3S).then_inc(wTe, 1)
            act_ffn(act, 0, 0, True)

            act.wait_ge(setup, 1)
            act.wait_ge(zero, 2)
            for n in range(KH):
                act_front(act, "t", n, 0, 0)
            act_front(act, "dt", 0, 0, 0)
            act_front(act, "c", 0, 0, 0)
            nc.scalar.activation(expA[:], expA[:], ACT.Exp).then_inc(expA_r, 1)
            act_dt_exp(act, 0)
            for n in range(1, CT):
                act_front(act, "c", n, 0, 0)
            for n in range(CT):
                act_silu_conv(act, n, 0, 0)
            act.wait_ge(down_done, UNITS * CH)
            act.wait_ge(hlo_ready, UNITS * CH)
            slots(act, act_slot)
            act_tile_sq(act, LAST_T, LAST_U)

            last_uses(act, UNITS * TILES)
            act_split_x(act, UNITS, 2 * UNITS, 0)
            act_ffn(act, UNITS, 2 * UNITS, False)

        @block.vector
        def _(dve):
            ln_stats(dve, 0)
            ln_apply(dve, 0, 0)
            dve.wait_ge(sumd, 1)
            nc.vector.tensor_scalar(thr[:, 0, :], xTb[0][:, 0:3], 1.0 / (FF * HID), Q_EPS, ALU.mult, ALU.add).then_inc(qstep, 1)
            dve.wait_ge(qstep, 1)
            nc.vector.tensor_scalar(thr[:, 1, :], thr[:, 0, :], -0.5, None, ALU.mult).then_inc(qstep, 1)
            dve.wait_ge(qstep, 2)
            nc.vector.tensor_scalar(thr[:, 0, :], thr[:, 0, :], 0.5, None, ALU.mult).then_inc(qstep, 1)
            dve.wait_ge(qstep, 3)
            for i in range(3):
                n = CH * HID if i < 2 else KH * FF
                nc.vector.tensor_scalar(wneg[:, 0:n], wst[i][:, 0:n], thr[:, 1, i:i + 1], None, ALU.is_lt).then_inc(qstep, 1)
                dve.wait_ge(qstep, 4 + 2 * i)
                nc.vector.scalar_tensor_tensor(out=wq16[i][:, 0:n], in0=wst[i][:, 0:n], scalar=thr[:, 0, i:i + 1],
                                               in1=wneg[:, 0:n], op0=ALU.is_gt, op1=ALU.subtract).then_inc(qstep, 1)
                dve.wait_ge(qstep, 5 + 2 * i)
            dve_split_x(dve, 0, 0)
            dve_ffn(dve, 0, 0, True)

            dve.wait_ge(pl, 16 * NPARAM)
            for n in range(CT):
                ins = nc.vector.tensor_scalar(cw[:, n, :], cw[:, n, :], mupc[:, Q + n:Q + n + 1], None, ALU.mult)
            ins.then_inc(setup, 1)
            dve.wait_ge(setup, 1)
            dve_dt_head(dve, 0)
            for n in range(XPS):
                dve_conv(dve, n, 0, 0)
            dve_dt_series(dve, 0)
            dve.wait_ge(expA_r, 1)
            dve_dt_tail(dve, 0, 0)
            for n in range(XPS, CT):
                dve_conv(dve, n, 0, 0)
            for q in range(Q):
                ins = nc.vector.tensor_scalar(wo[:, q, :], wo[:, q, :], nw[:, q:q + 1], None, ALU.mult)
            ins.then_inc(setup, 1)
            slots(dve, dve_slot)
            dve_tile_gate(dve, LAST_T, LAST_U, LAST_B)
            dve_tile_ms(dve, LAST_T, LAST_U)
            dve_tile_fin(dve, LAST_T, LAST_U)

            last_uses(dve, UNITS * TILES)
            dve_split_x(dve, UNITS, 0)
            dve_ffn(dve, UNITS, 2 * UNITS, False)


_INS = ['L0_attn_hidden_states', 'L0_attn_W_in', 'L0_attn_conv_w', 'L0_attn_conv_b', 'L0_attn_A_log', 'L0_attn_D',
        'L0_attn_dt_bias', 'L0_attn_norm_w', 'L0_attn_W_out', 'L0_attn_mup_vector', 'L0_ffn_w1', 'L0_ffn_w2',
        'L0_ffn_w3']


def kernel(**inputs):
    import numpy as _np
    import concourse.bacc as _bacc
    from concourse import mybir as _mybir
    from concourse.bass_utils import run_bass_kernel_spmd as _run

    nc = _bacc.Bacc("TRN2", target_bir_lowering=False, num_devices=1)
    arrays, args = {}, []
    for name in _INS:
        a = _np.ascontiguousarray(inputs[name])
        arrays[f"in_{name}_dram"] = a
        args.append(nc.dram_tensor(f"in_{name}_dram", a.shape, _mybir.dt.from_np(a.dtype), kind="ExternalInput").ap())
    out = nc.dram_tensor("out_0_dram", (BATCH, LEN, HID), _mybir.dt.float32, kind="ExternalOutput").ap()
    macaron_program(nc, *args, out)
    r = _run(nc, [arrays], core_ids=[0])
    return r.results[0]["out_0_dram"]
```

```python
from contextlib import ExitStack

import concourse.bass as bass
from concourse import mybir

F32 = mybir.dt.float32
F16 = mybir.dt.float16
ALU = mybir.AluOpType
ACT = mybir.ActivationFunctionType

P = 128
TILES = 4
UNIT = P * TILES
BATCH, LEN, HID = 2, 2048, 256
UNITS = BATCH * LEN // UNIT
KH = HID // P
FF = 704
CH = (FF + P - 1) // P
LAST = FF - (CH - 1) * P
D_SSM, STATE, HEADS, TAPS = 512, 128, 64, 4
HP = D_SSM // HEADS
Q = D_SSM // P
HQ = HEADS // Q
CT = Q + 2
BLK = 32
NB = P // BLK
PROJ = 2 * D_SSM + 2 * STATE + HEADS
DT0 = 2 * D_SSM + 2 * STATE
LN_EPS, RMS_EPS, Q_EPS = 1e-5, 1e-5, 1e-8
XS = 2.0 ** 11
W2S = 2.0 ** -4
W3S = 0.5 / (XS * W2S)
A_MAX = 120.0
AS = 2.0 ** 9
XPS = 3
SERIES = 8

V_BLK, V_TILE, U_1, U_2, U_3, W_END, TOTAL = range(7)
DECAYS = 7
SEG0 = 4
SEGS = SEG0 + BLK // 2
EARLY = 4
PROJS = KH + 1 + CT
BANKS = PROJS + Q

LN_STEPS = 3
CONV = CT * (TAPS - 1)
DTC = 12 + SERIES


def slot_head(has_next):
    seg = iter([("seg", s) for s in range(EARLY, SEGS)])
    items = [next(seg), ("turn", 0), next(seg)]
    if has_next:
        items += [("t", 0), next(seg), ("t", 1), next(seg), next(seg), ("square", 0), ("dt", 0), next(seg), next(seg),
                  ("exp", 0)]
    else:
        items += [("square", 0)]
    return items + [("out", 0), next(seg), ("state", 0)] + list(seg) + [("x", 0)]


def macaron_program(nc, x_in, W_in, conv_w, conv_b, A_log, D_w, dt_bias, norm_w, W_out, mup,
                    w1, w2, w3, out):
    ctx = ExitStack()
    with ctx:
        def sb(name, shape, dt=F32):
            return ctx.enter_context(nc.sbuf_tensor(name, shape, dt))

        def sem(name):
            return ctx.enter_context(nc.semaphore(name))

        mid1 = nc.dram_tensor("x_after_ffn1", (BATCH * LEN, HID), F32, kind="Internal").ap()
        mid2 = nc.dram_tensor("x_after_mamba", (BATCH * LEN, HID), F32, kind="Internal").ap()
        x_flat = x_in.rearrange("b l d -> (b l) d")
        out_flat = out.rearrange("b l d -> (b l) d")

        identf = sb("identf", [P, P])
        ident16 = sb("ident16", [P, P], F16)
        ones = sb("ones", [P, P])
        mhalf = sb("mhalf", [P, TILES])
        tok_mask = sb("tok_mask", [P, 8, P], F16)
        blk_mask = sb("blk_mask", [P, BLK, P], F16)
        causal = sb("causal", [P, BLK])
        off_mask = sb("off_mask", [P, P])
        wi = sb("wi", [P, KH, PROJ])
        wo = sb("wo", [P, Q, HID])
        w12T = sb("w12T", [P, KH, 2 * FF], F16)
        w3T = sb("w3T", [P, CH, HID], F16)
        nw = sb("nw", [P, Q])
        cw = sb("cw", [P, CT, TAPS])
        cb = sb("cb", [P, CT])
        mupc = sb("mupc", [P, DT0 // P])
        dcol = sb("dcol", [P, Q])
        mup_dt = sb("mup_dt", [P, HEADS])
        bias_dt = sb("bias_dt", [P, HEADS])
        expA = sb("expA", [P, HEADS])
        xln = sb("xln", [P, TILES, HID])
        xres = sb("xres", [P, TILES, HID])
        xn = sb("xn", [P, TILES, HID])
        stats = sb("stats", [P, TILES, 6])
        mv = sb("mv", [P, TILES, 2])
        veps = sb("veps", [P, TILES])
        rstd = sb("rstd", [P, TILES])

        shared = sb("shared", [P, BLK * TILES * HEADS])
        L = shared[:].rearrange("p (i t h) -> p i t h", i=BLK, t=TILES)
        s16 = shared[:].bitcast(F16)
        xs_n, h_n = KH * UNIT, CH * UNIT
        xsplit = [[s16[:, (2 * b + j) * xs_n:(2 * b + j + 1) * xs_n].rearrange("p (k n) -> p k n", k=KH)
                   for j in range(2)] for b in range(2)]
        hsplit = [s16[:, 4 * xs_n + j * h_n:4 * xs_n + (j + 1) * h_n].rearrange("p (m n) -> p m n", m=CH)
                  for j in range(2)]
        used = (4 * xs_n + 2 * h_n) // 2
        sig = [shared[:, used + j * UNIT:used + (j + 1) * UNIT] for j in range(2)]
        hid = [shared[:, used + (2 + j) * UNIT:used + (3 + j) * UNIT] for j in range(2)]

        dec = sb("dec", [P, 8, TILES, HEADS])
        M = [sb(f"M{i}", [P, HEADS, BLK]) for i in range(2)]
        XB = [sb(f"XB{i}", [P, NB, HQ, Q * HP]) for i in range(2)]
        xp = sb("xp", [P, XPS, UNIT + TAPS - 1])
        tails = [sb(f"tail{b}", [P, CT, TAPS - 1]) for b in range(2)]
        xc = [sb(f"xc{b}", [P, CT, UNIT]) for b in range(2)]
        zs = [sb(f"zs{b}", [P, Q, UNIT]) for b in range(2)]
        xnT = sb("xnT", [P, KH, UNIT])
        dtr = sb("dtr", [P, TILES, HEADS])
        dt_q = sb("dt_q", [P, TILES, HEADS])
        dt_e = sb("dt_e", [P, TILES, HEADS])
        dt_s = dec[:, DECAYS]
        dts = [sb(f"dts{b}", [P, TILES, HEADS]) for b in range(2)]
        a16 = [sb(f"a16_{b}", [P, 2, TILES, HEADS], F16) for b in range(2)]
        as16 = [sb(f"as16_{b}", [P, 2, TILES, NB, HQ], F16) for b in range(2)]
        S = [sb(f"S{b}", [P, D_SSM]) for b in range(2)]
        xdt = [sb(f"xdt{i}", [P, D_SSM]) for i in range(2)]
        xw = sb("xw", [P, D_SSM])
        xu = sb("xu", [P, NB - 1, D_SSM])
        Btok = sb("Btok", [P, STATE])
        Goff = sb("Goff", [P, P])
        Gd = sb("Gd", [P, NB, BLK])
        t1 = sb("t1", [P, D_SSM])
        t2 = sb("t2", [P, D_SSM])
        y = sb("y", [P, D_SSM])
        yd = y[:].rearrange("p (q n) -> p q n", q=Q)
        g = sb("g", [P, Q, P])
        g2 = sb("g2", [P, Q, P])
        ms = [sb(f"ms{i}", [P, 1]) for i in range(2)]
        rs = [sb(f"rs{i}", [P, 1]) for i in range(2)]

        wst = [xc[0][:].rearrange("p a b -> p (a b)")[:, 0:CH * HID], xc[1][:].rearrange("p a b -> p (a b)")[:, 0:CH * HID],
               xp[:].rearrange("p a b -> p (a b)")[:, 0:KH * FF]]
        wneg = M[0][:].rearrange("p a b -> p (a b)").bitcast(F16)[:, 0:CH * HID]
        wq16 = [M[1][:].rearrange("p a b -> p (a b)").bitcast(F16)[:, 0:CH * HID],
                M[1][:].rearrange("p a b -> p (a b)").bitcast(F16)[:, CH * HID:2 * CH * HID],
                zs[0][:].rearrange("p a b -> p (a b)").bitcast(F16)[:, 0:CH * HID]]
        wabs = shared[:, 0:CH * HID]
        wsum = sb("wsum", [P, 3])
        thr = sb("thr", [P, 2, 3])

        bank = [ctx.enter_context(nc.psum_tensor(f"bank{i}", [P, 512], F32)) for i in range(8)]
        B0, B1, YIN, YST, YOFF, DS = bank[2:]
        YT, XT, BG, OUT = YIN, YST, YOFF, DS

        cst = sem("constants_made")
        zero = sem("zeros_set")
        wl = [sem(f"w_loaded{i}") for i in range(3)]
        pl = sem("params_loaded")
        absd = sem("abs_summed")
        sumd = sem("sums_spread")
        qstep = sem("quant_step")
        wT = sem("weights_turned")
        wTe = sem("weights_kept")
        setup = sem("params_ready")
        expA_r = sem("expA_ready")

        xln_in, xres_in, x_out = sem("xln_in"), sem("xres_in"), sem("x_out")
        ln_step, ln_pow, xn_ready = sem("ln_step"), sem("ln_pow"), sem("xn_ready")
        turned, xhi_ready, xlo_ready = sem("xn_turned"), sem("ffn_xhi_ready"), sem("ffn_xlo_ready")
        up_ready, sig_ready, hid_ready = sem("up_ready"), sem("sig_ready"), sem("hid_ready")
        hhi_ready, hlo_ready, down_done = sem("hhi_ready"), sem("hlo_ready"), sem("down_done")
        res_done = sem("residual_added")
        bank_full, bank_read = sem("proj_bank_full"), sem("proj_bank_read")
        dtc, dt_abs, dt_exp, a_ready = sem("dt_chain"), sem("dt_abs_ready"), sem("dt_exp_ready"), sem("a_ready")
        tail_in, tail_out, tap0, conv_step = sem("tail_in"), sem("tail_kept"), sem("tap0_done"), sem("conv_step")
        silu_c = sem("xBC_ready")
        seg_full, seg_read = sem("seg_bank_full"), sem("seg_bank_read")
        xT_r, bg_r, yst_r, yoff_r = sem("xtok_ready"), sem("BG_ready"), sem("yst_ready"), sem("yoff_ready")
        ds_r, yin_r, yT_r, out_r = sem("dS_ready"), sem("yin_ready"), sem("yT_ready"), sem("proj_out_ready")
        bt_r, xb_r, g2_r = sem("Btok_ready"), sem("XB_ready"), sem("g2_ready")
        xdt_r, gm_r, m_r = sem("xdt_ready"), sem("G_masked"), sem("M_ready")
        t1_r, t2_r, st_r, y_r = sem("t1_ready"), sem("t2_ready"), sem("state_ready"), sem("y_ready")
        yd_r, g_r, ms_r, fin_r = sem("yd_ready"), sem("g_ready"), sem("ms_ready"), sem("tile_done")
        xu_r, xw_r, sd_r, t12_r = sem("xu_ready"), sem("xw_ready"), sem("SD_ready"), sem("t12_ready")
        g2h_r, g2s_r, rs_r = sem("g2_halved"), sem("g2s_ready"), sem("rs_ready")

        ctx.enter_context(nc.allow_non_contiguous_dma(reason="a few hundred parameters, one to a partition"))
        block = ctx.enter_context(nc.Block())

        def ln_stats(dve, u):
            dve.wait_ge(xln_in, u * 16 + 16)
            for t in range(TILES):
                ins = nc.vector.bn_stats(stats[:, t, :], xln[:, t, :])
            ins.then_inc(ln_step, 1)
            dve.wait_ge(ln_step, LN_STEPS * u + 1)
            nc.vector.memset(veps[:], 0.0)
            for t in range(TILES):
                ins = nc.vector.bn_aggr(mv[:, t, :], stats[:, t, :])
            ins.then_inc(ln_step, 1)
            dve.wait_ge(ln_step, LN_STEPS * u + 2)
            nc.vector.tensor_scalar_add(veps[:], mv[:, :, 1], LN_EPS).then_inc(ln_step, 1)

        def ln_apply(dve, u, f=None):
            dve.wait_ge(ln_pow, u + 1)
            if f is not None:
                dve.wait_ge(turned, f)
            for t in range(TILES):
                ins = nc.vector.tensor_scalar(xn[:, t, :], xln[:, t, :], mv[:, t, 0:1], rstd[:, t:t + 1],
                                              ALU.subtract, ALU.mult)
            ins.then_inc(xn_ready, 1)

        def ln_power(pool, u):
            pool.wait_ge(ln_step, LN_STEPS * u + 3)
            nc.gpsimd.tensor_tensor(rstd[:], veps[:], mhalf[:], ALU.pow).then_inc(ln_pow, 1)

        def up_banks(m):
            return bank[2 * (m % 2)], bank[2 * (m % 2) + 1]

        down = [bank[4], bank[5]]
        xTb = [bank[6], bank[7]]

        def pe_turn(pe, u, ffn_u, banks=None):
            pe.wait_ge(xn_ready, u + 1)
            if isinstance(ffn_u, int) and ffn_u == 0:
                pass
            else:
                pe.wait_ge(xlo_ready, ffn_u)
            for k in range(KH):
                for t in range(TILES):
                    ins = nc.tensor.transpose((banks or xTb)[k][:, t * P:(t + 1) * P], xn[:, t, k * P:(k + 1) * P],
                                              identf[:])
            ins.then_inc(turned, 1)

        def pe_up(pe, f, b, m):
            if m == 0:
                pe.wait_ge(xlo_ready, f + 1)
            if not (isinstance(f, int) and f == 0 and m < 2):
                pe.wait_ge(hid_ready, CH * f + m - 1)
            banks = up_banks(m)
            halves = [(banks[0], 2 * m * P, P), (banks[1], (2 * m + 1) * P, P)]
            if m == CH - 1:
                halves = [(banks[0], 2 * m * P, 2 * LAST)]
            for dst, col, n in halves:
                for k in range(KH):
                    for j in range(2):
                        ins = nc.tensor.matmul(dst[0:n, :], w12T[:, k, col:col + n], xsplit[b][j][:, k, :],
                                               start=(k == 0 and j == 0), stop=(k == KH - 1 and j == 1))
            ins.then_inc(up_ready, 1)

        def pe_down(pe, f, m):
            pe.wait_ge(hlo_ready, CH * f + m + 1)
            if m == 0 and not (isinstance(f, int) and f == 0):
                pe.wait_ge(res_done, f)
            n = P if m < CH - 1 else LAST
            for t in range(TILES):
                dst = down[t // 2][:, (t % 2) * HID:(t % 2 + 1) * HID]
                for j in range(2):
                    ins = nc.tensor.matmul(dst, hsplit[j][0:n, m, t * P:(t + 1) * P], w3T[0:n, m, :],
                                           start=(m == 0 and j == 0 and t % 2 == 0),
                                           stop=(m == CH - 1 and j == 1), skip_group_check=True)
            ins.then_inc(down_done, 1)

        def pe_ffn_unit(pe, f, u, b, first, has_next, ahead):
            for m in range(CH):
                pe_up(pe, f, b, m)
                if m == 4 and has_next:
                    pe_turn(pe, u + 1, f + 1)
                if m >= 2:
                    pe_down(pe, f, m - 2)
                elif not first:
                    pe_down(pe, f - 1, CH - 2 + m)

        def act_split_x(act, f, b, banks=None):
            act.wait_ge(turned, f + 1)
            if not (isinstance(f, int) and f < 2):
                act.wait_ge(up_ready, CH * (f - 1))
            for k in range(KH):
                ins = nc.scalar.activation(xsplit[b][0][:, k, :], (banks or xTb)[k][:], ACT.Copy, scale=XS)
            ins.then_inc(xhi_ready, 1)

        def dve_split_x(dve, f, b, banks=None):
            dve.wait_ge(xhi_ready, f + 1)
            for k in range(KH):
                ins = nc.vector.scalar_tensor_tensor(out=xsplit[b][1][:, k, :], in0=(banks or xTb)[k][:], scalar=XS,
                                                     in1=xsplit[b][0][:, k, :], op0=ALU.mult, op1=ALU.subtract)
            ins.then_inc(xlo_ready, 1)

        def rows(m):
            return P if m < CH - 1 else LAST

        def act_sig(act, f, m):
            act.wait_ge(up_ready, CH * f + m + 1)
            if not (isinstance(f, int) and f == 0 and m < 2):
                act.wait_ge(hid_ready, CH * f + m - 1)
            n, banks = rows(m), up_banks(m)
            src = banks[0][:] if m < CH - 1 else banks[0][LAST:2 * LAST, :]
            nc.scalar.activation(sig[m % 2][0:n, :], src, ACT.Sigmoid, scale=1.0 / XS).then_inc(sig_ready, 1)

        def act_hhi(act, f, m):
            act.wait_ge(hid_ready, CH * f + m + 1)
            if not (isinstance(f, int) and f == 0):
                act.wait_ge(down_done, CH * (f - 1) + m + 1)
            n = rows(m)
            nc.scalar.activation(hsplit[0][0:n, m, :], hid[m % 2][0:n, :], ACT.Copy).then_inc(hhi_ready, 1)

        def dve_hid(dve, f, m):
            dve.wait_ge(sig_ready, CH * f + m + 1)
            if not (isinstance(f, int) and f == 0 and m < 2):
                dve.wait_ge(hlo_ready, CH * f + m - 1)
            n, banks = rows(m), up_banks(m)
            src = banks[1][:] if m < CH - 1 else banks[0][0:LAST, :]
            nc.vector.tensor_tensor(hid[m % 2][0:n, :], src, sig[m % 2][0:n, :], ALU.mult).then_inc(hid_ready, 1)

        def pool_hlo(pool, f, m):
            pool.wait_ge(hhi_ready, CH * f + m + 1)
            n = rows(m)
            nc.gpsimd.tensor_tensor(hsplit[1][0:n, m, :], hid[m % 2][0:n, :], hsplit[0][0:n, m, :],
                                    ALU.subtract).then_inc(hlo_ready, 1)

        def dve_residual(dve, f, u):
            dve.wait_ge(down_done, CH * (f + 1))
            dve.wait_ge(xres_in, 16 * (u + 1))
            for j in range(2):
                ins = nc.vector.tensor_tensor(xres[:, 2 * j:2 * j + 2, :], xres[:, 2 * j:2 * j + 2, :],
                                              down[j][:].rearrange("p (t n) -> p t n", t=2), ALU.add)
            ins.then_inc(res_done, 1)

        def act_ffn_unit(act, f, u, b, first, has_next, ahead):
            for m in range(CH):
                act_sig(act, f, m)
                if m > 0:
                    act_hhi(act, f, m - 1)
                elif not first:
                    act_hhi(act, f - 1, CH - 1)
                if m == 4 and has_next:
                    act_split_x(act, f + 1, 1 - b)

        def dve_ffn_unit(dve, f, u, b, first, has_next, ahead):
            for m in range(CH):
                dve_hid(dve, f, m)
                if m == 1 and not first:
                    dve_residual(dve, f - 1, u - 1)
                if m == 2 and ahead:
                    ln_stats(dve, u + 1)
                if m == 3 and ahead:
                    ln_apply(dve, u + 1, f + 1)
                if m == 4 and has_next:
                    dve_split_x(dve, f + 1, 1 - b)

        def pool_ffn_unit(pool, f, u, b, first, has_next, ahead):
            for m in range(CH):
                if m > 0:
                    pool_hlo(pool, f, m - 1)
                elif not first:
                    pool_hlo(pool, f - 1, CH - 1)
                if m == 2 and ahead:
                    ln_power(pool, u + 1)

        def units(eng, body, f0, u0, more):
            body(eng, f0, u0, 0, True, True, True)
            with eng.Fori(0, (UNITS - 2) // 2) as i:
                body(eng, i * 2 + (f0 + 1), i * 2 + (u0 + 1), 1, False, True, True)
                body(eng, i * 2 + (f0 + 2), i * 2 + (u0 + 2), 0, False, True, True)
            body(eng, f0 + UNITS - 1, u0 + UNITS - 1, 1, False, False, more)

        def pe_ffn(pe, f0, u0, more):
            units(pe, pe_ffn_unit, f0, u0, more)
            for m in (CH - 2, CH - 1):
                pe_down(pe, f0 + UNITS - 1, m)

        def act_ffn(act, f0, u0, more):
            units(act, act_ffn_unit, f0, u0, more)
            act_hhi(act, f0 + UNITS - 1, CH - 1)

        def dve_ffn(dve, f0, u0, more):
            units(dve, dve_ffn_unit, f0, u0, more)
            dve_residual(dve, f0 + UNITS - 1, u0 + UNITS - 1)

        def pool_ffn(pool, f0, u0, more):
            units(pool, pool_ffn_unit, f0, u0, more)
            pool_hlo(pool, f0 + UNITS - 1, CH - 1)

        def tokens(dram, row):
            return dram[bass.ds(row, UNIT), :].rearrange("(t p) d -> p t d", p=P)

        def known(eng, value):
            return value if isinstance(value, int) else eng.snap(value)

        def sp_ffn(sp, src, dst, f0, u0, after):
            def unit(i, ahead_src, ahead_row):
                row, row2 = known(sp, i * UNIT), known(sp, ahead_row) if ahead_src is not None else None
                read, added, stored = (known(sp, i + (u0 + 2)), known(sp, i + (f0 + 1)),
                                       known(sp, i * 16 + 16 * u0))
                sp.wait_ge(x_out, stored)
                sp.dma_start(xres[:], tokens(src, row)).then_inc(xres_in, 16)
                if ahead_src is not None:
                    sp.wait_ge(xn_ready, read)
                    sp.dma_start(xln[:], tokens(ahead_src, row2)).then_inc(xln_in, 16)
                sp.wait_ge(res_done, added)
                sp.dma_start(tokens(dst, row), xres[:]).then_inc(x_out, 16)
            unit(0, src, 2 * UNIT)
            with sp.Fori(1, UNITS - 2) as i:
                unit(i, src, i * UNIT + 2 * UNIT)
            for i in range(2):
                if after:
                    unit(UNITS - 2 + i, dst, after[i])
                else:
                    unit(UNITS - 2 + i, None, None)

        M0 = UNITS

        def front_bank(b, n):
            return bank[(b * BANKS + n) % 2]

        def heads_bc(ap):
            return ap.unsqueeze(2).broadcast_to([P, HEADS, HP])

        def by_head(ap):
            return ap.rearrange("p (h c) -> p h c", h=HEADS)

        def pe_bank_free(pe, k_base, n, v_is_first):
            if v_is_first and n < 2:
                return
            pe.wait_ge(bank_read, k_base + n - 1)

        def pe_front(pe, kind, n, v, b):
            first = isinstance(v, int) and v == 0
            at = {"t": 0, "dt": KH, "c": KH + 1}[kind] + n
            dst = front_bank(b, at)
            pe_bank_free(pe, v * BANKS, at, first)
            if kind == "t":
                if n == 0:
                    pe.wait_ge(xn_ready, v + M0 + 1)
                for t in range(TILES):
                    ins = nc.tensor.transpose(dst[:, t * P:(t + 1) * P], xn[:, t, n * P:(n + 1) * P], identf[:])
            elif kind == "dt":
                pe.wait_ge(bank_read, v * BANKS + KH)
                for t in range(TILES):
                    for k in range(KH):
                        ins = nc.tensor.matmul(dst[:, t * HEADS:(t + 1) * HEADS], xnT[:, k, t * P:(t + 1) * P],
                                               wi[:, k, DT0:PROJ], start=(k == 0), stop=(k == KH - 1))
            else:
                col = D_SSM + n * P
                for k in range(KH):
                    ins = nc.tensor.matmul(dst[:], wi[:, k, col:col + P], xnT[:, k, :],
                                           start=(k == 0), stop=(k == KH - 1))
            ins.then_inc(bank_full, 1)

        def pe_z(pe, n, u, b):
            at = PROJS + n
            pe_bank_free(pe, u * BANKS, at, False)
            dst = front_bank(b, at)
            for k in range(KH):
                ins = nc.tensor.matmul(dst[:], wi[:, k, n * P:(n + 1) * P], xnT[:, k, :],
                                       start=(k == 0), stop=(k == KH - 1))
            ins.then_inc(bank_full, 1)

        def masks_of(s):
            if s < SEG0:
                return [(tok_mask[:, n, :], False) for n in (2 * s, 2 * s + 1) if n < DECAYS]
            return [(blk_mask[:, n, :], True) for n in (2 * (s - SEG0), 2 * (s - SEG0) + 1)]

        def pe_seg(pe, s, u, b):
            dst = (B0, B1)[s % 2]
            if not (isinstance(u, int) and u == 0 and s < 2):
                pe.wait_ge(seg_read, u * SEGS + s - 1)
            if s == 0:
                pe.wait_ge(a_ready, u + 1)
            for j, (mask, stacked) in enumerate(masks_of(s)):
                for part in range(2):
                    src = (as16[b][:, part].rearrange("p t c h -> p (t c h)") if stacked
                           else a16[b][:, part].rearrange("p t h -> p (t h)"))
                    ins = nc.tensor.matmul(dst[:, j * 256:(j + 1) * 256], mask, src,
                                           start=(part == 0), stop=(part == 1))
            ins.then_inc(seg_full, 1)

        def pe_tile_in(pe, t, u, b):
            T = u * TILES + t
            if t == 0:
                pe.wait_ge(silu_c, (u + 1) * CT)
            pe.wait_ge(t1_r, T)
            tok = slice(t * P, (t + 1) * P)
            for q in range(Q):
                ins = nc.tensor.transpose(XT[:, q * P:(q + 1) * P], xc[b][:, q, tok], identf[:])
            ins.then_inc(xT_r, 1)
            pe.wait_ge(t2_r, T)
            nc.tensor.transpose(BG[:, 0:P], xc[b][:, Q, tok], identf[:])
            nc.tensor.matmul(BG[:, P:2 * P], xc[b][:, Q, tok], xc[b][:, Q + 1, tok], start=True, stop=True)
            for c in range(NB):
                blk = slice(t * P + c * BLK, t * P + (c + 1) * BLK)
                for q in range(Q):
                    ins = nc.tensor.matmul(BG[q * BLK:(q + 1) * BLK, 2 * P + c * BLK:2 * P + (c + 1) * BLK],
                                           xc[b][:, Q, blk], xc[b][:, Q + 1, blk], start=True, stop=True,
                                           tile_position=(0, q * BLK))
            ins.then_inc(bg_r, 1)

        def pe_tile_cs(pe, t, u, b):
            T = u * TILES + t
            pe.wait_ge(xdt_r, T + 1)
            pe.wait_ge(st_r, T)
            for c in range(NB):
                blk = slice(t * P + c * BLK, t * P + (c + 1) * BLK)
                ins = nc.tensor.matmul(YST[c * BLK:(c + 1) * BLK, :], xc[b][:, Q + 1, blk], S[b][:],
                                       start=True, stop=True, tile_position=(0, c * BLK))
            ins.then_inc(yst_r, 1)
            pe.wait_ge(gm_r, T + 1)
            pe.wait_ge(bt_r, T + 1)
            pe.wait_ge(xu_r, T + 1)
            for c in range(NB):
                ins = nc.tensor.matmul(YOFF[c * BLK:(c + 1) * BLK, :], Goff[:, c * BLK:(c + 1) * BLK],
                                       xu[:, max(c - 1, 0), :], start=True, stop=True,
                                       tile_position=(0, c * BLK))
            ins.then_inc(yoff_r, 1)

        def pe_tile_ds(pe, t, u):
            T = u * TILES + t
            pe.wait_ge(xw_r, T + 1)
            pe.wait_ge(fin_r, T if t == 0 else T - 1)
            nc.tensor.matmul(DS[:], Btok[:], xw[:], start=True, stop=True).then_inc(ds_r, 1)

        def pe_tile_diag(pe, t, u):
            T = u * TILES + t
            pe.wait_ge(yd_r, T)
            pe.wait_ge(m_r, T + 1)
            pe.wait_ge(xb_r, T + 1)
            for h in range(HQ):
                for c in range(NB):
                    dst = YIN[c * BLK:(c + 1) * BLK, :].rearrange("i (q h p) -> i q h p", q=Q, h=HQ)[:, :, h, :]
                    ins = nc.tensor.matmul(dst, M[t % 2][:, c * HQ + h, :], XB[t % 2][:, c, h, :],
                                           start=True, stop=True, tile_position=(0, c * BLK))
            ins.then_inc(yin_r, 1)

        def pe_tile_turn(pe, t, u):
            T = u * TILES + t
            pe.wait_ge(y_r, T + 1)
            for q in range(Q):
                ins = nc.tensor.transpose(YT[:, q * P:(q + 1) * P], y[:, q * P:(q + 1) * P], identf[:])
            ins.then_inc(yT_r, 1)

        def pe_tile_out(pe, t, u):
            T = u * TILES + t
            pe.wait_ge(st_r, T + 1 if t == TILES - 1 else T + 2)
            pe.wait_ge(fin_r, T)
            pe.wait_ge(g_r, T + 1)
            for q in range(Q):
                nc.tensor.matmul(OUT[:, 0:HID], g[:, q, :], wo[:, q, :], start=(q == 0), stop=(q == Q - 1))
            pe.wait_ge(g2s_r, T + 1)
            nc.tensor.matmul(OUT[:, HID:HID + 1], g2[:, 0, :], ones[:, 0:1], start=True, stop=True).then_inc(out_r, 1)

        def pe_slot(pe, u, b, first, has_next):
            pe_tile_in(pe, 0, u, b)
            for kind, n in slot_head(has_next):
                if kind == "seg":
                    pe_seg(pe, n, u, b)
                elif kind == "turn":
                    if not first:
                        pe_tile_turn(pe, TILES - 1, u - 1)
                elif kind == "out":
                    if not first:
                        pe_tile_out(pe, TILES - 1, u - 1)
                elif kind == "state":
                    pe_tile_cs(pe, 0, u, b)
                elif kind in ("t", "dt"):
                    pe_front(pe, kind, n, u + 1, 1 - b)
            for t in range(TILES):
                if t > 0:
                    pe_tile_cs(pe, t, u, b)
                if t + 1 < TILES:
                    pe_tile_in(pe, t + 1, u, b)
                if t > 0:
                    pe_tile_turn(pe, t - 1, u)
                if t < TILES - 1:
                    pe_tile_ds(pe, t, u)
                if has_next and 2 * t < CT:
                    pe_front(pe, "c", 2 * t, u + 1, 1 - b)
                if has_next and t == TILES - 1:
                    pe_z(pe, 0, u + 1, 1 - b)
                if t == TILES - 1:
                    pe_tile_ds(pe, t, u)
                if has_next and t == TILES - 1:
                    for s in range(2):
                        pe_seg(pe, s, u + 1, 1 - b)
                    pe_z(pe, 1, u + 1, 1 - b)
                pe_tile_diag(pe, t, u)
                if has_next and t == TILES - 1:
                    pe_z(pe, 2, u + 1, 1 - b)
                    pe_z(pe, 3, u + 1, 1 - b)
                if has_next and 2 * t < CT:
                    pe_front(pe, "c", 2 * t + 1, u + 1, 1 - b)
                if t > 0:
                    pe_tile_out(pe, t - 1, u)
                if has_next and t == TILES - 1:
                    for s in range(2, EARLY):
                        pe_seg(pe, s, u + 1, 1 - b)

        def act_front(act, kind, n, v, b):
            at = {"t": 0, "dt": KH, "c": KH + 1}[kind] + n
            src = front_bank(b, at)
            act.wait_ge(bank_full, v * BANKS + at + 1)
            if kind == "t":
                nc.scalar.activation(xnT[:, n, :], src[:], ACT.Copy).then_inc(bank_read, 1)
            elif kind == "dt":
                if not (isinstance(v, int) and v == 0):
                    act.wait_ge(dtc, v * DTC)
                nc.scalar.activation(dtr[:].rearrange("p t h -> p (t h)"), src[:, 0:TILES * HEADS],
                                     ACT.Copy).then_inc(bank_read, 1)
            else:
                rows_of = xp[:, n % XPS]
                if not (isinstance(v, int) and v == 0 and n < XPS):
                    act.wait_ge(tail_out, v * CT + n - XPS + 1)
                nc.scalar.activation(rows_of[:, 0:TAPS - 1], tails[b][:, n, :], ACT.Copy).then_inc(tail_in, 1)
                nc.scalar.activation(rows_of[:, TAPS - 1:], src[:], ACT.Copy).then_inc(bank_read, 1)
                act.wait_ge(tail_in, v * CT + n + 1)
                act.wait_ge(bank_read, v * BANKS + at + 1)
                nc.scalar.activation(xc[b][:, n, :], rows_of[:, 0:UNIT], ACT.Identity,
                                     scale=cw[:, n, 0:1], bias=cb[:, n:n + 1]).then_inc(tap0, 1)

        def act_z(act, n, u, b):
            act.wait_ge(bank_full, u * BANKS + PROJS + n + 1)
            nc.scalar.activation(zs[b][:, n, :], front_bank(b, PROJS + n)[:], ACT.Silu,
                                 scale=mupc[:, n:n + 1]).then_inc(bank_read, 1)

        def act_seg(act, s, u):
            act.wait_ge(seg_full, u * SEGS + s + 1)
            if s == 0:
                act.wait_ge(m_r, u * TILES)
                act.wait_ge(sd_r, u * TILES)
                act.wait_ge(xu_r, u * TILES)
                act.wait_ge(xw_r, u * TILES)
                act.wait_ge(t2_r, u * TILES)
            src = (B0, B1)[s % 2]
            n = len(masks_of(s))
            dst = dec[:, 2 * s:2 * s + n] if s < SEG0 else L[:, 2 * (s - SEG0):2 * (s - SEG0) + n]
            nc.scalar.activation(dst.rearrange("p n t h -> p (n t h)"), src[:, 0:n * 256], ACT.Exp,
                                 scale=-1.0 / AS).then_inc(seg_read, 1)

        def act_dt_exp(act, v):
            act.wait_ge(dt_abs, v + 1)
            nc.scalar.activation(dt_e[:], dt_e[:], ACT.Exp, scale=-1.0).then_inc(dt_exp, 1)

        def act_stack(act, v, b):
            act.wait_ge(dtc, (v + 1) * DTC)
            for q in range(Q):
                for c in range(NB):
                    ins = nc.scalar.activation(as16[b][q * BLK:(q + 1) * BLK, :, :, c, :],
                                               a16[b][c * BLK:(c + 1) * BLK, :, :, q * HQ:(q + 1) * HQ], ACT.Copy)
            ins.then_inc(a_ready, 1)

        def act_silu_conv(act, n, v, b):
            act.wait_ge(conv_step, v * CONV + (n + 1) * (TAPS - 1))
            nc.scalar.activation(xc[b][:, n, :], xc[b][:, n, :], ACT.Silu).then_inc(silu_c, 1)

        def act_tile_b(act, t, u):
            T = u * TILES + t
            act.wait_ge(gm_r, T + 1)
            act.wait_ge(ds_r, T)
            nc.scalar.activation(Btok[:], BG[:, 0:P], ACT.Copy).then_inc(bt_r, 1)

        def act_tile_xb(act, t, u):
            T = u * TILES + t
            act.wait_ge(xdt_r, T + 1)
            act.wait_ge(yin_r, max(t - 1, 0) + u * TILES)
            for q in range(Q):
                for c in range(NB):
                    ins = nc.scalar.activation(
                        XB[t % 2][q * BLK:(q + 1) * BLK, c, :, q * HP:(q + 1) * HP],
                        xdt[t % 2][c * BLK:(c + 1) * BLK, q * P:(q + 1) * P].rearrange("p (h c) -> p h c", c=HP),
                        ACT.Copy)
            ins.then_inc(xb_r, 1)

        def act_tile_sq(act, t, u):
            T = u * TILES + t
            act.wait_ge(g_r, T + 1)
            act.wait_ge(g2s_r, T)
            nc.scalar.activation(g2[:], g[:], ACT.Square).then_inc(g2_r, 1)

        def act_slot(act, u, b, first, has_next):
            v, bv = u + 1, 1 - b
            act_tile_b(act, 0, u)
            for kind, n in slot_head(has_next):
                if kind == "seg":
                    act_seg(act, n, u)
                elif kind == "square":
                    if not first:
                        act_tile_sq(act, TILES - 1, u - 1)
                elif kind == "exp":
                    act_dt_exp(act, v)
                elif kind == "x":
                    act_tile_xb(act, 0, u)
                elif kind in ("t", "dt"):
                    act_front(act, kind, n, v, bv)
            for t in range(TILES):
                if t + 1 < TILES:
                    act_tile_b(act, t + 1, u)
                if t > 0:
                    act_tile_sq(act, t - 1, u)
                if has_next and 2 * t < CT:
                    act_front(act, "c", 2 * t, v, bv)
                if t + 1 < TILES:
                    act_tile_xb(act, t + 1, u)
                if has_next and 2 * t < CT:
                    act_front(act, "c", 2 * t + 1, v, bv)
                elif has_next:
                    act_z(act, 0, v, bv)
                    act_z(act, 1, v, bv)
                if has_next and t > 0:
                    act_silu_conv(act, 2 * t - 2, v, bv)
                    act_silu_conv(act, 2 * t - 1, v, bv)
                if has_next and t == 1:
                    act_stack(act, v, bv)
            if has_next:
                act_z(act, 2, v, bv)
                act_z(act, 3, v, bv)
                for s in range(EARLY):
                    act_seg(act, s, v)

        def dve_dt_head(dve, v):
            c = v * DTC
            dve.wait_ge(bank_read, v * BANKS + KH + 1)
            mb = mup_dt[:].unsqueeze(1).broadcast_to([P, TILES, HEADS])
            bb = bias_dt[:].unsqueeze(1).broadcast_to([P, TILES, HEADS])
            nc.vector.tensor_tensor(dt_q[:], dtr[:], mb, ALU.mult).then_inc(dtc, 1)
            dve.wait_ge(dtc, c + 1)
            nc.vector.tensor_tensor(dt_q[:], dt_q[:], bb, ALU.add).then_inc(dtc, 1)
            dve.wait_ge(dtc, c + 2)
            nc.vector.scalar_tensor_tensor(out=dt_e[:], in0=dt_q[:], scalar=-1.0, in1=dt_q[:],
                                           op0=ALU.mult, op1=ALU.max).then_inc(dt_abs, 1)

        def dve_dt_series(dve, v):
            n = v * DTC + 2

            def step(k):
                dve.wait_ge(dtc, n + k)

            dve.wait_ge(dt_exp, v + 1)
            nc.vector.tensor_scalar_add(dt_s, dt_e[:], 2.0).then_inc(dtc, 1)
            step(1)
            nc.vector.reciprocal(dt_s, dt_s).then_inc(dtc, 1)
            step(2)
            nc.vector.tensor_tensor(dt_s, dt_e[:], dt_s, ALU.mult).then_inc(dtc, 1)
            step(3)
            nc.vector.tensor_tensor(dtr[:], dt_s, dt_s, ALU.mult).then_inc(dtc, 1)
            step(4)
            nc.vector.tensor_scalar(dt_e[:], dtr[:], 1.0 / (2 * SERIES - 1), None, ALU.mult).then_inc(dtc, 1)
            for k in range(SERIES - 2):
                step(5 + k)
                nc.vector.scalar_tensor_tensor(out=dt_e[:], in0=dt_e[:], scalar=1.0 / (2 * (SERIES - 2 - k) + 1),
                                               in1=dtr[:], op0=ALU.add, op1=ALU.mult).then_inc(dtc, 1)

        def dve_dt_softplus(dve, v, b):
            n = v * DTC + 2

            def step(k):
                dve.wait_ge(dtc, n + k)

            k = 5 + SERIES - 2
            step(k)
            nc.vector.scalar_tensor_tensor(out=dt_e[:], in0=dt_e[:], scalar=1.0, in1=dt_s,
                                           op0=ALU.add, op1=ALU.mult).then_inc(dtc, 1)
            step(k + 1)
            nc.vector.tensor_scalar(dt_e[:], dt_e[:], 2.0, None, ALU.mult).then_inc(dtc, 1)
            step(k + 2)
            nc.vector.scalar_tensor_tensor(out=dts[b][:], in0=dt_q[:], scalar=0.0, in1=dt_e[:],
                                           op0=ALU.max, op1=ALU.add).then_inc(dtc, 1)
            step(k + 3)
            ea = expA[:].unsqueeze(1).broadcast_to([P, TILES, HEADS])
            nc.vector.tensor_tensor(dt_e[:], dts[b][:], ea, ALU.mult).then_inc(dtc, 1)
            step(k + 4)
            nc.vector.tensor_scalar(dt_e[:], dt_e[:], A_MAX, AS, ALU.min, ALU.mult).then_inc(dtc, 1)

        def dve_dt_split(dve, v, b):
            n = v * DTC + 2

            def step(k):
                dve.wait_ge(dtc, n + k)

            k = 5 + SERIES - 2
            step(k + 5)
            nc.vector.tensor_copy(a16[b][:, 0], dt_e[:]).then_inc(dtc, 1)
            step(k + 6)
            nc.vector.tensor_tensor(a16[b][:, 1], dt_e[:], a16[b][:, 0], ALU.subtract).then_inc(dtc, 1)
            assert 2 + k + 7 == DTC

        def dve_conv(dve, n, v, b):
            dve.wait_ge(tap0, v * CT + n + 1)
            for k in range(1, TAPS):
                if k > 1:
                    dve.wait_ge(conv_step, v * CONV + n * (TAPS - 1) + k - 1)
                nc.vector.scalar_tensor_tensor(out=xc[b][:, n, :], in0=xp[:, n % XPS, k:k + UNIT], scalar=cw[:, n, k:k + 1],
                                               in1=xc[b][:, n, :], op0=ALU.mult, op1=ALU.add).then_inc(conv_step, 1)

            nc.vector.tensor_copy(tails[b][:, n, :], xp[:, n % XPS, UNIT:]).then_inc(tail_out, 1)

        def dve_tile_in(dve, t, u, b):
            T = u * TILES + t
            lag = max(t - 1, 0) + u * TILES
            dve.wait_ge(xT_r, T + 1)
            dve.wait_ge(xb_r, lag)
            dve.wait_ge(xu_r, lag)
            dve.wait_ge(xw_r, lag)
            nc.vector.tensor_tensor(by_head(xdt[t % 2][:]), by_head(XT[:]), heads_bc(dts[b][:, t, :]),
                                    ALU.mult).then_inc(xdt_r, 1)
            dve.wait_ge(bg_r, T + 1)
            dve.wait_ge(yoff_r, T)
            dve.wait_ge(m_r, T)
            nc.vector.tensor_tensor(Gd[:], BG[:, 2 * P:3 * P].rearrange("p (c i) -> p c i", c=NB),
                                    causal[:].unsqueeze(1).broadcast_to([P, NB, BLK]), ALU.mult)
            nc.vector.tensor_tensor(Goff[:], BG[:, P:2 * P], off_mask[:], ALU.mult).then_inc(gm_r, 1)

        def dve_tile_m(dve, t, u):
            T = u * TILES + t
            if t == 0:
                dve.wait_ge(seg_read, (u + 1) * SEGS)
            dve.wait_ge(gm_r, T + 1)
            dve.wait_ge(yin_r, max(t - 1, 0) + u * TILES)
            nc.vector.tensor_tensor(M[t % 2][:].rearrange("p (c h) i -> p c h i", c=NB),
                                    L[:, :, t, :].rearrange("p i (c h) -> p c h i", c=NB),
                                    Gd[:].unsqueeze(2).broadcast_to([P, NB, HQ, BLK]), ALU.mult).then_inc(m_r, 1)

        def dve_tile_cs(dve, t, u):
            T = u * TILES + t
            dve.wait_ge(yst_r, T + 1)
            dve.wait_ge(y_r, T)
            nc.vector.tensor_tensor(by_head(t1[:]), by_head(YST[:]), heads_bc(dec[:, V_TILE, t, :]),
                                    ALU.mult).then_inc(t1_r, 1)
            dve.wait_ge(yoff_r, T + 1)
            dve.wait_ge(t12_r, T)
            nc.vector.tensor_tensor(by_head(t2[:]), by_head(YOFF[:]), heads_bc(dec[:, V_BLK, t, :]),
                                    ALU.mult).then_inc(t2_r, 1)

        def dve_tile_s(dve, t, u, b):
            T = u * TILES + t
            dve.wait_ge(ds_r, T + 1)
            dve.wait_ge(sd_r, T + 1)
            nc.vector.tensor_tensor(S[b][:], S[b][:], DS[:], ALU.add).then_inc(st_r, 1)

        def dve_tile_gate(dve, t, u, b):
            T = u * TILES + t
            tok = slice(t * P, (t + 1) * P)
            dve.wait_ge(yT_r, T + 1)
            dve.wait_ge(g_r, T)
            for q in range(Q):
                ins = nc.vector.scalar_tensor_tensor(out=yd[:, q, :], in0=xc[b][:, q, tok], scalar=dcol[:, q:q + 1],
                                                     in1=YT[:, q * P:(q + 1) * P], op0=ALU.mult, op1=ALU.add)
            ins.then_inc(yd_r, 1)
            if t == 0:
                dve.wait_ge(bank_read, (u + 1) * BANKS)
            dve.wait_ge(yd_r, T + 1)
            dve.wait_ge(out_r, T)
            dve.wait_ge(g2_r, T)
            nc.vector.tensor_tensor(g[:], yd, zs[b][:, :, tok], ALU.mult).then_inc(g_r, 1)

        def dve_tile_y(dve, t, u):
            T = u * TILES + t
            dve.wait_ge(yin_r, T + 1)
            dve.wait_ge(t12_r, T + 1)
            dve.wait_ge(g_r, T)
            nc.vector.tensor_tensor(y[:], t1[:], YIN[:], ALU.add).then_inc(y_r, 1)

        def dve_tile_ms(dve, t, u):
            T = u * TILES + t
            dve.wait_ge(out_r, T + 1)
            nc.vector.tensor_scalar(ms[t % 2][:], OUT[:, HID:HID + 1], 1.0 / D_SSM, RMS_EPS,
                                    ALU.mult, ALU.add).then_inc(ms_r, 1)

        def dve_tile_fin(dve, t, u):
            T = u * TILES + t
            if t == 0:
                dve.wait_ge(xres_in, (u + M0 + 1) * 16)
            dve.wait_ge(rs_r, T + 1)
            nc.vector.scalar_tensor_tensor(out=xres[:, t, :], in0=OUT[:, 0:HID], scalar=rs[t % 2][:],
                                           in1=xres[:, t, :], op0=ALU.mult, op1=ALU.add).then_inc(fin_r, 1)

        def dve_slot(dve, u, b, first, has_next):
            v, bv = u + 1, 1 - b
            dve_tile_in(dve, 0, u, b)
            if not first:
                dve_tile_ms(dve, TILES - 2, u - 1)
                dve_tile_fin(dve, TILES - 2, u - 1)
                dve_tile_gate(dve, TILES - 1, u - 1, bv)
            if has_next:
                dve_dt_head(dve, v)
                dve_dt_series(dve, v)
            if not first:
                dve_tile_ms(dve, TILES - 1, u - 1)
                dve_tile_fin(dve, TILES - 1, u - 1)
            dve_tile_cs(dve, 0, u)
            dve_tile_m(dve, 0, u)
            for t in range(TILES):
                if t > 1:
                    dve_tile_ms(dve, t - 2, u)
                if t > 0:
                    dve_tile_cs(dve, t, u)
                if t + 1 < TILES:
                    dve_tile_in(dve, t + 1, u, b)
                if t > 1:
                    dve_tile_fin(dve, t - 2, u)
                if t > 0:
                    dve_tile_gate(dve, t - 1, u, b)
                dve_tile_s(dve, t, u, b)
                if has_next and t > 0:
                    dve_conv(dve, 2 * t - 1, v, bv)
                if has_next and t == 0:
                    dve_dt_softplus(dve, v, bv)
                if t + 1 < TILES:
                    dve_tile_m(dve, t + 1, u)
                if has_next and t == 1:
                    dve_dt_split(dve, v, bv)
                dve_tile_y(dve, t, u)
                if has_next and 2 * t < CT:
                    dve_conv(dve, 2 * t, v, bv)
            if has_next:
                ln_stats(dve, u + (M0 + 2))
                ln_apply(dve, u + (M0 + 2))

        def pool_tile_x(pool, t, u):
            T = u * TILES + t
            src = by_head(xdt[t % 2][:])
            pool.wait_ge(xdt_r, T + 1)
            if t == 0:
                pool.wait_ge(seg_read, u * SEGS + SEG0)
            pool.wait_ge(yoff_r, T)
            for i in range(NB - 1):
                ins = nc.gpsimd.tensor_tensor(by_head(xu[:, i, :]), src, heads_bc(dec[:, U_1 + i, t, :]), ALU.mult)
            ins.then_inc(xu_r, 1)
            pool.wait_ge(ds_r, T)
            nc.gpsimd.tensor_tensor(by_head(xw[:]), src, heads_bc(dec[:, W_END, t, :]), ALU.mult).then_inc(xw_r, 1)

        def pool_tile_sd(pool, t, u, b):
            T = u * TILES + t
            pool.wait_ge(yst_r, T + 1)
            nc.gpsimd.tensor_tensor(by_head(S[b][:]), by_head(S[b][:]), heads_bc(dec[:, TOTAL, t, :]),
                                    ALU.mult).then_inc(sd_r, 1)

        def pool_tile_sum(pool, t, u):
            T = u * TILES + t
            pool.wait_ge(t1_r, T + 1)
            pool.wait_ge(t2_r, T + 1)
            nc.gpsimd.tensor_tensor(t1[:], t1[:], t2[:], ALU.add).then_inc(t12_r, 1)

        def pool_tile_sq(pool, t, u):
            T = u * TILES + t
            pool.wait_ge(g2_r, T + 1)
            nc.gpsimd.tensor_tensor(g2[:, 0:2, :], g2[:, 0:2, :], g2[:, 2:4, :], ALU.add).then_inc(g2h_r, 1)
            pool.wait_ge(g2h_r, T + 1)
            pool.wait_ge(out_r, T)
            nc.gpsimd.tensor_tensor(g2[:, 0, :], g2[:, 0, :], g2[:, 1, :], ALU.add).then_inc(g2s_r, 1)

        def pool_tile_rs(pool, t, u):
            T = u * TILES + t
            pool.wait_ge(ms_r, T + 1)
            pool.wait_ge(fin_r, max(t - 1, 0) + u * TILES)
            nc.gpsimd.tensor_tensor(rs[t % 2][:], ms[t % 2][:], mhalf[:, 0:1], ALU.pow).then_inc(rs_r, 1)

        def pool_slot(pool, u, b, first, has_next):
            if not first:
                pool_tile_rs(pool, TILES - 2, u - 1)
            pool_tile_x(pool, 0, u)
            if not first:
                pool_tile_sq(pool, TILES - 1, u - 1)
                pool_tile_rs(pool, TILES - 1, u - 1)
            pool_tile_sd(pool, 0, u, b)
            pool_tile_sum(pool, 0, u)
            for t in range(TILES):
                if t > 1:
                    pool_tile_rs(pool, t - 2, u)
                if t > 0:
                    pool_tile_sd(pool, t, u, b)
                    pool_tile_sum(pool, t, u)
                if t + 1 < TILES:
                    pool_tile_x(pool, t + 1, u)
                if t > 0:
                    pool_tile_sq(pool, t - 1, u)
            if has_next:
                ln_power(pool, u + (M0 + 2))

        def slots(eng, body):
            body(eng, 0, 0, True, True)
            with eng.Fori(0, UNITS // 2 - 1) as i:
                body(eng, i * 2 + 1, 1, False, True)
                body(eng, i * 2 + 2, 0, False, True)
            body(eng, UNITS - 1, 1, False, False)

        def row_of(i, b):
            return i * UNIT + b * LEN

        def sp_mamba(sp):
            def unit(i, b, ahead_src, ahead_row):
                u = i * 2 + b
                row, row2 = known(sp, row_of(i, b)), known(sp, ahead_row)
                read, summed, stored = (known(sp, u + (M0 + 2)), known(sp, u * TILES + TILES),
                                        known(sp, u * 16 + 16 * M0))
                sp.wait_ge(x_out, stored)
                sp.dma_start(xres[:], tokens(mid1, row)).then_inc(xres_in, 16)
                sp.wait_ge(xn_ready, read)
                sp.dma_start(xln[:], tokens(ahead_src, row2)).then_inc(xln_in, 16)
                sp.wait_ge(fin_r, summed)
                sp.dma_start(tokens(mid2, row), xres[:]).then_inc(x_out, 16)
            for b in range(2):
                unit(0, b, mid1, row_of(1, b))
            with sp.Fori(1, UNITS // 2 - 1) as i:
                for b in range(2):
                    unit(i, b, mid1, row_of(i, b) + UNIT)
            for b in range(2):
                unit(UNITS // 2 - 1, b, mid2, b * UNIT)

        def last_uses(eng, tiles):
            eng.wait_ge(bank_read, UNITS * BANKS)
            eng.wait_ge(seg_read, UNITS * SEGS)
            for s in (m_r, t1_r, t2_r, yd_r, fin_r):
                eng.wait_ge(s, tiles)

        NPARAM = 9 + Q
        FFN_CONST, MASKS = 3, 23
        LAST_U, LAST_T, LAST_B = UNITS - 1, TILES - 1, (UNITS - 1) % 2

        @block.sync
        def _(sp):
            sp.dma_start(xln[:], tokens(x_flat, 0)).then_inc(xln_in, 16)
            sp.wait_ge(zero, 1)
            for i, w in enumerate((w1, w2)):
                full = (CH - 1) * P
                v = wst[i].rearrange("p (r k) -> p r k", k=HID)
                sp.dma_start(v[:, 0:CH - 1, :], w[0:full, :].rearrange("(r p) k -> p r k", p=P)).then_inc(wl[i], 16)
                sp.dma_start(v[0:LAST, CH - 1, :], w[full:FF, :]).then_inc(wl[i], 16)
            sp.dma_start(wst[2].rearrange("p (o f) -> p o f", f=FF),
                         w3.rearrange("(o p) f -> p o f", p=P)).then_inc(wl[2], 16)
            sp.wait_ge(xn_ready, 1)
            sp.dma_start(xln[:], tokens(x_flat, UNIT)).then_inc(xln_in, 16)

            def cols(ap):
                return ap.rearrange("(c p) -> p c", p=P)
            sp.dma_start(wi[:], W_in.rearrange("(k p) n -> p k n", p=P)).then_inc(pl, 16)
            sp.dma_start(wo[:], W_out.rearrange("(q p) n -> p q n", p=P)).then_inc(pl, 16)
            sp.dma_start(nw[:], cols(norm_w)).then_inc(pl, 16)
            sp.dma_start(cw[:], conv_w.rearrange("(c p) k -> p c k", p=P)).then_inc(pl, 16)
            sp.dma_start(cb[:], cols(conv_b)).then_inc(pl, 16)
            sp.dma_start(mupc[:], cols(mup[0:DT0])).then_inc(pl, 16)
            for q in range(Q):
                sp.dma_start(dcol[:, q:q + 1],
                             D_w[q * HQ:(q + 1) * HQ].unsqueeze(1).broadcast_to([HQ, HP])).then_inc(pl, 16)
            sp.dma_start(mup_dt[:], mup[DT0:PROJ].unsqueeze(0).broadcast_to([P, HEADS])).then_inc(pl, 16)
            sp.dma_start(bias_dt[:], dt_bias.unsqueeze(0).broadcast_to([P, HEADS])).then_inc(pl, 16)
            sp.dma_start(expA[:], A_log.unsqueeze(0).broadcast_to([P, HEADS])).then_inc(pl, 16)

            sp_ffn(sp, x_flat, mid1, 0, 0, (row_of(0, 0), row_of(0, 1)))
            sp_mamba(sp)
            sp_ffn(sp, mid2, out_flat, UNITS, 2 * UNITS, None)
            sp.wait_ge(x_out, 16 * UNITS * 3)

        @block.gpsimd
        def _(pool):
            fp = nc.gpsimd
            made = [0]

            def step(ins):
                ins.then_inc(cst, 1)
                made[0] += 1

            def select(ap, op, fill, base, pattern, mult):
                pool.wait_ge(cst, made[0])
                step(fp.affine_select(out=ap, in_=ap, compare_op=op, fill=fill, base=base, pattern=pattern,
                                      channel_multiplier=mult))

            fp.memset(wst[0][:, (CH - 1) * HID:], 0.0)
            fp.memset(wst[1][:, (CH - 1) * HID:], 0.0).then_inc(zero, 1)
            fp.memset(ones[:], 1.0)
            fp.memset(mhalf[:], -0.5)
            fp.memset(identf[:], 0.0)
            step(fp.memset(ident16[:], 0.0))
            select(identf[:], ALU.not_equal, 1.0, 0, [[-1, P]], 1)
            select(ident16[:], ALU.not_equal, 1.0, 0, [[-1, P]], 1)
            assert made[0] == FFN_CONST
            ln_power(pool, 0)

            fp.memset(tok_mask[:], 1.0)
            fp.memset(causal[:], 1.0)
            step(fp.memset(off_mask[:], 1.0))
            select(tok_mask[:, V_BLK], ALU.is_ge, 0.0, 0, [[1, P]], -1)
            select(tok_mask[:, V_TILE], ALU.is_ge, 0.0, 0, [[1, P]], -1)
            for i in range(NB - 1):
                select(tok_mask[:, U_1 + i], ALU.is_gt, 0.0, 0, [[-1, P]], 1)
            select(tok_mask[:, W_END], ALU.is_gt, 0.0, 0, [[-1, P]], 1)
            select(off_mask[:].rearrange("p (c i) -> p c i", c=NB), ALU.is_gt, 0.0, 0, [[BLK, NB], [0, BLK]], -1)
            for q in range(NB):
                select(causal[q * BLK:(q + 1) * BLK, :], ALU.is_ge, 0.0, 0, [[1, BLK]], -1)
            select(tok_mask[:, V_BLK].rearrange("p (c i) -> p c i", c=NB), ALU.is_ge, 0.0, 0,
                   [[-BLK, NB], [0, BLK]], 1)
            for i in range(NB - 1):
                select(tok_mask[:, U_1 + i], ALU.is_ge, 0.0, BLK * (i + 1) - 1, [[0, P]], -1)

            pool_ffn(pool, 0, 0, True)

            for b in range(2):
                fp.memset(S[b][:], 0.0)
                ins = fp.memset(tails[b][:], 0.0)
            ins.then_inc(zero, 1)
            step(fp.memset(blk_mask[:], 1.0))
            ln_power(pool, M0 + 1)
            bm = blk_mask[:].rearrange("p i (q j) -> p i q j", q=Q)
            select(bm, ALU.is_gt, 0.0, 0, [[0, BLK], [-BLK, Q], [-1, BLK]], 1)
            select(bm, ALU.is_ge, 0.0, 0, [[1, BLK], [BLK, Q], [0, BLK]], -1)
            fp.memset(XB[0][:], 0.0)
            step(fp.memset(XB[1][:], 0.0))
            assert made[0] == MASKS

            slots(pool, pool_slot)
            pool_tile_rs(pool, LAST_T - 1, LAST_U)
            pool_tile_sq(pool, LAST_T, LAST_U)
            pool_tile_rs(pool, LAST_T, LAST_U)
            pool_ffn(pool, UNITS, 2 * UNITS, False)

        @block.tensor
        def _(pe):
            pe.wait_ge(cst, FFN_CONST)
            pe.wait_ge(absd, 3)
            nc.tensor.matmul(xTb[0][:, 0:3], ones[:], wsum[:], start=True, stop=True).then_inc(sumd, 1)
            pe.wait_ge(qstep, 1)
            pe_turn(pe, 0, 0)
            for i in range(6):
                w, k = i // 2, i % 2
                dst = bank[i][:].bitcast(F16)
                pe.wait_ge(qstep, 5 + 2 * w)
                if w < 2:
                    v = wq16[w].rearrange("p (r k) -> p r k", k=HID)
                    for r in range(CH):
                        n = P if r < CH - 1 else LAST
                        ins = nc.tensor.transpose(dst[:, r * P:r * P + n], v[0:n, r, k * P:(k + 1) * P],
                                                  ident16[0:n, 0:n])
                else:
                    v = wq16[2][:, 0:KH * FF].rearrange("p (o f) -> p o f", f=FF)
                    for r in range(CH):
                        n = P if r < CH - 1 else LAST
                        ins = nc.tensor.transpose(dst[0:n, r * P:(r + 1) * P], v[:, k, r * P:r * P + n], ident16[:])
                ins.then_inc(wT, 1)
            pe.wait_ge(wTe, 6)
            pe_ffn(pe, 0, 0, True)

            pe.wait_ge(pl, 16 * NPARAM)
            pe.wait_ge(hid_ready, UNITS * CH)
            for n in range(KH):
                pe_front(pe, "t", n, 0, 0)
            pe_front(pe, "dt", 0, 0, 0)
            for n in range(CT - 1):
                pe_front(pe, "c", n, 0, 0)
            pe.wait_ge(xlo_ready, UNITS)
            pe.wait_ge(res_done, UNITS)
            pe.wait_ge(zero, 2)
            pe.wait_ge(cst, MASKS)
            for n in range(EARLY):
                pe_seg(pe, n, 0, 0)
            pe_front(pe, "c", CT - 1, 0, 0)
            for n in range(Q):
                pe_z(pe, n, 0, 0)
            pe.wait_ge(setup, 2)
            slots(pe, pe_slot)
            pe_tile_turn(pe, LAST_T, LAST_U)
            pe.wait_ge(bank_read, UNITS * BANKS)
            pe.wait_ge(seg_read, UNITS * SEGS)
            pe_turn(pe, 2 * UNITS, UNITS, (B0, B1))
            pe_tile_out(pe, LAST_T, LAST_U)
            last_uses(pe, UNITS * TILES)
            pe_ffn(pe, UNITS, 2 * UNITS, False)

        @block.scalar
        def _(act):
            for i in range(3):
                act.wait_ge(wl[i], 32 if i < 2 else 16)
                if i > 0:
                    act.wait_ge(absd, i)
                n = CH * HID if i < 2 else KH * FF
                nc.scalar.activation(wabs[:, 0:n], wst[i][:, 0:n], ACT.Abs, accum_out=wsum[:, i:i + 1]).then_inc(absd, 1)
            act.wait_ge(absd, 3)
            act_split_x(act, 0, 0)
            for i in range(6):
                w, k = i // 2, i % 2
                src = bank[i][:].bitcast(F16)
                act.wait_ge(wT, i + 1)
                if w < 2:
                    scale = (1.0, W2S)[w]
                    main = w12T[:, k, 0:2 * (CH - 1) * P].rearrange("p (m s n) -> p m s n", s=2, n=P)[:, :, w, :]
                    col = 2 * (CH - 1) * P + (LAST if w == 0 else 0)
                    nc.scalar.activation(main, src[:, 0:(CH - 1) * P].rearrange("p (m n) -> p m n", n=P),
                                         ACT.Copy, scale=scale)
                    nc.scalar.activation(w12T[:, k, col:col + LAST], src[:, (CH - 1) * P:(CH - 1) * P + LAST],
                                         ACT.Copy, scale=scale).then_inc(wTe, 1)
                else:
                    nc.scalar.activation(w3T[:, 0:CH - 1, k * P:(k + 1) * P],
                                         src[:, 0:(CH - 1) * P].rearrange("p (m n) -> p m n", n=P),
                                         ACT.Copy, scale=W3S)
                    nc.scalar.activation(w3T[0:LAST, CH - 1, k * P:(k + 1) * P],
                                         src[0:LAST, (CH - 1) * P:CH * P], ACT.Copy, scale=W3S).then_inc(wTe, 1)
            act_ffn(act, 0, 0, True)

            act.wait_ge(setup, 1)
            nc.scalar.activation(expA[:], expA[:], ACT.Exp).then_inc(expA_r, 1)
            act.wait_ge(zero, 2)
            for n in range(KH):
                act_front(act, "t", n, 0, 0)
            act_front(act, "dt", 0, 0, 0)
            act_dt_exp(act, 0)
            act_front(act, "c", 0, 0, 0)
            for n in range(1, XPS):
                act_front(act, "c", n, 0, 0)
            act_stack(act, 0, 0)
            act.wait_ge(down_done, UNITS * CH)
            act.wait_ge(hlo_ready, UNITS * CH)
            for n in range(EARLY):
                act_seg(act, n, 0)
            for n in range(XPS, CT):
                act_front(act, "c", n, 0, 0)
            for n in range(Q):
                act_z(act, n, 0, 0)
            for n in range(CT):
                act_silu_conv(act, n, 0, 0)
            slots(act, act_slot)
            act.wait_ge(m_r, UNITS * TILES)
            act_split_x(act, UNITS, 0, (B0, B1))
            act_tile_sq(act, LAST_T, LAST_U)
            last_uses(act, UNITS * TILES)
            act_ffn(act, UNITS, 2 * UNITS, False)

        @block.vector
        def _(dve):
            ln_stats(dve, 0)
            ln_apply(dve, 0, 0)
            dve.wait_ge(sumd, 1)
            nc.vector.tensor_scalar(thr[:, 0, :], xTb[0][:, 0:3], 1.0 / (FF * HID), Q_EPS,
                                    ALU.mult, ALU.add).then_inc(qstep, 1)
            dve.wait_ge(qstep, 1)
            nc.vector.tensor_scalar(thr[:, 1, :], thr[:, 0, :], -0.5, None, ALU.mult).then_inc(qstep, 1)
            dve.wait_ge(qstep, 2)
            nc.vector.tensor_scalar(thr[:, 0, :], thr[:, 0, :], 0.5, None, ALU.mult).then_inc(qstep, 1)
            dve.wait_ge(qstep, 3)
            for i in range(3):
                n = CH * HID if i < 2 else KH * FF
                nc.vector.tensor_scalar(wneg[:, 0:n], wst[i][:, 0:n], thr[:, 1, i:i + 1], None, ALU.is_lt).then_inc(qstep, 1)
                dve.wait_ge(qstep, 4 + 2 * i)
                nc.vector.scalar_tensor_tensor(out=wq16[i][:, 0:n], in0=wst[i][:, 0:n], scalar=thr[:, 0, i:i + 1],
                                               in1=wneg[:, 0:n], op0=ALU.is_gt, op1=ALU.subtract).then_inc(qstep, 1)
                dve.wait_ge(qstep, 5 + 2 * i)
            dve_split_x(dve, 0, 0)
            dve_ffn(dve, 0, 0, True)

            dve.wait_ge(pl, 16 * NPARAM)
            for n in range(CT):
                ins = nc.vector.tensor_scalar(cw[:, n, :], cw[:, n, :], mupc[:, Q + n:Q + n + 1], None, ALU.mult)
            ins.then_inc(setup, 1)
            for q in range(Q):
                ins = nc.vector.tensor_scalar(wo[:, q, :], wo[:, q, :], nw[:, q:q + 1], None, ALU.mult)
            ins.then_inc(setup, 1)
            ln_stats(dve, M0 + 1)
            dve.wait_ge(setup, 2)
            dve_dt_head(dve, 0)
            ln_apply(dve, M0 + 1)
            dve_dt_series(dve, 0)
            dve.wait_ge(expA_r, 1)
            dve_dt_softplus(dve, 0, 0)
            dve_dt_split(dve, 0, 0)
            for n in range(CT):
                dve_conv(dve, n, 0, 0)
            slots(dve, dve_slot)
            dve.wait_ge(m_r, UNITS * TILES)
            dve_tile_ms(dve, LAST_T - 1, LAST_U)
            dve_tile_fin(dve, LAST_T - 1, LAST_U)
            dve_tile_gate(dve, LAST_T, LAST_U, LAST_B)
            dve_split_x(dve, UNITS, 0, (B0, B1))
            dve_tile_ms(dve, LAST_T, LAST_U)
            dve_tile_fin(dve, LAST_T, LAST_U)

            last_uses(dve, UNITS * TILES)
            dve_ffn(dve, UNITS, 2 * UNITS, False)


_INS = ['L0_attn_hidden_states', 'L0_attn_W_in', 'L0_attn_conv_w', 'L0_attn_conv_b', 'L0_attn_A_log', 'L0_attn_D',
        'L0_attn_dt_bias', 'L0_attn_norm_w', 'L0_attn_W_out', 'L0_attn_mup_vector', 'L0_ffn_w1', 'L0_ffn_w2',
        'L0_ffn_w3']


def kernel(**inputs):
    import numpy as _np
    import concourse.bacc as _bacc
    from concourse import mybir as _mybir
    from concourse.bass_utils import run_bass_kernel_spmd as _run

    nc = _bacc.Bacc("TRN2", target_bir_lowering=False, num_devices=1)
    arrays, args = {}, []
    for name in _INS:
        a = _np.ascontiguousarray(inputs[name])
        arrays[f"in_{name}_dram"] = a
        args.append(nc.dram_tensor(f"in_{name}_dram", a.shape, _mybir.dt.from_np(a.dtype), kind="ExternalInput").ap())
    out = nc.dram_tensor("out_0_dram", (BATCH, LEN, HID), _mybir.dt.float32, kind="ExternalOutput").ap()
    macaron_program(nc, *args, out)
    r = _run(nc, [arrays], core_ids=[0])
    return r.results[0]["out_0_dram"]
```
